# Optimizing a Trainium2 kernel written in Bass

```python
import numpy as np
import jax
import jax.numpy as jnp

def _softmax(x, axis=-1):
    return jax.nn.softmax(x, axis=axis)

def _gelu(x):
    return jax.nn.gelu(x, approximate=True)

def _silu(x):
    return jax.nn.silu(x)

def _sigmoid(x):
    return jax.nn.sigmoid(x)

def _layernorm(x, axis=-1, eps=1e-05):
    m = jnp.mean(x, axis=axis, keepdims=True)
    v = jnp.var(x, axis=axis, keepdims=True)
    return (x - m) / jnp.sqrt(v + eps)

def _scatter_add(tgt, idx, src, axis=0):
    return tgt.at[idx].add(src)

def _segment_sum(src, seg, n):
    return jax.ops.segment_sum(src, seg, n)
kernel_name = 'mk_recurrent_d2_jaxref_r8_b16e94'

def setup_inputs(seed: int=0):
    np.random.seed(seed)
    _w = jnp.asarray

    def _L0_attn_setup():
        import jax, jax.numpy as jnp
        import numpy as np
        D_IN = 256
        D_OUT = 256
        NUM_HEADS = 16
        HEAD_DIM = D_OUT // NUM_HEADS
        BLOCK_SIZE = 256
        BATCH = 4
        key = jax.random.key(seed)
        k_x, k_q, k_k, k_v, k_o = jax.random.split(key, 5)
        scale = 1.0 / np.sqrt(D_IN)
        return {'x': jax.random.normal(k_x, (BATCH, BLOCK_SIZE, D_IN), dtype=jnp.float32), 'Wq': jax.random.normal(k_q, (D_OUT, D_IN), dtype=jnp.float32) * scale, 'Wk': jax.random.normal(k_k, (D_OUT, D_IN), dtype=jnp.float32) * scale, 'Wv': jax.random.normal(k_v, (D_OUT, D_IN), dtype=jnp.float32) * scale, 'Wo': jax.random.normal(k_o, (D_OUT, D_OUT), dtype=jnp.float32) * scale}
    _L0_attn_in = _L0_attn_setup()

    def _L0_ffn_setup():
        import jax, jax.numpy as jnp
        import numpy as np
        B, S, D, H = (4, 256, 256, 1024)

        def fwht(x):
            orig_shape = x.shape
            n = orig_shape[-1]
            x = x.reshape(-1, n)
            h = 1
            while h < n:
                xb = x.reshape(-1, n // (2 * h), 2, h)
                a = xb[:, :, 0, :]
                b = xb[:, :, 1, :]
                x = jnp.stack([a + b, a - b], axis=2).reshape(-1, n)
                h *= 2
            scale = jnp.asarray(1.0 / np.sqrt(n), dtype=x.dtype)
            return (x * scale).reshape(orig_shape)
        key = jax.random.key(seed)
        kx, k1, k2, k3 = jax.random.split(key, 4)
        x = jax.random.normal(kx, (B, S, D), dtype=jnp.float32)
        W1 = jax.random.normal(k1, (H, D), dtype=jnp.float32) * (1.0 / np.sqrt(D))
        W2 = jax.random.normal(k2, (D, H), dtype=jnp.float32) * (1.0 / np.sqrt(H))
        W3 = jax.random.normal(k3, (H, D), dtype=jnp.float32) * (1.0 / np.sqrt(D))
        return {'x': x, 'W1': W1, 'W2': W2, 'W3': W3}
    _L0_ffn_in = _L0_ffn_setup()

    def _L1_attn_setup():
        import jax, jax.numpy as jnp
        import numpy as np
        B, S, H_DIM = (2, 256, 256)
        N_HEADS, D_HEAD = (16, 128)
        key = jax.random.key(seed)
        k1, k2, k3 = jax.random.split(key, 3)
        x = jax.random.normal(k1, (B, S, H_DIM), dtype=jnp.float32)
        w_qkv = jax.random.normal(k2, (H_DIM, 3 * N_HEADS * D_HEAD), dtype=jnp.float32) * 0.02
        w_o = jax.random.normal(k3, (N_HEADS * D_HEAD, H_DIM), dtype=jnp.float32) * 0.02
        return {'x': x, 'w_qkv': w_qkv, 'w_o': w_o}
    _L1_attn_in = _L1_attn_setup()

    def _L1_ffn_setup():
        import jax, jax.numpy as jnp
        import numpy as np
        B, S, H = (2, 256, 256)
        E, G, TKG, K = (32, 8, 4, 8)
        I, SI = (128, 256)
        ROUTED_SCALE = 2.5

        def _moe_forward(hidden_states, router_w, router_bias, w_gate, w_up, w_down, sw_gate, sw_up, sw_down):
            x = hidden_states.reshape(-1, H)
            T = x.shape[0]
            logits = x.astype(jnp.float32) @ router_w.astype(jnp.float32)
            scores = jax.nn.sigmoid(logits)
            scores_grouped = (scores + router_bias).reshape(T, G, E // G)
            top2, _ = jax.lax.top_k(scores_grouped, 2)
            group_scores = top2.sum(-1)
            _, top_groups = jax.lax.top_k(group_scores, TKG)
            mask = jnp.ones((T, G), bool).at[jnp.arange(T)[:, None], top_groups].set(False)
            masked = jnp.where(mask[:, :, None], 0.0, scores_grouped).reshape(T, E)
            _, top_k_index = jax.lax.top_k(masked, K)
            tkw = jnp.take_along_axis(scores, top_k_index, axis=-1)
            tkw = tkw / tkw.sum(-1, keepdims=True)
            tkw = (tkw * ROUTED_SCALE).astype(hidden_states.dtype)
            flat_idx = top_k_index.reshape(-1)
            sort_idx = jnp.argsort(flat_idx)
            xs = jnp.repeat(x, K, axis=0)[sort_idx]
            group_sizes = jnp.bincount(flat_idx, length=E).astype(jnp.int32)
            gate = jax.lax.ragged_dot(xs, w_gate, group_sizes)
            up = jax.lax.ragged_dot(xs, w_up, group_sizes)
            down = jax.lax.ragged_dot(jax.nn.silu(gate) * up, w_down, group_sizes)
            unsort = jnp.argsort(sort_idx)
            routed = (down[unsort].reshape(T, K, H) * tkw[..., None]).sum(axis=1)
            shared = jax.nn.silu(x @ sw_gate) * (x @ sw_up) @ sw_down
            return (routed + shared).reshape(hidden_states.shape)
        key = jax.random.key(seed)
        ks = jax.random.split(key, 9)

        def w(k, shape, fan_in):
            return jax.random.normal(k, shape, jnp.float32) / np.float32(np.sqrt(fan_in))
        return dict(hidden_states=jax.random.normal(ks[0], (B, S, H), jnp.float32), router_w=w(ks[1], (H, E), H), router_bias=jnp.zeros((E,), jnp.float32), w_gate=w(ks[2], (E, H, I), H), w_up=w(ks[3], (E, H, I), H), w_down=w(ks[4], (E, I, H), I), sw_gate=w(ks[5], (H, SI), H), sw_up=w(ks[6], (H, SI), H), sw_down=w(ks[7], (SI, H), SI))
    _L1_ffn_in = _L1_ffn_setup()
    _d = {'L0_attn_x': _L0_attn_in['x'], 'L0_attn_Wq': _L0_attn_in['Wq'], 'L0_attn_Wk': _L0_attn_in['Wk'], 'L0_attn_Wv': _L0_attn_in['Wv'], 'L0_attn_Wo': _L0_attn_in['Wo'], 'L0_ffn_W1': _L0_ffn_in['W1'], 'L0_ffn_W2': _L0_ffn_in['W2'], 'L0_ffn_W3': _L0_ffn_in['W3'], 'L1_attn_w_qkv': _L1_attn_in['w_qkv'], 'L1_attn_w_o': _L1_attn_in['w_o'], 'L1_ffn_router_w': _L1_ffn_in['router_w'], 'L1_ffn_router_bias': _L1_ffn_in['router_bias'], 'L1_ffn_w_gate': _L1_ffn_in['w_gate'], 'L1_ffn_w_up': _L1_ffn_in['w_up'], 'L1_ffn_w_down': _L1_ffn_in['w_down'], 'L1_ffn_sw_gate': _L1_ffn_in['sw_gate'], 'L1_ffn_sw_up': _L1_ffn_in['sw_up'], 'L1_ffn_sw_down': _L1_ffn_in['sw_down']}
    _x0 = _d['L0_attn_x']
    _d['L0_attn_x'] = jax.random.normal(jax.random.fold_in(jax.random.key(seed), 1), (8, 256, 256), dtype=_x0.dtype)
    del _x0
    return _d

def reference(L0_attn_x, L0_attn_Wq, L0_attn_Wk, L0_attn_Wv, L0_attn_Wo, L0_ffn_W1, L0_ffn_W2, L0_ffn_W3, L1_attn_w_qkv, L1_attn_w_o, L1_ffn_router_w, L1_ffn_router_bias, L1_ffn_w_gate, L1_ffn_w_up, L1_ffn_w_down, L1_ffn_sw_gate, L1_ffn_sw_up, L1_ffn_sw_down):

    def _L0_attn_ref(x, Wq, Wk, Wv, Wo):
        import jax, jax.numpy as jnp
        import numpy as np
        D_IN = 256
        D_OUT = 256
        NUM_HEADS = 16
        HEAD_DIM = D_OUT // NUM_HEADS
        BLOCK_SIZE = 256
        BATCH = 4
        b, t, _ = x.shape

        def proj(W):
            return (x @ W.T).reshape(b, t, NUM_HEADS, HEAD_DIM).transpose(0, 2, 1, 3)
        q, k, v = (proj(Wq), proj(Wk), proj(Wv))
        scores = jnp.einsum('bhqd,bhkd->bhqk', q, k) / jnp.sqrt(jnp.float32(HEAD_DIM))
        causal = jnp.triu(jnp.ones((t, t), dtype=bool), k=1)
        scores = jnp.where(causal, -jnp.inf, scores)
        attn = jax.nn.softmax(scores, axis=-1)
        ctx = jnp.einsum('bhqk,bhkd->bhqd', attn, v)
        ctx = ctx.transpose(0, 2, 1, 3).reshape(b, t, D_OUT)
        return ctx @ Wo.T

    def _L0_ffn_ref(x, W1, W2, W3):
        import jax, jax.numpy as jnp
        import numpy as np
        B, S, D, H = (4, 256, 256, 1024)

        def fwht(x):
            orig_shape = x.shape
            n = orig_shape[-1]
            x = x.reshape(-1, n)
            h = 1
            while h < n:
                xb = x.reshape(-1, n // (2 * h), 2, h)
                a = xb[:, :, 0, :]
                b = xb[:, :, 1, :]
                x = jnp.stack([a + b, a - b], axis=2).reshape(-1, n)
                h *= 2
            scale = jnp.asarray(1.0 / np.sqrt(n), dtype=x.dtype)
            return (x * scale).reshape(orig_shape)
        up_gate = jnp.einsum('bsd,hd->bsh', x, W1)
        up_lin = jnp.einsum('bsd,hd->bsh', x, W3)
        hidden = jax.nn.silu(up_gate) * up_lin
        hidden = fwht(hidden)
        out = jnp.einsum('bsh,dh->bsd', hidden, W2)
        return out

    def _L1_attn_ref(x, w_qkv, w_o):
        import jax, jax.numpy as jnp
        import numpy as np
        B, S, H_DIM = (2, 256, 256)
        N_HEADS, D_HEAD = (16, 128)
        b, s, _ = x.shape
        qkv = jnp.einsum('bsh,hf->bsf', x, w_qkv)
        qkv = qkv.reshape(b, s, 3, N_HEADS, D_HEAD)
        q, k, v = (qkv[:, :, 0], qkv[:, :, 1], qkv[:, :, 2])
        q = q.transpose(0, 2, 1, 3)
        k = k.transpose(0, 2, 1, 3)
        v = v.transpose(0, 2, 1, 3)
        scores = jnp.einsum('bhqd,bhkd->bhqk', q, k) / jnp.sqrt(jnp.float32(D_HEAD))
        probs = jax.nn.softmax(scores, axis=-1)
        values = jnp.einsum('bhqk,bhkd->bhkd', probs, v)
        values = values.transpose(0, 2, 1, 3).reshape(b, s, N_HEADS * D_HEAD)
        out = jnp.einsum('bsf,fh->bsh', values, w_o)
        return out

    def _L1_ffn_ref(hidden_states, router_w, router_bias, w_gate, w_up, w_down, sw_gate, sw_up, sw_down):
        import jax, jax.numpy as jnp
        import numpy as np
        B, S, H = (2, 256, 256)
        E, G, TKG, K = (32, 8, 4, 8)
        I, SI = (128, 256)
        ROUTED_SCALE = 2.5

        def _moe_forward(hidden_states, router_w, router_bias, w_gate, w_up, w_down, sw_gate, sw_up, sw_down):
            x = hidden_states.reshape(-1, H)
            T = x.shape[0]
            logits = x.astype(jnp.float32) @ router_w.astype(jnp.float32)
            scores = jax.nn.sigmoid(logits)
            scores_grouped = (scores + router_bias).reshape(T, G, E // G)
            top2, _ = jax.lax.top_k(scores_grouped, 2)
            group_scores = top2.sum(-1)
            _, top_groups = jax.lax.top_k(group_scores, TKG)
            mask = jnp.ones((T, G), bool).at[jnp.arange(T)[:, None], top_groups].set(False)
            masked = jnp.where(mask[:, :, None], 0.0, scores_grouped).reshape(T, E)
            _, top_k_index = jax.lax.top_k(masked, K)
            tkw = jnp.take_along_axis(scores, top_k_index, axis=-1)
            tkw = tkw / tkw.sum(-1, keepdims=True)
            tkw = (tkw * ROUTED_SCALE).astype(hidden_states.dtype)
            flat_idx = top_k_index.reshape(-1)
            sort_idx = jnp.argsort(flat_idx)
            xs = jnp.repeat(x, K, axis=0)[sort_idx]
            group_sizes = jnp.bincount(flat_idx, length=E).astype(jnp.int32)
            gate = jax.lax.ragged_dot(xs, w_gate, group_sizes)
            up = jax.lax.ragged_dot(xs, w_up, group_sizes)
            down = jax.lax.ragged_dot(jax.nn.silu(gate) * up, w_down, group_sizes)
            unsort = jnp.argsort(sort_idx)
            routed = (down[unsort].reshape(T, K, H) * tkw[..., None]).sum(axis=1)
            shared = jax.nn.silu(x @ sw_gate) * (x @ sw_up) @ sw_down
            return (routed + shared).reshape(hidden_states.shape)
        return _moe_forward(hidden_states, router_w, router_bias, w_gate, w_up, w_down, sw_gate, sw_up, sw_down)
    x = L0_attn_x
    xn = _layernorm(x, axis=-1)
    s = _L0_attn_ref(xn, L0_attn_Wq, L0_attn_Wk, L0_attn_Wv, L0_attn_Wo)
    g = _silu(_L0_ffn_ref(xn, L0_ffn_W1, L0_ffn_W2, L0_ffn_W3))
    x = x + s * g
    xn = _layernorm(x, axis=-1)
    s = _L1_attn_ref(xn, L1_attn_w_qkv, L1_attn_w_o)
    g = _silu(_L1_ffn_ref(xn, L1_ffn_router_w, L1_ffn_router_bias, L1_ffn_w_gate, L1_ffn_w_up, L1_ffn_w_down, L1_ffn_sw_gate, L1_ffn_sw_up, L1_ffn_sw_down))
    x = x + s * g
    return x

_drawn_inputs = setup_inputs


def setup_inputs(seed=0):
    import zlib

    import numpy as np

    out = dict(_drawn_inputs(seed))
    spreads = {'L1_ffn_router_bias': (0.0, 0.1)}
    factors = {}
    for name, (base, spread) in spreads.items():
        noise = np.random.default_rng([zlib.crc32(name.encode()), seed]).standard_normal(out[name].shape)
        drawn = base * np.exp(spread * noise) if base else spread * noise
        out[name] = jnp.asarray(drawn.astype(out[name].dtype))
    for name, factor in factors.items():
        out[name] = (out[name] * factor).astype(out[name].dtype)
    return out
```

```python
from contextlib import ExitStack

import concourse.bass as bass
from concourse import mybir

P = 128
ALU = mybir.AluOpType
ACT = mybir.ActivationFunctionType
AX = mybir.AxisListType
F32 = mybir.dt.float32
F32R = mybir.dt.float32r
EPS = 1e-5
MASKED = -1e30


class Batch:

    def __init__(self, half, off):
        self.half, self.off = half, off
        self.par = off % 2
        self.n = 2 * half + off
        self.uses = half + off // 2 + 1

    def back(self, k):
        return Batch(self.half, self.off - k)


def wait(eng, sem, value):
    if isinstance(value, int) and value <= 0:
        return
    eng.wait_ge(sem, value)


def layer0(nc, ctx, t, x, x2, w, last_b):
    D, S, NB, NH = 256, 256, 8, 16
    NJ = 8

    def sb(name, shape, dt=F32):
        return ctx.enter_context(nc.sbuf_tensor(name, shape, dt))

    def ps(name, shape):
        return ctx.enter_context(nc.psum_tensor(name, shape, F32))

    def sem(name):
        return ctx.enter_context(nc.semaphore(name))

    xb = sb("xb", [P, 2, 2, D])
    stats = sb("stats", [P, 2, 6])
    mv = sb("mv", [P, 2, 2])
    veps = sb("veps", [P, 2])
    rstd = sb("rstd", [P, 2])
    xn = sb("xn", [P, 2, D])
    xhi = sb("xhi", [P, 2, 2, S], F32R)
    xlo = sb("xlo", [P, 2, 2, S], F32R)
    chi = [sb("qch_hi", [P, 2, S], F32R), sb("kch_hi", [P, 2, S], F32R)]
    clo = [sb("qch_lo", [P, 2, S], F32R), sb("kch_lo", [P, 2, S], F32R)]
    qst = sb("qst", [P, 2, 8, S], F32R)
    kst = sb("kst", [P, 2, 8, S], F32R)
    VW = 8 * 144
    vhi = sb("vhi", [P, 2, 2, VW], F32R)
    vlo = sb("vlo", [P, 2, 2, VW], F32R)
    negmax = sb("negmax", [P, NH, 2])
    den = sb("den", [P, 2, 2, NH])
    rden = sb("rden", [P, 2, NH])
    rden_b = sb("rden_b", [P, 2, NH, 16])
    e = sb("e", [P, 2, 384])
    eThi = sb("eThi", [P, 2, 384], F32R)
    eTlo = sb("eTlo", [P, 2, 384], F32R)
    rT = sb("rT", [P, 512])
    ctxn = sb("ctxn", [P, 512])
    cxhi = sb("cxhi", [P, 2, S], F32R)
    cxlo = sb("cxlo", [P, 2, S], F32R)
    th = sb("th", [P, S])
    ga = sb("ga", [P, S])
    hid = sb("hid", [P, S])
    hhi = sb("hhi", [P, 2, S], F32R)
    hlo = sb("hlo", [P, 2, S], F32R)
    thf = sb("thf", [P, 512])
    gf = sb("gf", [P, 512])
    sg = sb("sg", [P, 512])

    psS = [ps("psS0", [P, 512]), ps("psS1", [P, 512])]
    psT = [ps("psT0", [P, 512]), ps("psT1", [P, 512])]
    psC = ps("psC", [P, 512])
    psG = ps("psG", [P, 512])
    psF = ps("psF", [P, 512])
    psM = ps("psM", [P, 512])

    qk_dram = nc.dram_tensor("qk_scratch", [2, 4, 2, P, S], F32, kind="Internal").ap()

    x_in = [sem("x_in0"), sem("x_in1")]
    stats_ok, aggr_ok, veps_ok, rstd_ok, xn_ok = (sem(n) for n in ("stats_ok", "aggr_ok", "veps_ok", "rstd_ok", "xn_ok"))
    xT_ok, xhi_ok, xlo_ok = sem("xT_ok"), sem("xhi_ok"), sem("xlo_ok")
    proj_ok = [sem("q_ok"), sem("k_ok"), sem("v_ok")]
    phi_ok = [sem("qhi_ok"), sem("khi_ok"), sem("vhi_ok")]
    plo_ok = [sem("qlo_ok"), sem("klo_ok"), sem("vlo_ok")]
    stored = [[sem("q_stored0"), sem("q_stored1")], [sem("k_stored0"), sem("k_stored1")]]
    stacked = [sem("stacked0"), sem("stacked1")]
    scores_ok, max_ok, exp_ok, eT_ok, eThi_ok, eTlo_ok, pv_ok = (
        sem(n) for n in ("scores_ok", "max_ok", "exp_ok", "eT_ok", "eThi_ok", "eTlo_ok", "pv_ok"))
    up_ok, tanh_ok, gate_ok, hid_ok, hhi_ok, hlo_ok, down_ok = (
        sem(n) for n in ("up_ok", "tanh_ok", "gate_ok", "hid_ok", "hhi_ok", "hlo_ok", "down_ok"))
    rden_ok, rdenb_ok, rT_ok, rTc_ok, ctxn_ok, cxhi_ok, cxlo_ok, so_ok = (
        sem(n) for n in ("rden_ok", "rdenb_ok", "rT_ok", "rTc_ok", "ctxn_ok", "cxhi_ok", "cxlo_ok", "so_ok"))
    tanhf_ok, gf_ok, sg_ok, x2_ok = sem("tanhf_ok"), sem("gf_ok"), sem("sg_ok"), sem("x2_ok")
    zeroed = sem("zeroed")
    wait_done = sem("wait_done")

    def drive(sequence):
        eng, prepare, heads = sequence
        prepare(Batch(0, 0))
        heads(Batch(0, 0), Batch(0, 1))
        with eng.Fori(0, (NB - 2) // 2) as i:
            heads(Batch(i, 1), Batch(i, 2))
            heads(Batch(i, 2), Batch(i, 3))
        heads(Batch(NB // 2 - 1, 1), None)

    block = ctx.enter_context(nc.Block())

    @block.sync
    def _(sp):
        def load(a):
            wait(sp, x2_ok, a.n - 1)
            sp.dma_start(xb[:, a.par], x.rearrange("(b t p) d -> b p t d", t=2, p=P)[a.n]).then_inc(x_in[a.par], 16)

        def restack(a):
            done = a.n + 1 if isinstance(a.n, int) else sp.snap(a.n + 1)
            in_scratch = 32 * a.uses if isinstance(a.n, int) else sp.snap(32 * a.uses)
            used = 16 * (a.n - 1) if isinstance(a.n, int) else sp.snap(16 * (a.n - 1))
            wait(sp, stacked[a.par], 256 * (a.uses - 1))
            sp.sem_inc(wait_done, 1)
            for i, sem_lo in enumerate(plo_ok[0:2]):
                sp.wait_ge(sem_lo, done)
                for part, buf in enumerate((chi[i], clo[i])):
                    sp.dma_start(qk_dram[a.par, 2 * i + part].rearrange("m p s -> p m s"), buf[:].bitcast(F32)).then_inc(stored[i][a.par], 16)
            wait(sp, scores_ok, used)
            for i, dst in enumerate((qst, kst)):
                sp.wait_ge(stored[i][a.par], in_scratch)
                for r in range(2):
                    for s in range(4):
                        part = s // 2 if i == 0 else s % 2
                        src = qk_dram[a.par, 2 * i + part].rearrange("m (j r d) s -> r d m j s", r=2, d=16)[r]
                        row = 64 * r + 16 * s
                        sp.dma_start(dst[row:row + 16, a.par].bitcast(F32).rearrange("p (m j) s -> p m j s", m=2), src).then_inc(stacked[a.par], 16)

        load(Batch(0, 0))
        load(Batch(0, 1))

        def prepare(a):
            restack(a)

        def heads(b, a):
            if a is not None:
                restack(a)
                nxt = Batch(a.half, a.off + 1)
                if not (isinstance(nxt.n, int) and nxt.n >= NB):
                    load(nxt)

        prepare(Batch(0, 0))
        heads(Batch(0, 0), Batch(0, 1))
        with sp.Fori(0, (NB - 2) // 2 - 1) as i:
            heads(Batch(i, 1), Batch(i, 2))
            heads(Batch(i, 2), Batch(i, 3))
        h = (NB - 2) // 2 - 1
        heads(Batch(h, 1), Batch(h, 2))
        heads(Batch(h, 2), Batch(h, 3))
        sp.wait_ge(stacked[0], 256 * (NB // 2))
        sp.wait_ge(stacked[1], 256 * (NB // 2))

    @block.tensor
    def _(pe):
        mm = pe.matmul

        def x_turn(a):
            pe.wait_ge(xn_ok, 2 * a.n + 2)
            if isinstance(a.n, int) and a.n < 2:
                wait(pe, plo_ok[2], a.n)
            else:
                pe.wait_ge(sg_ok, a.n - 1)
            for c in range(2):
                for i in range(2):
                    m = pe.transpose(psM[:, c * S + i * P:c * S + (i + 1) * P], xn[:, i, c * P:(c + 1) * P], t["ident"][:])
            m.then_inc(xT_ok, 1)

        def proj_qk(a, i):
            pe.wait_ge(xlo_ok if i == 0 else plo_ok[0], a.n + 1)
            for m in range(2):
                for c in range(2):
                    wc = (slice(None), i, c, slice(m * P, (m + 1) * P))
                    last = split3(mm, psM[:, m * S:(m + 1) * S], w["hi"][wc], w["lo"][wc],
                                  xhi[:, a.par, c], xlo[:, a.par, c], c == 0, c == 1)
            last.then_inc(proj_ok[i], 1)

        def proj_v(a):
            pe.wait_ge(plo_ok[1], a.n + 1)
            for m in range(2):
                for c in range(2):
                    tok = (slice(None), a.par, c, slice(m * P, (m + 1) * P))
                    last = split3(mm, psM[:, m * S:(m + 1) * S], xhi[tok], xlo[tok], w["hi"][:, 2, c], w["lo"][:, 2, c], c == 0, c == 1)
            last.then_inc(proj_ok[2], 1)

        def scores(b, h):
            wait(pe, exp_ok, 16 * b.n + h - 1)
            if h == 0:
                pe.wait_ge(stacked[b.par], 256 * b.uses)
            out = psS[h % 2]
            r = slice(64 * (h % 2), 64 * (h % 2) + 64)
            j = (h // 8) * 4 + (h % 8) // 2
            mm(out[:, 0:P], qst[r, b.par, j, 0:P], kst[r, b.par, j, 0:P], start=True, stop=False)
            mm(out[:, 0:P], t["ident_r"][:], t["mask_r"][:], start=False, stop=True)
            mm(out[:, P:3 * P], qst[r, b.par, j, P:2 * P], kst[r, b.par, j, 0:2 * P], start=True, stop=False, skip_group_check=True)
            mm(out[:, 2 * P:3 * P], t["ident_r"][:], t["mask_r"][:], start=False, stop=True, skip_group_check=True).then_inc(scores_ok, 1)

        def e_turn(b, h):
            pe.wait_ge(exp_ok, 16 * b.n + h + 1)
            wait(pe, eTlo_ok, 16 * b.n + h - 1)
            out = psT[h % 2]
            pe.transpose(out[:, 0:P], e[:, h % 2, 0:P], t["ident"][:])
            pe.transpose(out[:, P:2 * P], e[:, h % 2, P:2 * P], t["ident"][:])
            pe.transpose(out[:, 2 * P:3 * P], e[:, h % 2, 2 * P:3 * P], t["ident"][:]).then_inc(eT_ok, 1)

        def pv(b, h):
            pe.wait_ge(eTlo_ok, 16 * b.n + h + 1)
            if h == 0:
                pe.wait_ge(plo_ok[2], b.n + 1)
                wait(pe, ctxn_ok, b.n)
            g, hh = h // 8, h % 8
            vb = slice(hh * P, hh * P + P)
            o, q = g * S, h % 2
            split3(mm, psC[:, o:o + S], vhi[:, 0, g, vb], vlo[:, 0, g, vb], eThi[:, q, 0:S], eTlo[:, q, 0:S], hh == 0, False, True)
            split3(mm, psC[:, o + P:o + S], vhi[:, 1, g, vb], vlo[:, 1, g, vb], eThi[:, q, S:384], eTlo[:, q, S:384],
                   False, hh == 7, True).then_inc(pv_ok, 1)

        def up(b, j):
            wait(pe, hid_ok, 8 * b.n + j)
            for k in range(2):
                for c in range(2):
                    wc = (slice(None), k, c, slice(j * P, (j + 1) * P))
                    last = split3(mm, psG[:, k * S:(k + 1) * S], w["up_hi"][wc], w["up_lo"][wc],
                                  xhi[:, b.par, c], xlo[:, b.par, c], c == 0, c == 1)
            last.then_inc(up_ok, 1)

        def down(b, j):
            pe.wait_ge(hlo_ok, 8 * b.n + j + 1)
            if j == 0:
                wait(pe, gf_ok, b.n)
            for i in range(2):
                tok = (slice(None), j % 2, slice(i * P, (i + 1) * P))
                last = split3(mm, psF[:, i * D:(i + 1) * D], hhi[tok], hlo[tok], w["dn_hi"][:, j], w["dn_lo"][:, j],
                              j == 0 and i == 0, j == NJ - 1, True)
            last.then_inc(down_ok, 1)

        def rden_turn(b, a):
            pe.wait_ge(rdenb_ok, b.n + 1)
            if a is not None:
                pe.wait_ge(plo_ok[2], a.n + 1)
            else:
                pe.wait_ge(sg_ok, b.n)
            for g in range(2):
                for i in range(2):
                    src = rden_b[:, i, 8 * g:8 * g + 8].rearrange("p h d -> p (h d)")
                    m = pe.transpose(psM[:, g * S + i * P:g * S + (i + 1) * P], src, t["ident"][:])
            m.then_inc(rT_ok, 1)

        def out_proj(b):
            pe.wait_ge(rTc_ok, b.n + 1)
            pe.wait_ge(cxlo_ok, b.n + 1)
            for i in range(2):
                for g in range(2):
                    tok = (slice(None), g, slice(i * P, (i + 1) * P))
                    last = split3(mm, psM[:, i * D:(i + 1) * D], cxhi[tok], cxlo[tok], w["hi"][:, 3, g], w["lo"][:, 3, g], g == 0, g == 1)
            last.then_inc(so_ok, 1)

        def prepare(a):
            x_turn(a)
            proj_qk(a, 0)
            proj_qk(a, 1)
            proj_v(a)

        def heads(b, a):
            for h in range(NH + 2):
                if h < NH:
                    scores(b, h)
                    if h % 2 == 0:
                        up(b, h // 2)
                if h % 2 == 1 and h >= 3:
                    down(b, (h - 3) // 2)
                if 1 <= h <= NH:
                    e_turn(b, h - 1)
                if a is not None and h == 5:
                    x_turn(a)
                if a is not None and h in (8, 11):
                    proj_qk(a, (h - 8) // 3)
                if h >= 2:
                    pv(b, h - 2)
            if a is not None:
                proj_v(a)
            rden_turn(b, a)
            out_proj(b)

        drive((pe, prepare, heads))

    @block.scalar
    def _(act):
        def x_hi(a):
            act.wait_ge(xT_ok, a.n + 1)
            act.activation(xhi[:, a.par].rearrange("p c s -> p (c s)"), psM[:], ACT.Copy).then_inc(xhi_ok, 1)

        def qk_hi(a, i):
            act.wait_ge(proj_ok[i], a.n + 1)
            prev = a.back(1)
            wait(act, stored[i][prev.par], 32 * prev.uses)
            act.activation(chi[i][:].rearrange("p c s -> p (c s)"), psM[:], ACT.Copy, scale=0.25 if i == 0 else 1.0).then_inc(phi_ok[i], 1)

        def v_dst(buf, i):
            return buf[:, i].rearrange("p g (h c) -> p g h c", c=144)[:, :, :, 0:16]

        def v_hi(a):
            act.wait_ge(proj_ok[2], a.n + 1)
            if a.off == 0:
                act.wait_ge(zeroed, 1)
            wait(act, pv_ok, 16 * a.n)
            for i in range(2):
                m = act.activation(v_dst(vhi, i), psM[:, i * D:(i + 1) * D].rearrange("p (g h d) -> p g h d", g=2, d=16), ACT.Copy)
            m.then_inc(phi_ok[2], 1)

        def exp(b, h):
            act.wait_ge(max_ok, 16 * b.n + h + 1)
            wait(act, eT_ok, 16 * b.n + h - 1)
            act.activation(e[:, h % 2, 0:P], psS[h % 2][:, 0:P], ACT.Exp, bias=negmax[:, h, 0:1], accum_out=den[:, b.par, 0, h:h + 1])
            act.activation(e[:, h % 2, P:384], psS[h % 2][:, P:384], ACT.Exp, bias=negmax[:, h, 1:2],
                           accum_out=den[:, b.par, 1, h:h + 1]).then_inc(exp_ok, 1)

        def eT_hi(b, h):
            act.wait_ge(eT_ok, 16 * b.n + h + 1)
            wait(act, pv_ok, 16 * b.n + h - 1)
            act.activation(eThi[:, h % 2], psT[h % 2][:, 0:384], ACT.Copy).then_inc(eThi_ok, 1)

        def gate_tanh(b, j):
            act.wait_ge(up_ok, 8 * b.n + j + 1)
            wait(act, gate_ok, 8 * b.n + j)
            act.activation(th[:], psG[:, 0:S], ACT.Tanh, scale=0.5).then_inc(tanh_ok, 1)

        def hid_hi(b, j):
            act.wait_ge(hid_ok, 8 * b.n + j + 1)
            wait(act, down_ok, 8 * b.n + j - 1)
            act.activation(hhi[:, j % 2], hid[:], ACT.Copy).then_inc(hhi_ok, 1)

        def prepare(a):
            x_hi(a)
            qk_hi(a, 0)
            qk_hi(a, 1)
            v_hi(a)

        def heads(b, a):
            for h in range(NH + 2):
                if h < NH:
                    exp(b, h)
                    if h % 2 == 0:
                        gate_tanh(b, h // 2)
                if h < NH and h % 2 == 1:
                    hid_hi(b, h // 2)
                if 1 <= h <= NH:
                    eT_hi(b, h - 1)
                if a is not None and h == 6:
                    x_hi(a)
                if a is not None and h in (9, 12):
                    qk_hi(a, (h - 9) // 3)
            if a is not None:
                v_hi(a)
            act.wait_ge(down_ok, 8 * b.n + 8)
            wait(act, gf_ok, b.n)
            act.activation(thf[:], psF[:], ACT.Tanh, scale=0.5).then_inc(tanhf_ok, 1)
            act.wait_ge(rT_ok, b.n + 1)
            wait(act, ctxn_ok, b.n)
            act.activation(rT[:], psM[:], ACT.Copy).then_inc(rTc_ok, 1)
            act.wait_ge(ctxn_ok, b.n + 1)
            wait(act, so_ok, b.n)
            act.activation(cxhi[:].rearrange("p g s -> p (g s)"), ctxn[:], ACT.Copy).then_inc(cxhi_ok, 1)

        drive((act, prepare, heads))

    @block.vector
    def _(dve):
        def x_stats(a):
            dve.wait_ge(x_in[a.par], 16 * a.uses)
            for i in range(2):
                m = dve.bn_stats(stats[:, i], xb[:, a.par, i])
            m.then_inc(stats_ok, 1)
            dve.wait_ge(stats_ok, a.n + 1)
            dve.sem_inc(wait_done, 1)
            for i in range(2):
                m = dve.bn_aggr(mv[:, i], stats[:, i])
            m.then_inc(aggr_ok, 1)
            dve.wait_ge(aggr_ok, a.n + 1)
            dve.tensor_scalar(veps[:], mv[:, :, 1], EPS, None, ALU.add).then_inc(veps_ok, 1)

        def x_norm(a):
            dve.wait_ge(rstd_ok, a.n + 1)
            wait(dve, xT_ok, a.n)
            for i in range(2):
                dve.tensor_scalar(xn[:, i], xb[:, a.par, i], mv[:, i, 0:1], rstd[:, i:i + 1], ALU.subtract, ALU.mult).then_inc(xn_ok, 1)

        def x_lo(a):
            dve.wait_ge(xhi_ok, a.n + 1)
            dve.tensor_tensor(xlo[:, a.par].rearrange("p c s -> p (c s)"), psM[:], xhi[:, a.par].bitcast(F32).rearrange("p c s -> p (c s)"),
                              ALU.subtract).then_inc(xlo_ok, 1)

        def qk_lo(a, i):
            dve.wait_ge(phi_ok[i], a.n + 1)
            flat = lambda z: z.rearrange("p c s -> p (c s)")
            if i == 0:
                dve.scalar_tensor_tensor(flat(clo[0][:]), psM[:], 0.25, flat(chi[0][:].bitcast(F32)), ALU.mult, ALU.subtract).then_inc(plo_ok[0], 1)
            else:
                dve.tensor_tensor(flat(clo[1][:]), psM[:], flat(chi[1][:].bitcast(F32)), ALU.subtract).then_inc(plo_ok[1], 1)

        def v_dst(buf, i):
            return buf.rearrange("p g (h c) -> p g h c", c=144)[:, :, :, 0:16]

        def v_lo(a):
            dve.wait_ge(phi_ok[2], a.n + 1)
            if a.off == 0:
                dve.wait_ge(zeroed, 2)
            for i in range(2):
                m = dve.tensor_tensor(v_dst(vlo[:, i], i), psM[:, i * D:(i + 1) * D].rearrange("p (g h d) -> p g h d", g=2, d=16),
                                      v_dst(vhi[:, i].bitcast(F32), i), ALU.subtract)
            m.then_inc(plo_ok[2], 1)

        def row_max(b, h):
            dve.wait_ge(scores_ok, 16 * b.n + h + 1)
            dve.tensor_reduce(negmax[:, h, 0:1], psS[h % 2][:, 0:P], AX.X, ALU.max, negate=True)
            dve.tensor_reduce(negmax[:, h, 1:2], psS[h % 2][:, P:384], AX.X, ALU.max, negate=True).then_inc(max_ok, 1)

        def eT_lo(b, h):
            dve.wait_ge(eThi_ok, 16 * b.n + h + 1)
            dve.tensor_tensor(eTlo[:, h % 2], psT[h % 2][:, 0:384], eThi[:, h % 2].bitcast(F32), ALU.subtract).then_inc(eTlo_ok, 1)

        def gate(b, j):
            dve.wait_ge(tanh_ok, 8 * b.n + j + 1)
            dve.scalar_tensor_tensor(ga[:], th[:], 1.0, psG[:, 0:S], ALU.add, ALU.mult).then_inc(gate_ok, 1)
            dve.wait_ge(gate_ok, 8 * b.n + j + 1)
            wait(dve, hlo_ok, 8 * b.n + j)
            dve.scalar_tensor_tensor(hid[:], ga[:], 0.5, psG[:, S:2 * S], ALU.mult, ALU.mult).then_inc(hid_ok, 1)

        def prepare(a):
            x_stats(a)
            x_norm(a)
            x_lo(a)
            qk_lo(a, 0)
            qk_lo(a, 1)
            v_lo(a)

        def heads(b, a):
            for h in range(NH + 2):
                if h < NH:
                    row_max(b, h)
                if 1 <= h <= NH:
                    eT_lo(b, h - 1)
                if h < NH and h % 2 == 0:
                    gate(b, h // 2)
                if a is not None:
                    if h == 1:
                        x_stats(a)
                    if h == 3:
                        x_norm(a)
                    if h == 6:
                        x_lo(a)
                    if h in (9, 12):
                        qk_lo(a, (h - 9) // 3)
            if a is not None:
                v_lo(a)
            dve.wait_ge(exp_ok, 16 * b.n + 16)
            dve.reciprocal(rden[:], den[:, b.par]).then_inc(rden_ok, 1)
            dve.wait_ge(rden_ok, b.n + 1)
            dve.tensor_copy(rden_b[:], rden[:].unsqueeze(3).to_broadcast([P, 2, NH, 16])).then_inc(rdenb_ok, 1)
            dve.wait_ge(tanhf_ok, b.n + 1)
            dve.scalar_tensor_tensor(gf[:], thf[:], 1.0, psF[:], ALU.add, ALU.mult).then_inc(gf_ok, 1)
            dve.wait_ge(rTc_ok, b.n + 1)
            dve.wait_ge(pv_ok, 16 * b.n + 16)
            dve.tensor_tensor(ctxn[:], psC[:], rT[:], ALU.mult).then_inc(ctxn_ok, 1)
            dve.wait_ge(cxhi_ok, b.n + 1)
            dve.tensor_tensor(cxlo[:].rearrange("p g s -> p (g s)"), ctxn[:], cxhi[:].bitcast(F32).rearrange("p g s -> p (g s)"),
                              ALU.subtract).then_inc(cxlo_ok, 1)
            dve.wait_ge(so_ok, b.n + 1)
            wait(dve, x2_ok, b.n)
            dve.scalar_tensor_tensor(sg[:], gf[:], 0.5, psM[:], ALU.mult, ALU.mult).then_inc(sg_ok, 1)

        drive((dve, prepare, heads))

    @block.gpsimd
    def _(pool):
        def deviation(a):
            pool.wait_ge(veps_ok, a.n + 1)
            pool.tensor_tensor(rstd[:], veps[:], t["neg_half"][:, 0:2], ALU.pow).then_inc(rstd_ok, 1)

        def hid_lo(b, j):
            pool.wait_ge(hhi_ok, 8 * b.n + j + 1)
            pool.tensor_tensor(hlo[:, j % 2], hid[:], hhi[:, j % 2].bitcast(F32), ALU.subtract).then_inc(hlo_ok, 1)

        def heads(b, a):
            for j in range(NJ):
                hid_lo(b, j)
                if a is not None and j == 0:
                    deviation(a)
            pool.wait_ge(sg_ok, b.n + 1)
            dst = x2.rearrange("p (b t) d -> p b (t d)", t=2)
            dst = dst[:, b.n] if isinstance(b.n, int) else dst[:, bass.ds(b.n, 1)].rearrange("p o n -> p (o n)")
            pool.tensor_tensor(dst, sg[:], xb[:, b.par].rearrange("p t d -> p (t d)"), ALU.add).then_inc(x2_ok, 1)

        pool.memset(vhi[:].bitcast(F32), 0.0).then_inc(zeroed, 1)
        pool.memset(vlo[:].bitcast(F32), 0.0).then_inc(zeroed, 1)
        drive((pool, deviation, heads))


def prepare_weights(nc, ctx, t, w, args):
    def sb(name, shape, dt=F32):
        return ctx.enter_context(nc.sbuf_tensor(name, shape, dt))

    def sem(name):
        return ctx.enter_context(nc.semaphore(name))

    raw = sb("raw_qkvo", [P, 4, 2, 256])
    raw_up = sb("raw_up", [P, 2, 2, 1024])
    raw_dn = sb("raw_dn", [P, 8, 256])
    fold = [sb("fold0", [P, 8, 256]), sb("fold1", [P, 8, 256])]
    had = sb("had", [P, P])
    mask = sb("mask", [P, P])
    psW = [ctx.enter_context(nc.psum_tensor(f"psW{i}", [P, 512], F32)) for i in range(4)]
    const_in, dn_in, qkvo_in, up_in = sem("const_in"), sem("dn_in"), sem("qkvo_in"), sem("up_in")
    folded, rotated, dnhi_ok, split_a, split_d, split_p = (
        sem(n) for n in ("folded", "rotated", "dnhi_ok", "split_a", "split_d", "split_p"))
    block = ctx.enter_context(nc.Block())
    flat4 = lambda z: z.rearrange("p a b c -> p (a b c)")

    @block.sync
    def _(sp):
        sp.dma_start(raw_dn[:], args["W2T"].rearrange("(c p) d -> p c d", p=P)).then_inc(dn_in, 16)
        sp.dma_start(had[:], args["hadamard"]).then_inc(const_in, 16)
        sp.dma_start(t["ident"][:], args["ident"]).then_inc(const_in, 16)
        sp.dma_start(mask[:], args["mask"]).then_inc(const_in, 16)
        sp.dma_start(raw[:], args["qkvoT"].rearrange("a (c p) n -> p a c n", p=P)).then_inc(qkvo_in, 16)
        sp.dma_start(raw_up[:], args["upT"].rearrange("a (c p) n -> p a c n", p=P)).then_inc(up_in, 16)

    @block.vector
    def _(dve):
        dve.wait_ge(dn_in, 16)
        src = raw_dn
        for n, half in enumerate((1, 2, 4)):
            dst = fold[n % 2]
            s = src[:].rearrange("p (a two b) d -> p a two (b d)", two=2, b=half)
            d = dst[:].rearrange("p (a two b) d -> p a two (b d)", two=2, b=half)
            if n:
                dve.wait_ge(folded, 2 * n)
            dve.tensor_tensor(d[:, :, 0], s[:, :, 0], s[:, :, 1], ALU.add).then_inc(folded, 1)
            dve.tensor_tensor(d[:, :, 1], s[:, :, 0], s[:, :, 1], ALU.subtract).then_inc(folded, 1)
            src = dst
        for i in range(4):
            dve.wait_ge(dnhi_ok, i + 1)
            dve.scalar_tensor_tensor(w["dn_lo"][:, 2 * i:2 * i + 2].rearrange("p c d -> p (c d)"), psW[i][:], 1.0 / 32.0,
                                     w["dn_hi"][:, 2 * i:2 * i + 2].bitcast(F32).rearrange("p c d -> p (c d)"), ALU.mult, ALU.subtract)
        dve.wait_ge(split_a, 3)
        dve.tensor_tensor(flat4(w["up_lo"][:]), flat4(raw_up[:]), flat4(w["up_hi"][:].bitcast(F32)), ALU.subtract)

    @block.tensor
    def _(pe):
        pe.wait_ge(folded, 6)
        pe.wait_ge(const_in, 48)
        for i in range(4):
            src = fold[0][:, 2 * i:2 * i + 2].rearrange("p c d -> p (c d)")
            pe.matmul(psW[i][:], had[:], src, start=True, stop=True).then_inc(rotated, 1)

    @block.scalar
    def _(act):
        act.wait_ge(const_in, 48)
        act.activation(t["ident_r"][:], t["ident"][:], ACT.Copy).then_inc(split_a, 1)
        act.activation(t["mask_r"][:], mask[:], ACT.Copy).then_inc(split_a, 1)
        act.wait_ge(up_in, 16)
        act.activation(flat4(w["up_hi"][:]), flat4(raw_up[:]), ACT.Copy).then_inc(split_a, 1)
        for i in range(4):
            act.wait_ge(rotated, i + 1)
            act.activation(w["dn_hi"][:, 2 * i:2 * i + 2].rearrange("p c d -> p (c d)"), psW[i][:], ACT.Copy, scale=1.0 / 32.0).then_inc(dnhi_ok, 1)

    @block.gpsimd
    def _(pool):
        pool.memset(t["neg_half"][:], -0.5)
        pool.wait_ge(qkvo_in, 16)
        pool.tensor_copy(flat4(w["hi"][:]), flat4(raw[:])).then_inc(split_p, 1)
        pool.wait_ge(split_p, 1)
        pool.tensor_tensor(flat4(w["lo"][:]), flat4(raw[:]), flat4(w["hi"][:].bitcast(F32)), ALU.subtract)


def split3(mm, out, a_hi, a_lo, b_hi, b_lo, start, stop, skip=False):
    mm(out, a_hi, b_hi, start=start, stop=False, skip_group_check=skip)
    mm(out, a_hi, b_lo, start=False, stop=False, skip_group_check=skip)
    return mm(out, a_lo, b_hi, start=False, stop=stop, skip_group_check=skip)


def normalise_and_route(nc, ctx, t, zeros, x2, xhi, xlo, wts, args):
    NT, NE = 16, 32

    def sb(name, shape, dt=F32):
        return ctx.enter_context(nc.sbuf_tensor(name, shape, dt))

    def sem(name):
        return ctx.enter_context(nc.semaphore(name))

    stats = sb("stats1", [P, NT, 6])
    mv = sb("mv1", [P, NT, 2])
    veps = sb("veps1", [P, NT])
    rstd = sb("rstd1", [P, NT])
    xn = sb("xn1", [P, NT, 256])
    rw = sb("rw", [P, 2, NE])
    rw_hi = sb("rw_hi", [P, 2, NE], F32R)
    rw_lo = sb("rw_lo", [P, 2, NE], F32R)
    bias = sb("bias", [P, NE])
    tri = sb("tri", [P, 64])
    score = sb("score", [P, NT, NE])
    biased = sb("biased", [P, NT, NE])
    pmax = sb("pmax", [P, NT * 8, 2])
    pmin = sb("pmin", [P, NT * 8, 2])
    top = sb("top", [P, NT * 8])
    low = sb("low", [P, NT * 8])
    other = sb("other", [P, NT * 8])
    second = sb("second", [P, NT * 8])
    group = sb("group", [P, NT, 8])
    above = sb("above", [P, NT, 8, 8])
    equal = sb("equal", [P, NT, 8, 8])
    rank = sb("rank", [P, NT, 8])
    keep = sb("keep", [P, NT, 8])
    masked = sb("masked", [P, NT, NE])
    best = sb("best", [P, NT, 8])
    rest = sb("rest", [P, NT, NE])
    chosen = sb("chosen", [P, NT, NE])
    total = sb("total", [P, NT])
    rtotal = sb("rtotal", [P, NT])
    psX = [ctx.enter_context(nc.psum_tensor(f"psX{i}", [P, 512], F32)) for i in range(4)]
    psL = ctx.enter_context(nc.psum_tensor("psL", [P, NT, NE], F32))

    (const_in, stats_ok, aggr_ok, veps_ok, rstd_ok, xn_ok, xT_ok, xhi_ok, xlo_ok, rw_ok, logits_ok, score_ok, chain) = (
        sem(n) for n in ("const1_in", "stats1_ok", "aggr1_ok", "veps1_ok", "rstd1_ok", "xn1_ok", "xT1_ok", "xhi1_ok", "xlo1_ok",
                         "rw_ok", "logits_ok", "score_ok", "route_step"))
    block = ctx.enter_context(nc.Block())
    pair = lambda z, k: z[:, :, 256 * k:256 * (k + 1)]

    @block.sync
    def _(sp):
        sp.dma_start(rw[:], args["router_w"].rearrange("(c p) e -> p c e", p=P)).then_inc(const_in, 16)
        sp.dma_start(bias[:], args["router_bias"].broadcast_to([P, NE])).then_inc(const_in, 16)
        sp.dma_start(tri[:], args["earlier"].broadcast_to([P, 64])).then_inc(const_in, 16)

    @block.gpsimd
    def _(pool):
        pool.wait_ge(veps_ok, 1)
        pool.tensor_tensor(rstd[:], veps[:], t["neg_half"][:], ALU.pow).then_inc(rstd_ok, 1)
        pool.memset(zeros[:], 0.0)
        pool.memset(wts[:, NE:NE + 2], 1.0)
        pool.wait_ge(const_in, 48)
        pool.tensor_copy(rw_hi[:], rw[:]).then_inc(rw_ok, 1)
        pool.wait_ge(rw_ok, 1)
        pool.tensor_tensor(rw_lo[:], rw[:], rw_hi[:].bitcast(F32), ALU.subtract).then_inc(rw_ok, 1)

    @block.tensor
    def _(pe):
        for k in range(NT // 2):
            pe.wait_ge(xn_ok, 2 * k + 2)
            wait(pe, xlo_ok, k - 3)
            for c in range(2):
                for i in range(2):
                    m = pe.transpose(psX[k % 4][:, c * 256 + i * P:c * 256 + (i + 1) * P], xn[:, 2 * k + i, c * P:(c + 1) * P], t["ident"][:])
            m.then_inc(xT_ok, 1)
        pe.wait_ge(rw_ok, 2)
        pe.wait_ge(xlo_ok, NT // 2)
        for i in range(NT):
            for c in range(2):
                tok = (slice(None), c, slice(i * P, (i + 1) * P))
                m = split3(pe.matmul, psL[:, i], xhi[tok], xlo[tok], rw_hi[:, c], rw_lo[:, c], c == 0, c == 1)
        m.then_inc(logits_ok, 1)

    @block.scalar
    def _(act):
        for k in range(NT // 2):
            act.wait_ge(xT_ok, k + 1)
            act.activation(pair(xhi, k), psX[k % 4][:].rearrange("p (c s) -> p c s", c=2), ACT.Copy).then_inc(xhi_ok, 1)
        act.wait_ge(logits_ok, 1)
        act.activation(score[:], psL[:], ACT.Sigmoid).then_inc(score_ok, 1)

    @block.vector
    def _(dve):
        for i in range(NT):
            m = dve.bn_stats(stats[:, i], x2[:, i])
        m.then_inc(stats_ok, 1)
        dve.wait_ge(stats_ok, 1)
        for i in range(NT):
            m = dve.bn_aggr(mv[:, i], stats[:, i])
        m.then_inc(aggr_ok, 1)
        dve.wait_ge(aggr_ok, 1)
        dve.tensor_scalar(veps[:], mv[:, :, 1], EPS, None, ALU.add).then_inc(veps_ok, 1)
        dve.wait_ge(rstd_ok, 1)

        def x_lo(k):
            dve.wait_ge(xhi_ok, k + 1)
            dve.tensor_tensor(pair(xlo, k), psX[k % 4][:].rearrange("p (c s) -> p c s", c=2), pair(xhi, k).bitcast(F32), ALU.subtract).then_inc(xlo_ok, 1)

        for i in range(NT):
            dve.tensor_scalar(xn[:, i], x2[:, i], mv[:, i, 0:1], rstd[:, i:i + 1], ALU.subtract, ALU.mult).then_inc(xn_ok, 1)
            if i % 2 == 1 and i >= 3:
                x_lo((i - 3) // 2)
        x_lo(NT // 2 - 1)
        dve.wait_ge(score_ok, 1)
        dve.wait_ge(const_in, 48)
        steps = 0

        def step(ins):
            nonlocal steps
            steps += 1
            ins.then_inc(chain, 1)
            dve.wait_ge(chain, steps)

        step(dve.tensor_tensor(biased[:], score[:], bias[:].unsqueeze(1).to_broadcast([P, NT, NE]), ALU.add))
        quad = biased[:].rearrange("p t (g b a) -> p (t g) b a", b=2, a=2)
        dve.tensor_tensor(pmax[:], quad[:, :, :, 0], quad[:, :, :, 1], ALU.max)
        step(dve.tensor_tensor(pmin[:], quad[:, :, :, 0], quad[:, :, :, 1], ALU.min))
        dve.tensor_tensor(top[:], pmax[:, :, 0], pmax[:, :, 1], ALU.max)
        dve.tensor_tensor(low[:], pmax[:, :, 0], pmax[:, :, 1], ALU.min)
        step(dve.tensor_tensor(other[:], pmin[:, :, 0], pmin[:, :, 1], ALU.max))
        step(dve.tensor_tensor(second[:], low[:], other[:], ALU.max))
        step(dve.tensor_tensor(group[:].rearrange("p t g -> p (t g)"), top[:], second[:], ALU.add))
        mine = group[:].unsqueeze(3).to_broadcast([P, NT, 8, 8])
        theirs = group[:].unsqueeze(2).to_broadcast([P, NT, 8, 8])
        dve.tensor_tensor(above[:], theirs, mine, ALU.is_gt)
        step(dve.tensor_tensor(equal[:], theirs, mine, ALU.is_equal))
        flat = lambda z: z.rearrange("p t g h -> p t (g h)")
        step(dve.tensor_tensor(flat(equal[:]), flat(equal[:]), tri[:].unsqueeze(1).to_broadcast([P, NT, 64]), ALU.mult))
        step(dve.tensor_tensor(flat(above[:]), flat(above[:]), flat(equal[:]), ALU.add))
        step(dve.tensor_reduce(rank[:], above[:], AX.X, ALU.add))
        step(dve.tensor_scalar(keep[:], rank[:], 3.5, None, ALU.is_lt))
        by_group = lambda z: z.rearrange("p t (g a) -> p (t g) a", a=4)
        step(dve.tensor_tensor(by_group(masked[:]), by_group(biased[:]),
                               keep[:].rearrange("p t g -> p (t g)").unsqueeze(2).to_broadcast([P, NT * 8, 4]), ALU.mult))
        step(dve.tensor_scalar(masked[:], masked[:], 0.0, None, ALU.add))
        for i in range(NT):
            m = dve.max(best[:, i], masked[:, i])
        step(m)
        for i in range(NT):
            m = dve.match_replace(rest[:, i], best[:, i], masked[:, i], -3.0e38)
        step(m)
        step(dve.tensor_tensor(chosen[:], rest[:], masked[:], ALU.not_equal))
        step(dve.tensor_tensor(chosen[:], chosen[:], score[:], ALU.mult))
        step(dve.tensor_reduce(total[:], chosen[:], AX.X, ALU.add))
        step(dve.reciprocal(rtotal[:], total[:]))
        dve.scalar_tensor_tensor(wts[:, 0:NE].rearrange("p e t -> p t e"), chosen[:], 2.5,
                                 rtotal[:].unsqueeze(2).to_broadcast([P, NT, NE]), ALU.mult, ALU.mult)


class Step:

    def __init__(self, i, k):
        self.i, self.k = i, k
        self.n = 8 * i + k
        self.g = k % 4
        self.par = (k // 4) % 2
        self.head = 2 * i + k // 4

    def back(self, j):
        return Step(self.i, self.k - j)


def attention1(nc, ctx, zeros, xhi, xlo, s1, args):
    NH, NG = 16, 4
    SCALE = 128.0 ** -0.5

    def sb(name, shape, dt=F32):
        return ctx.enter_context(nc.sbuf_tensor(name, shape, dt))

    def sem(name):
        return ctx.enter_context(nc.semaphore(name))

    raw = sb("raw_head", [P, 2, 1024])
    whi = sb("head_hi", [P, 2, 1024], F32R)
    wlo = sb("head_lo", [P, 2, 1024], F32R)
    ohi = [sb("q1_hi", [P, 512], F32R), sb("k1_hi", [P, 512], F32R)]
    olo = [sb("q1_lo", [P, 512], F32R), sb("k1_lo", [P, 512], F32R)]
    negmax = sb("negmax1", [P, 4])
    e = sb("e1", [P, 4, 256])
    den = sb("den1", [P, 4])
    rden = sb("rden1", [P, 4])
    rden_b = sb("rden1_b", [P, 4, P])
    csum = sb("csum", [P, 512])
    val = sb("val", [P, 512])
    vhi = sb("val_hi", [P, 2, 512], F32R)
    vlo = sb("val_lo", [P, 2, 512], F32R)
    ps = lambda n: ctx.enter_context(nc.psum_tensor(n, [P, 512], F32))
    psQK, psV, psS, psC, psO = [ps("psQ1"), ps("psK1")], ps("psV1"), [ps("psS10"), ps("psS11")], ps("psC1"), [ps("psO0"), ps("psO1")]

    raw_in = [sem("head_in0"), sem("head_in1")]
    whi_ok, wlo_ok, v_ok, scores_ok, max_ok, exp_ok, rden_ok, rdenb_ok, c_ok, csum_ok, val_ok, vhi_ok, vlo_ok, o_ok, acc_ok, zeroed = (
        sem("a1_" + n) for n in ("whi_ok", "wlo_ok", "v_ok", "scores_ok", "max_ok", "exp_ok", "rden_ok", "rdenb_ok",
                                 "c_ok", "csum_ok", "val_ok", "vhi_ok", "vlo_ok", "o_ok", "acc_ok", "zeroed"))
    p_ok = [sem("a1_q_ok"), sem("a1_k_ok")]
    phi_ok = [sem("a1_qhi_ok"), sem("a1_khi_ok")]
    plo_ok = [sem("a1_qlo_ok"), sem("a1_klo_ok")]
    block = ctx.enter_context(nc.Block())

    def drive(eng, step, tail):
        for k in range(8):
            step(Step(0, k))
        with eng.Fori(1, NH // 2) as i:
            for k in range(8):
                step(Step(i, k))
        for k in range(2):
            tail(Step(NH // 2, k))

    exists = lambda n: not isinstance(n, int) or n >= 0

    @block.sync
    def _(sp):
        def load(head_i, par, uses):
            wait(sp, wlo_ok, 2 * (uses - 2) + par + 1)
            src = args["heads"][2 * head_i + par]
            sp.dma_start(raw[:, par], src).then_inc(raw_in[par], 16)
        for par in range(2):
            load(0, par, 1)
        with sp.Fori(1, NH // 2) as i:
            for par in range(2):
                load(i, par, i + 1)

    @block.gpsimd
    def _(pool):
        def split(i, par):
            pool.wait_ge(raw_in[par], 16 * (i + 1))
            wait(pool, o_ok, 8 * i + 4 * par - 4)
            pool.tensor_tensor(whi[:, par], raw[:, par], zeros[:, 0:raw.shape[2]], ALU.add).then_inc(whi_ok, 1)
            pool.wait_ge(whi_ok, 2 * i + par + 1)
            pool.tensor_tensor(wlo[:, par], raw[:, par], whi[:, par].bitcast(F32), ALU.subtract).then_inc(wlo_ok, 1)

        def finish(s):
            pool.wait_ge(rden_ok, s.n + 1)
            wait(pool, c_ok, s.n)
            pool.tensor_tensor(rden_b[:], rden[:].unsqueeze(2).to_broadcast([P, 4, P]), zeros[:, 0:512].rearrange("p (a b) -> p a b", a=4), ALU.add).then_inc(rdenb_ok, 1)
            pool.wait_ge(val_ok, s.n + 1)
            wait(pool, o_ok, s.n - 1)
            pool.tensor_tensor(vhi[:, s.k % 2], val[:], zeros[:, 0:512], ALU.add).then_inc(vhi_ok, 1)
            pool.wait_ge(vhi_ok, s.n + 1)
            pool.tensor_tensor(vlo[:, s.k % 2], val[:], vhi[:, s.k % 2].bitcast(F32), ALU.subtract).then_inc(vlo_ok, 1)

        def step(s, last=False):
            if exists(s.n - 1):
                finish(s.back(1))
            if s.g == 2 and not last:
                nxt = Step(s.i, s.k + 4)
                split(nxt.i if nxt.k < 8 else nxt.i + 1, nxt.par)

        pool.memset(s1[:], 0.0).then_inc(zeroed, 1)
        split(0, 0)
        for k in range(8):
            step(Step(0, k))
        with pool.Fori(1, NH // 2 - 1) as i:
            for k in range(8):
                step(Step(i, k))
        for k in range(8):
            step(Step(NH // 2 - 1, k), last=k >= 4)
        finish(Step(NH // 2, -1))

    @block.tensor
    def _(pe):
        mm = pe.matmul

        def proj(s, j, out, done):
            for c in range(2):
                wc = (slice(None), s.par, slice(256 * j + P * c, 256 * j + P * (c + 1)))
                tok = (slice(None), c, slice(512 * s.g, 512 * s.g + 512))
                last = split3(mm, out[:], whi[wc], wlo[wc], xhi[tok], xlo[tok], c == 0, c == 1)
            last.then_inc(done, 1)

        def column_sums(s):
            pe.wait_ge(rdenb_ok, s.n + 1)
            wait(pe, csum_ok, s.n)
            for b in range(2):
                mm(psC[:, 256 * b:256 * b + 256], rden_b[:, 2 * b], e[:, 2 * b], start=True, stop=False)
                last = mm(psC[:, 256 * b:256 * b + 256], rden_b[:, 2 * b + 1], e[:, 2 * b + 1], start=False, stop=True)
            last.then_inc(c_ok, 1)

        def out_proj(s):
            pe.wait_ge(vlo_ok, s.n + 1)
            wait(pe, acc_ok, s.n)
            wo = (slice(None), s.par, slice(768, 1024))
            for i in range(4):
                tok = (slice(None), s.k % 2, slice(P * i, P * i + P))
                last = split3(mm, psO[i // 2][:, 256 * (i % 2):256 * (i % 2) + 256], vhi[tok], vlo[tok], whi[wo], wlo[wo], True, True)
            last.then_inc(o_ok, 1)

        def step(s):
            if s.g == 0:
                pe.wait_ge(wlo_ok, s.head + 1)
            for j in range(2):
                wait(pe, plo_ok[j], s.n)
                proj(s, j, psQK[j], p_ok[j])
            if exists(s.n - 1):
                column_sums(s.back(1))
            if exists(s.n - 2):
                out_proj(s.back(2))
            pe.wait_ge(plo_ok[1], s.n + 1)
            wait(pe, exp_ok, s.n)
            for b in range(2):
                for i in range(2):
                    qt = slice(256 * b + P * i, 256 * b + P * (i + 1))
                    kt = slice(256 * b, 256 * b + 256)
                    last = split3(mm, psS[b][:, 256 * i:256 * i + 256], ohi[0][:, qt], olo[0][:, qt], ohi[1][:, kt], olo[1][:, kt], True, True)
            last.then_inc(scores_ok, 1)
            wait(pe, val_ok, s.n)
            proj(s, 2, psV, v_ok)

        def tail(s):
            if s.k == 0:
                column_sums(s.back(1))
            out_proj(s.back(2))

        drive(pe, step, tail)

    @block.scalar
    def _(act):
        def csum_copy(s):
            act.wait_ge(c_ok, s.n + 1)
            wait(act, val_ok, s.n)
            act.activation(csum[:], psC[:], ACT.Copy).then_inc(csum_ok, 1)

        def step(s):
            for j in range(2):
                act.wait_ge(p_ok[j], s.n + 1)
                wait(act, scores_ok, s.n)
                act.activation(ohi[j][:], psQK[j][:], ACT.Copy, scale=SCALE if j == 0 else 1.0).then_inc(phi_ok[j], 1)
            if exists(s.n - 1):
                csum_copy(s.back(1))
            act.wait_ge(max_ok, s.n + 1)
            for b in range(2):
                for i in range(2):
                    c = 2 * b + i
                    m = act.activation(e[:, c], psS[b][:, 256 * i:256 * i + 256], ACT.Exp, bias=negmax[:, c:c + 1], accum_out=den[:, c:c + 1])
            m.then_inc(exp_ok, 1)

        drive(act, step, lambda s: csum_copy(s.back(1)) if s.k == 0 else None)

    @block.vector
    def _(dve):
        def proj_lo(s, j):
            dve.wait_ge(phi_ok[j], s.n + 1)
            if j == 0:
                dve.scalar_tensor_tensor(olo[0][:], psQK[0][:], SCALE, ohi[0][:].bitcast(F32), ALU.mult, ALU.subtract).then_inc(plo_ok[0], 1)
            else:
                dve.tensor_tensor(olo[1][:], psQK[1][:], ohi[1][:].bitcast(F32), ALU.subtract).then_inc(plo_ok[1], 1)

        def reciprocals(s):
            dve.wait_ge(exp_ok, s.n + 1)
            wait(dve, rdenb_ok, s.n)
            dve.reciprocal(rden[:], den[:]).then_inc(rden_ok, 1)

        def values(s):
            dve.wait_ge(csum_ok, s.n + 1)
            dve.wait_ge(v_ok, s.n + 1)
            wait(dve, vlo_ok, s.n)
            dve.tensor_tensor(val[:], psV[:], csum[:], ALU.mult).then_inc(val_ok, 1)

        def accumulate(s):
            dve.wait_ge(o_ok, s.n + 1)
            for i in range(2):
                dst = s1[:, 4 * s.g + 2 * i:4 * s.g + 2 * i + 2].rearrange("p t d -> p (t d)")
                m = dve.tensor_tensor(dst, psO[i][:], dst, ALU.add)
            m.then_inc(acc_ok, 1)

        def step(s):
            proj_lo(s, 0)
            if exists(s.n - 1):
                reciprocals(s.back(1))
            proj_lo(s, 1)
            if exists(s.n - 1):
                values(s.back(1))
            if exists(s.n - 2):
                accumulate(s.back(2))
            dve.wait_ge(scores_ok, s.n + 1)
            for b in range(2):
                m = dve.tensor_reduce(negmax[:, 2 * b:2 * b + 2], psS[b][:].rearrange("p (i k) -> p i k", i=2), AX.X, ALU.max, negate=True)
            m.then_inc(max_ok, 1)

        def tail(s):
            if s.k == 0:
                reciprocals(s.back(1))
                values(s.back(1))
            accumulate(s.back(2))

        dve.wait_ge(zeroed, 1)
        drive(dve, step, tail)


def experts(nc, ctx, zeros, xhi, xlo, wts, f, args):
    NE = 34

    def sb(name, shape, dt=F32):
        return ctx.enter_context(nc.sbuf_tensor(name, shape, dt))

    def sem(name):
        return ctx.enter_context(nc.semaphore(name))

    raw = sb("raw_expert", [P, 2, 768])
    whi = sb("expert_hi", [P, 2, 768], F32R)
    wlo = sb("expert_lo", [P, 2, 768], F32R)
    wcol = sb("wcol", [P, 2, 16])
    sil = sb("sil", [P, 2, 512])
    hid = sb("hid1", [P, 2, 512])
    hhi = sb("hid1_hi", [P, 2, 512], F32R)
    hlo = sb("hid1_lo", [P, 2, 512], F32R)
    ps = lambda n: ctx.enter_context(nc.psum_tensor(n, [P, 512], F32))
    psG, psU = [ps("psG0"), ps("psG1")], [ps("psU0"), ps("psU1")]
    psD = [[ps("psD00"), ps("psD01")], [ps("psD10"), ps("psD11")]]
    raw_in = [sem("expert_in0"), sem("expert_in1")]
    whi_ok, wlo_ok, wcol_ok, g_ok, u_ok, sil_ok, hid_ok, hhi_ok, hlo_ok, d_ok, acc_ok, zeroed = (
        sem("m_" + n) for n in ("whi_ok", "wlo_ok", "wcol_ok", "g_ok", "u_ok", "sil_ok", "hid_ok", "hhi_ok", "hlo_ok", "d_ok", "acc_ok", "zeroed"))
    block = ctx.enter_context(nc.Block())
    exists = lambda n: not isinstance(n, int) or n >= 0

    def drive(eng, step, tail):
        for k in range(8):
            step(Step(0, k))
        with eng.Fori(1, NE // 2) as i:
            for k in range(8):
                step(Step(i, k))
        tail(Step(NE // 2, 0))

    @block.sync
    def _(sp):
        def load(i, par):
            wait(sp, wlo_ok, 2 * i + par - 1)
            sp.dma_start(raw[:, par], args["experts"][2 * i + par]).then_inc(raw_in[par], 16)
        for par in range(2):
            load(0, par)
        with sp.Fori(1, NE // 2) as i:
            for par in range(2):
                load(i, par)

    @block.gpsimd
    def _(pool):
        def split(i, par):
            pool.wait_ge(raw_in[par], 16 * (i + 1))
            wait(pool, d_ok, 8 * i + 4 * par - 4)
            pool.tensor_tensor(whi[:, par], raw[:, par], zeros[:, 0:raw.shape[2]], ALU.add).then_inc(whi_ok, 1)
            pool.wait_ge(whi_ok, 2 * i + par + 1)
            pool.tensor_tensor(wlo[:, par], raw[:, par], whi[:, par].bitcast(F32), ALU.subtract).then_inc(wlo_ok, 1)
            wait(pool, acc_ok, 8 * i + 4 * par - 4)
            src = wts[:, 2 * i + par] if isinstance(i, int) else wts[:, bass.ds(2 * i + par, 1)].rearrange("p o t -> p (o t)")
            pool.tensor_tensor(wcol[:, par], src, zeros[:, 0:16], ALU.add).then_inc(wcol_ok, 1)

        def step(s, last=False):
            pool.wait_ge(hhi_ok, s.n + 1)
            pool.tensor_tensor(hlo[:, s.k % 2], hid[:, s.k % 2], hhi[:, s.k % 2].bitcast(F32), ALU.subtract).then_inc(hlo_ok, 1)
            if s.g == 1 and not last:
                nxt = Step(s.i, s.k + 4)
                split(nxt.i if nxt.k < 8 else nxt.i + 1, nxt.par)

        pool.memset(f[:], 0.0).then_inc(zeroed, 1)
        split(0, 0)
        for k in range(8):
            step(Step(0, k))
        with pool.Fori(1, NE // 2 - 1) as i:
            for k in range(8):
                step(Step(i, k))
        for k in range(8):
            step(Step(NE // 2 - 1, k), last=k >= 4)

    @block.tensor
    def _(pe):
        mm = pe.matmul

        def proj(s, j, out, done):
            for c in range(2):
                wc = (slice(None), s.par, slice(256 * j + P * c, 256 * j + P * (c + 1)))
                tok = (slice(None), c, slice(512 * s.g, 512 * s.g + 512))
                last = split3(mm, out[:], whi[wc], wlo[wc], xhi[tok], xlo[tok], c == 0, c == 1)
            last.then_inc(done, 1)

        def down(s):
            pe.wait_ge(hlo_ok, s.n + 1)
            wait(pe, acc_ok, s.n - 1)
            wd = (slice(None), s.par, slice(512, 768))
            for i in range(4):
                tok = (slice(None), s.k % 2, slice(P * i, P * i + P))
                out = psD[s.k % 2][i // 2][:, 256 * (i % 2):256 * (i % 2) + 256]
                last = split3(mm, out, hhi[tok], hlo[tok], whi[wd], wlo[wd], True, True)
            last.then_inc(d_ok, 1)

        def step(s):
            if s.g == 0:
                pe.wait_ge(wlo_ok, s.head + 1)
            wait(pe, sil_ok, s.n - 1)
            proj(s, 0, psG[s.k % 2], g_ok)
            wait(pe, hid_ok, s.n - 1)
            proj(s, 1, psU[s.k % 2], u_ok)
            if exists(s.n - 1):
                down(s.back(1))

        drive(pe, step, lambda s: down(s.back(1)))

    @block.scalar
    def _(act):
        def step(s):
            act.wait_ge(g_ok, s.n + 1)
            wait(act, hid_ok, s.n - 1)
            act.activation(sil[:, s.k % 2], psG[s.k % 2][:], ACT.Silu).then_inc(sil_ok, 1)
            act.wait_ge(hid_ok, s.n + 1)
            wait(act, d_ok, s.n - 1)
            act.activation(hhi[:, s.k % 2], hid[:, s.k % 2], ACT.Copy).then_inc(hhi_ok, 1)

        drive(act, step, lambda s: None)

    @block.vector
    def _(dve):
        def accumulate(s):
            dve.wait_ge(d_ok, s.n + 1)
            if s.g == 0:
                dve.wait_ge(wcol_ok, s.head + 1)
            for i in range(4):
                tile = 4 * s.g + i
                m = dve.scalar_tensor_tensor(f[:, tile], psD[s.k % 2][i // 2][:, 256 * (i % 2):256 * (i % 2) + 256],
                                             wcol[:, s.par, tile:tile + 1], f[:, tile], ALU.mult, ALU.add)
            m.then_inc(acc_ok, 1)

        def step(s):
            dve.wait_ge(sil_ok, s.n + 1)
            dve.wait_ge(u_ok, s.n + 1)
            wait(dve, hlo_ok, s.n - 1)
            dve.tensor_tensor(hid[:, s.k % 2], psU[s.k % 2][:], sil[:, s.k % 2], ALU.mult).then_inc(hid_ok, 1)
            if exists(s.n - 1):
                accumulate(s.back(1))

        dve.wait_ge(zeroed, 1)
        drive(dve, step, lambda s: accumulate(s.back(1)))


def combine(nc, ctx, x2, s1, f, out):
    NP = 8
    sil = ctx.enter_context(nc.sbuf_tensor("silf", [P, 16, 256], F32))
    sil_ok, prod_ok, sum_ok, stored = (ctx.enter_context(nc.semaphore(n)) for n in ("silf_ok", "prod_ok", "sum_ok", "out_stored"))
    block = ctx.enter_context(nc.Block())
    two = lambda z, k: z[:, 2 * k:2 * k + 2].rearrange("p t d -> p (t d)")

    @block.scalar
    def _(act):
        for k in range(NP):
            act.activation(two(sil, k), two(f, k), ACT.Silu).then_inc(sil_ok, 1)

    @block.vector
    def _(dve):
        for k in range(NP):
            dve.wait_ge(sil_ok, k + 1)
            dve.tensor_tensor(two(sil, k), two(sil, k), two(s1, k), ALU.mult).then_inc(prod_ok, 1)

    @block.gpsimd
    def _(pool):
        for k in range(NP):
            pool.wait_ge(prod_ok, k + 1)
            pool.tensor_tensor(two(sil, k), two(sil, k), two(x2, k), ALU.add).then_inc(sum_ok, 1)

    @block.sync
    def _(sp):
        for k in range(NP):
            sp.wait_ge(sum_ok, k + 1)
            sp.dma_start(out.rearrange("(i p) d -> p i d", p=P)[:, 2 * k:2 * k + 2], sil[:, 2 * k:2 * k + 2]).then_inc(stored, 16)
        sp.wait_ge(stored, 16 * NP)


def build(nc, args, out, stop_after=None):
    T, D = 2048, 256
    with ExitStack() as all_ctx:
        def sb(ctx, name, shape, dt=F32):
            return ctx.enter_context(nc.sbuf_tensor(name, shape, dt))

        t = {
            "ident": sb(all_ctx, "ident", [P, P]),
            "neg_half": sb(all_ctx, "neg_half", [P, 16]),
        }
        x2 = sb(all_ctx, "x2", [P, T // P, D])
        with ExitStack() as c0:
            t["ident_r"] = sb(c0, "ident_r", [P, P], F32R)
            t["mask_r"] = sb(c0, "mask_r", [P, P], F32R)
            w = {
                "hi": sb(c0, "w_hi", [P, 4, 2, 256], F32R), "lo": sb(c0, "w_lo", [P, 4, 2, 256], F32R),
                "up_hi": sb(c0, "up_hi", [P, 2, 2, 1024], F32R), "up_lo": sb(c0, "up_lo", [P, 2, 2, 1024], F32R),
                "dn_hi": sb(c0, "dn_hi", [P, 8, 256], F32R), "dn_lo": sb(c0, "dn_lo", [P, 8, 256], F32R),
            }
            with ExitStack() as c:
                prepare_weights(nc, c, t, w, args)
            with ExitStack() as c:
                layer0(nc, c, t, args["x"], x2, w, None)
        def dump(src):
            with nc.semaphore("dumped") as done, nc.Block() as block:
                @block.sync
                def _(sp):
                    sp.dma_start(out.rearrange("(i p) d -> p i d", p=P), src[:]).then_inc(done, 16)
                    sp.wait_ge(done, 16)
        if stop_after == "0":
            return dump(x2)
        xhi = sb(all_ctx, "x1_hi", [P, 2, T], F32R)
        xlo = sb(all_ctx, "x1_lo", [P, 2, T], F32R)
        wts = sb(all_ctx, "wts", [P, 34, T // P])
        s1 = sb(all_ctx, "s1", [P, T // P, D])
        zeros = sb(all_ctx, "zeros", [P, 1024])
        f = sb(all_ctx, "f1", [P, T // P, D])
        with ExitStack() as c:
            normalise_and_route(nc, c, t, zeros, x2, xhi, xlo, wts, args)
        with ExitStack() as c:
            attention1(nc, c, zeros, xhi, xlo, s1, args)
        if stop_after == "1":
            return dump(s1)
        with ExitStack() as c:
            experts(nc, c, zeros, xhi, xlo, wts, f, args)
        with ExitStack() as c:
            combine(nc, c, x2, s1, f, out)


def layout(inputs):
    import numpy as np

    f = lambda name: np.asarray(inputs[name])
    hadamard = np.ones((1, 1), np.float32)
    for _ in range(7):
        hadamard = np.block([[hadamard, hadamard], [hadamard, -hadamard]])
    w_qkv = f("L1_attn_w_qkv")
    halves = lambda w: w.reshape(-1, 2, 128, 128).transpose(0, 2, 1, 3).reshape(-1, 128, 256)
    out = {
        "x": f("L0_attn_x").reshape(2048, 256),
        "qkvoT": np.stack([f("L0_attn_" + n).T for n in ("Wq", "Wk", "Wv", "Wo")]),
        "upT": np.stack([f("L0_ffn_W1").T, f("L0_ffn_W3").T]),
        "W2T": f("L0_ffn_W2").T,
        "ident": np.eye(128, dtype=np.float32),
        "hadamard": hadamard,
        "heads": np.concatenate(
            [halves(w_qkv[:, 2048 * j:2048 * (j + 1)].reshape(256, 16, 128).transpose(1, 0, 2)) for j in range(3)]
            + [f("L1_attn_w_o").reshape(16, 128, 256)], axis=2),
        "experts": np.concatenate(
            [halves(np.concatenate([f("L1_ffn_w_" + n), f("L1_ffn_sw_" + n).reshape(256, 2, 128).transpose(1, 0, 2)])) for n in ("gate", "up")]
            + [np.concatenate([f("L1_ffn_w_down"), f("L1_ffn_sw_down").reshape(2, 128, 256)])], axis=2),
        "router_w": f("L1_ffn_router_w"),
        "router_bias": f("L1_ffn_router_bias").reshape(1, 32),
        "earlier": np.tril(np.ones((8, 8), np.float32), -1).reshape(1, 64),
        "mask": np.triu(np.full((128, 128), MASKED, np.float32), 1),
    }
    return {k: np.ascontiguousarray(v) for k, v in out.items()}


def kernel(**inputs):
    import numpy as np
    import concourse.bacc as bacc
    from concourse.bass_utils import run_bass_kernel_spmd

    nc = bacc.Bacc("TRN2", target_bir_lowering=False, num_devices=1)
    arrays = {"in_" + k: v for k, v in layout(inputs).items()}
    args = {k[3:]: nc.dram_tensor(k, v.shape, mybir.dt.from_np(v.dtype), kind="ExternalInput").ap() for k, v in arrays.items()}
    out = nc.dram_tensor("out", (2048, 256), F32, kind="ExternalOutput").ap()
    build(nc, args, out)
    r = run_bass_kernel_spmd(nc, [arrays], core_ids=[0])
    return np.asarray(r.results[0]["out"]).reshape(8, 256, 256)
```

```python
from contextlib import ExitStack

import concourse.bass as bass
from concourse import mybir

P = 128
ALU = mybir.AluOpType
ACT = mybir.ActivationFunctionType
AX = mybir.AxisListType
F32 = mybir.dt.float32
F32R = mybir.dt.float32r
EPS = 1e-5
MASKED = -1e30


class Batch:

    def __init__(self, half, off):
        self.half, self.off = half, off
        self.par = off % 2
        self.n = 2 * half + off
        self.uses = half + off // 2 + 1

    def back(self, k):
        return Batch(self.half, self.off - k)


def wait(eng, sem, value):
    if isinstance(value, int) and value <= 0:
        return
    eng.wait_ge(sem, value)


def layer0(nc, ctx, t, x, x2, w, last_b):
    D, S, NB, NH = 256, 256, 8, 16
    NJ = 8

    def sb(name, shape, dt=F32):
        return ctx.enter_context(nc.sbuf_tensor(name, shape, dt))

    def ps(name, shape):
        return ctx.enter_context(nc.psum_tensor(name, shape, F32))

    def sem(name):
        return ctx.enter_context(nc.semaphore(name))

    stats = sb("stats", [P, 2, 6])
    mv = sb("mv", [P, 2, 2])
    veps = sb("veps", [P, 2])
    rstd = sb("rstd", [P, 2])
    xn = sb("xn", [P, 2, D])
    xhi = sb("xhi", [P, 2, 2, S], F32R)
    xlo = sb("xlo", [P, 2, 2, S], F32R)
    ch = [sb("qch", [P, 2, 2, S], F32R), sb("kch", [P, 2, 2, S], F32R)]
    chi, clo = [c[:, 0] for c in ch], [c[:, 1] for c in ch]
    qst = sb("qst", [P, 2, 8, S], F32R)
    kst = sb("kst", [P, 2, 8, S], F32R)
    VW = 8 * 144
    vhi = sb("vhi", [P, 2, 2, VW], F32R)
    vlo = sb("vlo", [P, 2, 2, VW], F32R)
    negmax = sb("negmax", [P, NH, 2])
    den = sb("den", [P, 2, 2, NH])
    rden = sb("rden", [P, 2, NH])
    rden_b = sb("rden_b", [P, 2, NH, 16])
    e = sb("e", [P, 4, 384])
    eThi = sb("eThi", [P, 4, 384], F32R)
    eTlo = sb("eTlo", [P, 4, 384], F32R)
    rT = sb("rT", [P, 512])
    ctxn = sb("ctxn", [P, 512])
    cxhi = sb("cxhi", [P, 2, S], F32R)
    cxlo = sb("cxlo", [P, 2, S], F32R)
    th = sb("th", [P, S])
    ga = sb("ga", [P, S])
    hid = sb("hid", [P, S])
    hhi = sb("hhi", [P, 2, S], F32R)
    hlo = sb("hlo", [P, 2, S], F32R)
    gf = sb("gf", [P, 512])
    sg = sb("sg", [P, 512])

    psS = [ps("psS0", [P, 512]), ps("psS1", [P, 512])]
    psT = [ps("psT0", [P, 512]), ps("psT1", [P, 512])]
    psC = ps("psC", [P, 512])
    psG = ps("psG", [P, 512])
    psF = ps("psF", [P, 512])
    psM = ps("psM", [P, 512])

    qk_dram = nc.dram_tensor("qk_scratch", [2, 2, 2, 2, P, S], F32, kind="Internal").ap()

    x_in = [sem("x_in_first"), sem("x_in_rest")]
    stats_ok, aggr_ok, veps_ok, rstd_ok, xn_ok = (sem(n) for n in ("stats_ok", "aggr_ok", "veps_ok", "rstd_ok", "xn_ok"))
    xT_ok, xhi_ok, xlo_ok = sem("xT_ok"), sem("xhi_ok"), sem("xlo_ok")
    proj_ok = [sem("q_ok"), sem("k_ok"), sem("v_ok")]
    phi_ok = [sem("qhi_ok"), sem("khi_ok"), sem("vhi_ok")]
    plo_ok = [sem("qlo_ok"), sem("klo_ok"), sem("vlo_ok")]
    stored = [[sem("q_stored0"), sem("q_stored1")], [sem("k_stored0"), sem("k_stored1")]]
    stacked = [sem("stacked0"), sem("stacked1")]
    scores_ok, max_ok, exp_ok, eT_ok, eThi_ok, eTlo_ok, pv_ok = (
        sem(n) for n in ("scores_ok", "max_ok", "exp_ok", "eT_ok", "eThi_ok", "eTlo_ok", "pv_ok"))
    up_ok, tanh_ok, gate_ok, hid_ok, hhi_ok, hlo_ok, down_ok = (
        sem(n) for n in ("up_ok", "tanh_ok", "gate_ok", "hid_ok", "hhi_ok", "hlo_ok", "down_ok"))
    rden_ok, rdenb_ok, rT_ok, rTc_ok, ctxn_ok, cxhi_ok, cxlo_ok, so_ok = (
        sem(n) for n in ("rden_ok", "rdenb_ok", "rT_ok", "rTc_ok", "ctxn_ok", "cxhi_ok", "cxlo_ok", "so_ok"))
    tanhf_ok, gf_ok, sg_ok, x2_ok = sem("tanhf_ok"), sem("gf_ok"), sem("sg_ok"), sem("x2_ok")
    zeroed = sem("zeroed")
    wait_done = sem("wait_done")

    def drive(eng, prepare, step):
        def batch(b, a, before):
            for h in range(NH):
                step(h, b, a, before)

        prepare(Batch(0, 0))
        batch(Batch(0, 0), Batch(0, 1), None)
        with eng.Fori(0, (NB - 2) // 2) as i:
            batch(Batch(i, 1), Batch(i, 2), Batch(i, 0))
            batch(Batch(i, 2), Batch(i, 3), Batch(i, 1))
        batch(Batch(NB // 2 - 1, 1), None, Batch(NB // 2 - 1, 0))
        for h in range(8):
            step(h, None, None, Batch(NB // 2 - 1, 1))

    def lagging(h, lag, b, before):
        if h >= lag:
            return (b, h - lag) if b is not None else None
        return (before, NH + h - lag) if before is not None else None

    def values_at(h, b, before):
        if h < 3:
            return [(before, k) for k in ((12, 13), (14,), (15,))[h]] if before is not None else []
        if h < 5 or b is None:
            return []
        return [(b, k) for k in ((0, 1) if h == 5 else (h - 4,))]

    def of_batch(buf, b):
        tiles = buf[:].rearrange("p (b t) d -> p b (t d)", t=2)
        return tiles[:, b.n] if isinstance(b.n, int) else tiles[:, bass.ds(b.n, 1)].rearrange("p o n -> p (o n)")

    block = ctx.enter_context(nc.Block())

    @block.sync
    def _(sp):
        def restack(a):
            done = a.n + 1 if isinstance(a.n, int) else sp.snap(a.n + 1)
            in_scratch = 16 * a.uses if isinstance(a.n, int) else sp.snap(16 * a.uses)
            used = 16 * (a.n - 1) if isinstance(a.n, int) else sp.snap(16 * (a.n - 1))
            wait(sp, stacked[a.par], 192 * (a.uses - 1))
            sp.sem_inc(wait_done, 1)
            wait(sp, scores_ok, used)
            sp.sem_inc(wait_done, 1)
            for i, dst in enumerate((qst, kst)):
                sp.wait_ge(plo_ok[i], done)
                sp.dma_start(qk_dram[a.par, i].rearrange("a m p s -> p (a m) s"), ch[i][:].rearrange("p a m s -> p (a m) s").bitcast(F32)).then_inc(stored[i][a.par], 16)
                sp.wait_ge(stored[i][a.par], in_scratch)
                for r in range(2):
                    for c, part in enumerate(((0, 0, 1), (0, 1, 0))[i]):
                        src = qk_dram[a.par, i, part].rearrange("m (j r d) s -> r d (m j) s", r=2, d=16)[r]
                        row = 64 * r + 16 * c
                        sp.dma_start(dst[row:row + 16, a.par].bitcast(F32), src).then_inc(stacked[a.par], 16)

        tiled = x.rearrange("(i p) d -> p i d", p=P)
        sp.dma_start(x2[:, 0:2], tiled[:, 0:2]).then_inc(x_in[0], 16)
        sp.dma_start(x2[:, 2:], tiled[:, 2:]).then_inc(x_in[1], 16)
        drive(sp, restack, lambda h, b, a, before: a is not None and h == 0 and restack(a))
        sp.wait_ge(stacked[0], 192 * (NB // 2))
        sp.wait_ge(stacked[1], 192 * (NB // 2))

    @block.tensor
    def _(pe):
        mm = pe.matmul

        def x_turn(a):
            pe.wait_ge(xn_ok, 2 * a.n + 2)
            if isinstance(a.n, int) and a.n < 2:
                wait(pe, plo_ok[2], a.n)
            else:
                pe.wait_ge(sg_ok, a.n - 1)
            for c in range(2):
                for i in range(2):
                    m = pe.transpose(psM[:, c * S + i * P:c * S + (i + 1) * P], xn[:, i, c * P:(c + 1) * P], t["ident"][:])
            m.then_inc(xT_ok, 1)

        def proj_qk(a, i):
            pe.wait_ge(xlo_ok if i == 0 else plo_ok[0], a.n + 1)
            for m in range(2):
                for c in range(2):
                    wc = (slice(None), i, c, slice(m * P, (m + 1) * P))
                    last = split3(mm, psM[:, m * S:(m + 1) * S], w["hi"][wc], w["lo"][wc],
                                  xhi[:, a.par, c], xlo[:, a.par, c], c == 0, c == 1)
            last.then_inc(proj_ok[i], 1)

        def proj_v(a):
            if isinstance(a.n, int) and a.n == 0:
                pe.wait_ge(plo_ok[1], 1)
            else:
                pe.wait_ge(rTc_ok, a.n)
            for m in range(2):
                for c in range(2):
                    tok = (slice(None), a.par, c, slice(m * P, (m + 1) * P))
                    last = split3(mm, psM[:, m * S:(m + 1) * S], xhi[tok], xlo[tok], w["hi"][:, 2, c], w["lo"][:, 2, c], c == 0, c == 1)
            last.then_inc(proj_ok[2], 1)

        def scores(b, h):
            wait(pe, exp_ok, 16 * b.n + h - 1)
            if h == 0:
                pe.wait_ge(stacked[b.par], 192 * b.uses)
            out = psS[h % 2]
            r = slice(64 * (h % 2), 64 * (h % 2) + 48)
            j = (h // 8) * 4 + (h % 8) // 2
            mm(out[:, 0:P], qst[r, b.par, j, 0:P], kst[r, b.par, j, 0:P], start=True, stop=False)
            mm(out[:, 0:P], t["ident_r"][:], t["mask_r"][:], start=False, stop=True)
            mm(out[:, P:3 * P], qst[r, b.par, j, P:2 * P], kst[r, b.par, j, 0:2 * P], start=True, stop=False, skip_group_check=True)
            mm(out[:, 2 * P:3 * P], t["ident_r"][:], t["mask_r"][:], start=False, stop=True, skip_group_check=True).then_inc(scores_ok, 1)

        def e_turn(b, h):
            pe.wait_ge(exp_ok, 16 * b.n + h + 1)
            wait(pe, eTlo_ok, 16 * b.n + h - 1)
            out = psT[h % 2]
            pe.transpose(out[:, 0:P], e[:, h % 4, 0:P], t["ident"][:])
            pe.transpose(out[:, P:2 * P], e[:, h % 4, P:2 * P], t["ident"][:])
            pe.transpose(out[:, 2 * P:3 * P], e[:, h % 4, 2 * P:3 * P], t["ident"][:]).then_inc(eT_ok, 1)

        def pv(b, h):
            pe.wait_ge(eTlo_ok, 16 * b.n + h + 1)
            if h == 0:
                pe.wait_ge(plo_ok[2], b.n + 1)
                wait(pe, ctxn_ok, b.n)
            g, hh = h // 8, h % 8
            vb = slice(hh * P, hh * P + P)
            o, q = g * S, h % 4
            split3(mm, psC[:, o:o + S], vhi[:, 0, g, vb], vlo[:, 0, g, vb], eThi[:, q, 0:S], eTlo[:, q, 0:S], hh == 0, False, True)
            split3(mm, psC[:, o + P:o + S], vhi[:, 1, g, vb], vlo[:, 1, g, vb], eThi[:, q, S:384], eTlo[:, q, S:384],
                   False, hh == 7, True).then_inc(pv_ok, 1)

        def up(b, j):
            wait(pe, hid_ok, 8 * b.n + j)
            for k in range(2):
                for c in range(2):
                    wc = (slice(None), k, c, slice(j * P, (j + 1) * P))
                    last = split3(mm, psG[:, k * S:(k + 1) * S], w["up_hi"][wc], w["up_lo"][wc],
                                  xhi[:, b.par, c], xlo[:, b.par, c], c == 0, c == 1)
            last.then_inc(up_ok, 1)

        def down(b, j):
            pe.wait_ge(hlo_ok, 8 * b.n + j + 1)
            if j == 0:
                wait(pe, gf_ok, b.n)
            for i in range(2):
                tok = (slice(None), j % 2, slice(i * P, (i + 1) * P))
                last = split3(mm, psF[:, i * D:(i + 1) * D], hhi[tok], hlo[tok], w["dn_hi"][:, j], w["dn_lo"][:, j],
                              j == 0 and i == 0, j == NJ - 1, True)
            last.then_inc(down_ok, 1)

        def rden_turn(b, a):
            pe.wait_ge(rdenb_ok, b.n + 1)
            if a is not None:
                pe.wait_ge(plo_ok[1], a.n + 1)
            else:
                pe.wait_ge(sg_ok, b.n)
            for g in range(2):
                for i in range(2):
                    src = rden_b[:, i, 8 * g:8 * g + 8].rearrange("p h d -> p (h d)")
                    m = pe.transpose(psM[:, g * S + i * P:g * S + (i + 1) * P], src, t["ident"][:])
            m.then_inc(rT_ok, 1)

        def out_proj(b, a):
            if a is not None:
                pe.wait_ge(plo_ok[2], a.n + 1)
            else:
                pe.wait_ge(rTc_ok, b.n + 1)
            pe.wait_ge(cxlo_ok, b.n + 1)
            for i in range(2):
                for g in range(2):
                    tok = (slice(None), g, slice(i * P, (i + 1) * P))
                    last = split3(mm, psM[:, i * D:(i + 1) * D], cxhi[tok], cxlo[tok], w["hi"][:, 3, g], w["lo"][:, 3, g], g == 0, g == 1)
            last.then_inc(so_ok, 1)

        def prepare(a):
            x_turn(a)
            proj_qk(a, 0)
            proj_qk(a, 1)

        def step(h, b, a, before):
            if b is not None:
                scores(b, h)
                if h % 2 == 0:
                    up(b, h // 2)
            if h % 2 == 1:
                late = lagging(h, 3, b, before)
                if late:
                    down(late[0], late[1] // 2)
            late = lagging(h, 2, b, before)
            if late:
                e_turn(*late)
            if before is not None and h == 1:
                rden_turn(before, b)
            for late in values_at(h, b, before):
                pv(*late)
            if b is not None and h == 2:
                proj_v(b)
            if before is not None and h == 5:
                out_proj(before, b)
            if a is not None and h == 7:
                x_turn(a)
            if a is not None and h in (9, 11):
                proj_qk(a, (h - 9) // 2)

        drive(pe, prepare, step)

    @block.scalar
    def _(act):
        def x_hi(a):
            act.wait_ge(xT_ok, a.n + 1)
            act.activation(xhi[:, a.par].rearrange("p c s -> p (c s)"), psM[:], ACT.Copy).then_inc(xhi_ok, 1)

        def qk_hi(a, i):
            act.wait_ge(proj_ok[i], a.n + 1)
            prev = a.back(1)
            wait(act, stored[i][prev.par], 16 * prev.uses)
            act.activation(chi[i].rearrange("p c s -> p (c s)"), psM[:], ACT.Copy, scale=0.25 if i == 0 else 1.0).then_inc(phi_ok[i], 1)

        def v_dst(buf, i):
            return buf[:, i].rearrange("p g (h c) -> p g h c", c=144)[:, :, :, 0:16]

        def v_hi(a):
            act.wait_ge(proj_ok[2], a.n + 1)
            if a.off == 0:
                act.wait_ge(zeroed, 1)
            wait(act, pv_ok, 16 * a.n)
            for i in range(2):
                m = act.activation(v_dst(vhi, i), psM[:, i * D:(i + 1) * D].rearrange("p (g h d) -> p g h d", g=2, d=16), ACT.Copy)
            m.then_inc(phi_ok[2], 1)

        def exp(b, h):
            act.wait_ge(max_ok, 16 * b.n + h + 1)
            wait(act, eT_ok, 16 * b.n + h - 3)
            act.activation(e[:, h % 4, 0:P], psS[h % 2][:, 0:P], ACT.Exp, bias=negmax[:, h, 0:1], accum_out=den[:, b.par, 0, h:h + 1])
            act.activation(e[:, h % 4, P:384], psS[h % 2][:, P:384], ACT.Exp, bias=negmax[:, h, 1:2],
                           accum_out=den[:, b.par, 1, h:h + 1]).then_inc(exp_ok, 1)

        def eT_hi(b, h):
            act.wait_ge(eT_ok, 16 * b.n + h + 1)
            wait(act, pv_ok, 16 * b.n + h - 3)
            act.activation(eThi[:, h % 4], psT[h % 2][:, 0:384], ACT.Copy).then_inc(eThi_ok, 1)

        def gate_tanh(b, j):
            act.wait_ge(up_ok, 8 * b.n + j + 1)
            wait(act, gate_ok, 8 * b.n + j)
            act.activation(th[:], psG[:, 0:S], ACT.Tanh, scale=0.5).then_inc(tanh_ok, 1)

        def hid_hi(b, j):
            act.wait_ge(hid_ok, 8 * b.n + j + 1)
            wait(act, down_ok, 8 * b.n + j - 1)
            act.activation(hhi[:, j % 2], hid[:], ACT.Copy).then_inc(hhi_ok, 1)

        def prepare(a):
            x_hi(a)
            qk_hi(a, 0)
            qk_hi(a, 1)

        def finish(b, part):
            if part == 0:
                act.wait_ge(down_ok, 8 * b.n + 8)
                wait(act, sg_ok, b.n)
                act.activation(gf[:], psF[:], ACT.Tanh, scale=0.5).then_inc(tanhf_ok, 1)
            elif part == 1:
                act.wait_ge(rT_ok, b.n + 1)
                wait(act, ctxn_ok, b.n)
                act.activation(rT[:], psM[:], ACT.Copy).then_inc(rTc_ok, 1)
            else:
                act.wait_ge(ctxn_ok, b.n + 1)
                wait(act, so_ok, b.n)
                act.activation(cxhi[:].rearrange("p g s -> p (g s)"), ctxn[:], ACT.Copy).then_inc(cxhi_ok, 1)

        def step(h, b, a, before):
            if b is not None:
                exp(b, h)
                if a is not None and h == 8:
                    x_hi(a)
                if a is not None and h in (10, 12):
                    qk_hi(a, (h - 10) // 2)
                if h % 2 == 0:
                    gate_tanh(b, h // 2)
                else:
                    hid_hi(b, h // 2)
            if before is not None and h == 2:
                finish(before, 0)
            late = lagging(h, 2, b, before)
            if late:
                eT_hi(*late)
            if before is not None and h == 1:
                finish(before, 1)
            if b is not None and h == 3:
                v_hi(b)
            if before is not None and h == 4:
                finish(before, 2)

        drive(act, prepare, step)

    @block.vector
    def _(dve):
        def x_stats(a):
            if isinstance(a.n, int) and a.n < 2:
                dve.wait_ge(x_in[a.n], 16)
            for i in range(2):
                m = dve.bn_stats(stats[:, i], of_batch(x2, a)[:, D * i:D * (i + 1)])
            m.then_inc(stats_ok, 1)
            dve.wait_ge(stats_ok, a.n + 1)
            dve.sem_inc(wait_done, 1)
            for i in range(2):
                m = dve.bn_aggr(mv[:, i], stats[:, i])
            m.then_inc(aggr_ok, 1)
            dve.wait_ge(aggr_ok, a.n + 1)
            dve.tensor_scalar(veps[:], mv[:, :, 1], EPS, None, ALU.add).then_inc(veps_ok, 1)

        def x_norm(a):
            dve.wait_ge(rstd_ok, a.n + 1)
            wait(dve, xT_ok, a.n)
            for i in range(2):
                dve.tensor_scalar(xn[:, i], of_batch(x2, a)[:, D * i:D * (i + 1)], mv[:, i, 0:1], rstd[:, i:i + 1], ALU.subtract, ALU.mult).then_inc(xn_ok, 1)

        def x_lo(a):
            dve.wait_ge(xhi_ok, a.n + 1)
            dve.tensor_tensor(xlo[:, a.par].rearrange("p c s -> p (c s)"), psM[:], xhi[:, a.par].bitcast(F32).rearrange("p c s -> p (c s)"),
                              ALU.subtract).then_inc(xlo_ok, 1)

        def qk_lo(a, i):
            dve.wait_ge(phi_ok[i], a.n + 1)
            flat = lambda z: z.rearrange("p c s -> p (c s)")
            if i == 0:
                dve.scalar_tensor_tensor(flat(clo[0]), psM[:], 0.25, flat(chi[0].bitcast(F32)), ALU.mult, ALU.subtract).then_inc(plo_ok[0], 1)
            else:
                dve.tensor_tensor(flat(clo[1]), psM[:], flat(chi[1].bitcast(F32)), ALU.subtract).then_inc(plo_ok[1], 1)

        def v_dst(buf, i):
            return buf.rearrange("p g (h c) -> p g h c", c=144)[:, :, :, 0:16]

        def v_lo(a):
            dve.wait_ge(phi_ok[2], a.n + 1)
            if a.off == 0:
                dve.wait_ge(zeroed, 2)
            for i in range(2):
                m = dve.tensor_tensor(v_dst(vlo[:, i], i), psM[:, i * D:(i + 1) * D].rearrange("p (g h d) -> p g h d", g=2, d=16),
                                      v_dst(vhi[:, i].bitcast(F32), i), ALU.subtract)
            m.then_inc(plo_ok[2], 1)

        def row_max(b, h):
            dve.wait_ge(scores_ok, 16 * b.n + h + 1)
            dve.tensor_reduce(negmax[:, h, 0:1], psS[h % 2][:, 0:P], AX.X, ALU.max, negate=True)
            dve.tensor_reduce(negmax[:, h, 1:2], psS[h % 2][:, P:384], AX.X, ALU.max, negate=True).then_inc(max_ok, 1)

        def eT_lo(b, h):
            dve.wait_ge(eThi_ok, 16 * b.n + h + 1)
            dve.tensor_tensor(eTlo[:, h % 4], psT[h % 2][:, 0:384], eThi[:, h % 4].bitcast(F32), ALU.subtract).then_inc(eTlo_ok, 1)

        def gate(b, j):
            dve.wait_ge(tanh_ok, 8 * b.n + j + 1)
            dve.scalar_tensor_tensor(ga[:], th[:], 1.0, psG[:, 0:S], ALU.add, ALU.mult).then_inc(gate_ok, 1)
            dve.wait_ge(gate_ok, 8 * b.n + j + 1)
            wait(dve, hlo_ok, 8 * b.n + j)
            dve.scalar_tensor_tensor(hid[:], ga[:], 0.5, psG[:, S:2 * S], ALU.mult, ALU.mult).then_inc(hid_ok, 1)

        def prepare(a):
            x_stats(a)
            x_norm(a)
            x_lo(a)
            qk_lo(a, 0)
            qk_lo(a, 1)

        def finish(b, part):
            if part == 0:
                dve.wait_ge(exp_ok, 16 * b.n + 16)
                dve.reciprocal(rden[:], den[:, b.par]).then_inc(rden_ok, 1)
                dve.wait_ge(rden_ok, b.n + 1)
                wait(dve, rT_ok, b.n)
                dve.tensor_copy(rden_b[:], rden[:].unsqueeze(3).to_broadcast([P, 2, NH, 16])).then_inc(rdenb_ok, 1)
            elif part == 1:
                dve.wait_ge(tanhf_ok, b.n + 1)
                dve.scalar_tensor_tensor(gf[:], gf[:], 1.0, psF[:], ALU.add, ALU.mult).then_inc(gf_ok, 1)
            elif part == 2:
                dve.wait_ge(rTc_ok, b.n + 1)
                dve.wait_ge(pv_ok, 16 * b.n + 16)
                dve.tensor_tensor(ctxn[:], psC[:], rT[:], ALU.mult).then_inc(ctxn_ok, 1)
            elif part == 3:
                dve.wait_ge(cxhi_ok, b.n + 1)
                dve.tensor_tensor(cxlo[:].rearrange("p g s -> p (g s)"), ctxn[:], cxhi[:].bitcast(F32).rearrange("p g s -> p (g s)"),
                                  ALU.subtract).then_inc(cxlo_ok, 1)
            else:
                dve.wait_ge(so_ok, b.n + 1)
                wait(dve, x2_ok, b.n)
                dve.scalar_tensor_tensor(sg[:], gf[:], 0.5, psM[:], ALU.mult, ALU.mult).then_inc(sg_ok, 1)

        def step(h, b, a, before):
            if b is not None:
                row_max(b, h)
                if a is not None:
                    if h == 1:
                        x_stats(a)
                    if h == 5:
                        x_norm(a)
                    if h == 8:
                        x_lo(a)
                    if h in (10, 12):
                        qk_lo(a, (h - 10) // 2)
                if h % 2 == 0:
                    gate(b, h // 2)
            if before is not None and h == 0:
                finish(before, 0)
            if before is not None and h == 3:
                finish(before, 1)
            late = lagging(h, 2, b, before)
            if late:
                eT_lo(*late)
            if before is not None and h == 3:
                finish(before, 2)
            if b is not None and h == 3:
                v_lo(b)
            if before is not None and h == 4:
                finish(before, 3)
            if before is not None and h == 6:
                finish(before, 4)

        drive(dve, prepare, step)

    @block.gpsimd
    def _(pool):
        def deviation(a):
            pool.wait_ge(veps_ok, a.n + 1)
            pool.tensor_tensor(rstd[:], veps[:], t["neg_half"][:, 0:2], ALU.pow).then_inc(rstd_ok, 1)

        def hid_lo(b, j):
            pool.wait_ge(hhi_ok, 8 * b.n + j + 1)
            pool.tensor_tensor(hlo[:, j % 2], hid[:], hhi[:, j % 2].bitcast(F32), ALU.subtract).then_inc(hlo_ok, 1)

        def residual(b):
            pool.wait_ge(sg_ok, b.n + 1)
            pool.tensor_tensor(of_batch(x2, b), sg[:], of_batch(x2, b), ALU.add).then_inc(x2_ok, 1)

        def step(h, b, a, before):
            if b is not None and h % 2 == 1:
                hid_lo(b, h // 2)
            if a is not None and h == 2:
                deviation(a)
            if before is not None and h == 7:
                residual(before)

        pool.memset(vhi[:].bitcast(F32), 0.0).then_inc(zeroed, 1)
        pool.memset(vlo[:].bitcast(F32), 0.0).then_inc(zeroed, 1)
        drive(pool, deviation, step)


def prepare_weights(nc, ctx, t, w, args):
    def sb(name, shape, dt=F32):
        return ctx.enter_context(nc.sbuf_tensor(name, shape, dt))

    def sem(name):
        return ctx.enter_context(nc.semaphore(name))

    raw = sb("raw_qkvo", [P, 4, 2, 256])
    raw_up = sb("raw_up", [P, 2, 2, 1024])
    raw_dn = sb("raw_dn", [P, 8, 256])
    fold = [sb("fold0", [P, 8, 256]), sb("fold1", [P, 8, 256])]
    had = sb("had", [P, P])
    mask = sb("mask", [P, P])
    psW = [ctx.enter_context(nc.psum_tensor(f"psW{i}", [P, 512], F32)) for i in range(4)]
    const_in, dn_in, qkvo_in, up_in = sem("const_in"), sem("dn_in"), sem("qkvo_in"), sem("up_in")
    folded, rotated, dnhi_ok, split_a, split_d, split_p = (
        sem(n) for n in ("folded", "rotated", "dnhi_ok", "split_a", "split_d", "split_p"))
    block = ctx.enter_context(nc.Block())
    flat4 = lambda z: z.rearrange("p a b c -> p (a b c)")

    @block.sync
    def _(sp):
        sp.dma_start(raw_dn[:], args["W2T"].rearrange("(c p) d -> p c d", p=P)).then_inc(dn_in, 16)
        sp.dma_start(had[:], args["hadamard"]).then_inc(const_in, 16)
        sp.dma_start(t["ident"][:], args["ident"]).then_inc(const_in, 16)
        sp.dma_start(mask[:], args["mask"]).then_inc(const_in, 16)
        sp.dma_start(raw[:], args["qkvoT"].rearrange("a (c p) n -> p a c n", p=P)).then_inc(qkvo_in, 16)
        sp.dma_start(raw_up[:], args["upT"].rearrange("a (c p) n -> p a c n", p=P)).then_inc(up_in, 16)

    @block.vector
    def _(dve):
        dve.wait_ge(dn_in, 16)
        src = raw_dn
        for n, half in enumerate((1, 2, 4)):
            dst = fold[n % 2]
            s = src[:].rearrange("p (a two b) d -> p a two (b d)", two=2, b=half)
            d = dst[:].rearrange("p (a two b) d -> p a two (b d)", two=2, b=half)
            if n:
                dve.wait_ge(folded, 2 * n)
            dve.tensor_tensor(d[:, :, 0], s[:, :, 0], s[:, :, 1], ALU.add).then_inc(folded, 1)
            dve.tensor_tensor(d[:, :, 1], s[:, :, 0], s[:, :, 1], ALU.subtract).then_inc(folded, 1)
            src = dst
        for i in range(4):
            dve.wait_ge(dnhi_ok, i + 1)
            dve.scalar_tensor_tensor(w["dn_lo"][:, 2 * i:2 * i + 2].rearrange("p c d -> p (c d)"), psW[i][:], 1.0 / 32.0,
                                     w["dn_hi"][:, 2 * i:2 * i + 2].bitcast(F32).rearrange("p c d -> p (c d)"), ALU.mult, ALU.subtract)
        dve.wait_ge(split_a, 3)
        dve.tensor_tensor(flat4(w["up_lo"][:]), flat4(raw_up[:]), flat4(w["up_hi"][:].bitcast(F32)), ALU.subtract)

    @block.tensor
    def _(pe):
        pe.wait_ge(folded, 6)
        pe.wait_ge(const_in, 48)
        for i in range(4):
            src = fold[0][:, 2 * i:2 * i + 2].rearrange("p c d -> p (c d)")
            pe.matmul(psW[i][:], had[:], src, start=True, stop=True).then_inc(rotated, 1)

    @block.scalar
    def _(act):
        act.wait_ge(const_in, 48)
        act.activation(t["ident_r"][:], t["ident"][:], ACT.Copy).then_inc(split_a, 1)
        act.activation(t["mask_r"][:], mask[:], ACT.Copy).then_inc(split_a, 1)
        act.wait_ge(up_in, 16)
        act.activation(flat4(w["up_hi"][:]), flat4(raw_up[:]), ACT.Copy).then_inc(split_a, 1)
        for i in range(4):
            act.wait_ge(rotated, i + 1)
            act.activation(w["dn_hi"][:, 2 * i:2 * i + 2].rearrange("p c d -> p (c d)"), psW[i][:], ACT.Copy, scale=1.0 / 32.0).then_inc(dnhi_ok, 1)

    @block.gpsimd
    def _(pool):
        pool.memset(t["neg_half"][:], -0.5)
        pool.wait_ge(qkvo_in, 16)
        pool.tensor_copy(flat4(w["hi"][:]), flat4(raw[:])).then_inc(split_p, 1)
        pool.wait_ge(split_p, 1)
        pool.tensor_tensor(flat4(w["lo"][:]), flat4(raw[:]), flat4(w["hi"][:].bitcast(F32)), ALU.subtract)


def split3(mm, out, a_hi, a_lo, b_hi, b_lo, start, stop, skip=False):
    mm(out, a_hi, b_hi, start=start, stop=False, skip_group_check=skip)
    mm(out, a_hi, b_lo, start=False, stop=False, skip_group_check=skip)
    return mm(out, a_lo, b_hi, start=False, stop=stop, skip_group_check=skip)


def normalise_and_route(nc, ctx, t, zeros, x2, xhi, xlo, wts, args):
    NT, NE = 16, 32

    def sb(name, shape, dt=F32):
        return ctx.enter_context(nc.sbuf_tensor(name, shape, dt))

    def sem(name):
        return ctx.enter_context(nc.semaphore(name))

    stats = sb("stats1", [P, NT, 6])
    mv = sb("mv1", [P, NT, 2])
    veps = sb("veps1", [P, NT])
    rstd = sb("rstd1", [P, NT])
    xn = sb("xn1", [P, NT, 256])
    rw = sb("rw", [P, 2, NE])
    rw_hi = sb("rw_hi", [P, 2, NE], F32R)
    rw_lo = sb("rw_lo", [P, 2, NE], F32R)
    bias = sb("bias", [P, NE])
    tri = sb("tri", [P, 64])
    score = sb("score", [P, NT, NE])
    biased = sb("biased", [P, NT, NE])
    pmax = sb("pmax", [P, NT * 8, 2])
    pmin = sb("pmin", [P, NT * 8, 2])
    top = sb("top", [P, NT * 8])
    low = sb("low", [P, NT * 8])
    other = sb("other", [P, NT * 8])
    second = sb("second", [P, NT * 8])
    group = sb("group", [P, NT, 8])
    above = sb("above", [P, NT, 8, 8])
    equal = sb("equal", [P, NT, 8, 8])
    rank = sb("rank", [P, NT, 8])
    keep = sb("keep", [P, NT, 8])
    masked = sb("masked", [P, NT, NE])
    best = sb("best", [P, NT, 8])
    rest = sb("rest", [P, NT, NE])
    chosen = sb("chosen", [P, NT, NE])
    total = sb("total", [P, NT])
    rtotal = sb("rtotal", [P, NT])
    psX = [ctx.enter_context(nc.psum_tensor(f"psX{i}", [P, 512], F32)) for i in range(4)]
    psL = ctx.enter_context(nc.psum_tensor("psL", [P, NT, NE], F32))

    (const_in, stats_ok, aggr_ok, veps_ok, rstd_ok, xn_ok, xT_ok, xhi_ok, xlo_ok, rw_ok, logits_ok, score_ok, chain) = (
        sem(n) for n in ("const1_in", "stats1_ok", "aggr1_ok", "veps1_ok", "rstd1_ok", "xn1_ok", "xT1_ok", "xhi1_ok", "xlo1_ok",
                         "rw_ok", "logits_ok", "score_ok", "route_step"))
    block = ctx.enter_context(nc.Block())
    pair = lambda z, k: z[:, :, 256 * k:256 * (k + 1)]

    @block.sync
    def _(sp):
        sp.dma_start(rw[:], args["router_w"].rearrange("(c p) e -> p c e", p=P)).then_inc(const_in, 16)
        sp.dma_start(bias[:], args["router_bias"].broadcast_to([P, NE])).then_inc(const_in, 16)
        sp.dma_start(tri[:], args["earlier"].broadcast_to([P, 64])).then_inc(const_in, 16)

    @block.gpsimd
    def _(pool):
        pool.wait_ge(veps_ok, 1)
        pool.tensor_tensor(rstd[:], veps[:], t["neg_half"][:], ALU.pow).then_inc(rstd_ok, 1)
        pool.memset(zeros[:], 0.0)
        pool.memset(wts[:, NE:NE + 2], 1.0)
        pool.wait_ge(const_in, 48)
        pool.tensor_copy(rw_hi[:], rw[:]).then_inc(rw_ok, 1)
        pool.wait_ge(rw_ok, 1)
        pool.tensor_tensor(rw_lo[:], rw[:], rw_hi[:].bitcast(F32), ALU.subtract).then_inc(rw_ok, 1)

    @block.tensor
    def _(pe):
        for k in range(NT // 2):
            pe.wait_ge(xn_ok, 2 * k + 2)
            wait(pe, xlo_ok, k - 3)
            for c in range(2):
                for i in range(2):
                    m = pe.transpose(psX[k % 4][:, c * 256 + i * P:c * 256 + (i + 1) * P], xn[:, 2 * k + i, c * P:(c + 1) * P], t["ident"][:])
            m.then_inc(xT_ok, 1)
        pe.wait_ge(rw_ok, 2)
        pe.wait_ge(xlo_ok, NT // 2)
        for i in range(NT):
            for c in range(2):
                tok = (slice(None), c, slice(i * P, (i + 1) * P))
                m = split3(pe.matmul, psL[:, i], xhi[tok], xlo[tok], rw_hi[:, c], rw_lo[:, c], c == 0, c == 1)
        m.then_inc(logits_ok, 1)

    @block.scalar
    def _(act):
        for k in range(NT // 2):
            act.wait_ge(xT_ok, k + 1)
            act.activation(pair(xhi, k), psX[k % 4][:].rearrange("p (c s) -> p c s", c=2), ACT.Copy).then_inc(xhi_ok, 1)
        act.wait_ge(logits_ok, 1)
        act.activation(score[:], psL[:], ACT.Sigmoid).then_inc(score_ok, 1)

    @block.vector
    def _(dve):
        for i in range(NT):
            m = dve.bn_stats(stats[:, i], x2[:, i])
        m.then_inc(stats_ok, 1)
        dve.wait_ge(stats_ok, 1)
        for i in range(NT):
            m = dve.bn_aggr(mv[:, i], stats[:, i])
        m.then_inc(aggr_ok, 1)
        dve.wait_ge(aggr_ok, 1)
        dve.tensor_scalar(veps[:], mv[:, :, 1], EPS, None, ALU.add).then_inc(veps_ok, 1)
        dve.wait_ge(rstd_ok, 1)

        def x_lo(k):
            dve.wait_ge(xhi_ok, k + 1)
            dve.tensor_tensor(pair(xlo, k), psX[k % 4][:].rearrange("p (c s) -> p c s", c=2), pair(xhi, k).bitcast(F32), ALU.subtract).then_inc(xlo_ok, 1)

        for i in range(NT):
            dve.tensor_scalar(xn[:, i], x2[:, i], mv[:, i, 0:1], rstd[:, i:i + 1], ALU.subtract, ALU.mult).then_inc(xn_ok, 1)
            if i % 2 == 1 and i >= 3:
                x_lo((i - 3) // 2)
        x_lo(NT // 2 - 1)
        dve.wait_ge(score_ok, 1)
        dve.wait_ge(const_in, 48)
        steps = 0

        def step(ins):
            nonlocal steps
            steps += 1
            ins.then_inc(chain, 1)
            dve.wait_ge(chain, steps)

        step(dve.tensor_tensor(biased[:], score[:], bias[:].unsqueeze(1).to_broadcast([P, NT, NE]), ALU.add))
        quad = biased[:].rearrange("p t (g b a) -> p (t g) b a", b=2, a=2)
        dve.tensor_tensor(pmax[:], quad[:, :, :, 0], quad[:, :, :, 1], ALU.max)
        step(dve.tensor_tensor(pmin[:], quad[:, :, :, 0], quad[:, :, :, 1], ALU.min))
        dve.tensor_tensor(top[:], pmax[:, :, 0], pmax[:, :, 1], ALU.max)
        dve.tensor_tensor(low[:], pmax[:, :, 0], pmax[:, :, 1], ALU.min)
        step(dve.tensor_tensor(other[:], pmin[:, :, 0], pmin[:, :, 1], ALU.max))
        step(dve.tensor_tensor(second[:], low[:], other[:], ALU.max))
        step(dve.tensor_tensor(group[:].rearrange("p t g -> p (t g)"), top[:], second[:], ALU.add))
        mine = group[:].unsqueeze(3).to_broadcast([P, NT, 8, 8])
        theirs = group[:].unsqueeze(2).to_broadcast([P, NT, 8, 8])
        dve.tensor_tensor(above[:], theirs, mine, ALU.is_gt)
        step(dve.tensor_tensor(equal[:], theirs, mine, ALU.is_equal))
        flat = lambda z: z.rearrange("p t g h -> p t (g h)")
        step(dve.tensor_tensor(flat(equal[:]), flat(equal[:]), tri[:].unsqueeze(1).to_broadcast([P, NT, 64]), ALU.mult))
        step(dve.tensor_tensor(flat(above[:]), flat(above[:]), flat(equal[:]), ALU.add))
        step(dve.tensor_reduce(rank[:], above[:], AX.X, ALU.add))
        step(dve.tensor_scalar(keep[:], rank[:], 3.5, None, ALU.is_lt))
        by_group = lambda z: z.rearrange("p t (g a) -> p (t g) a", a=4)
        step(dve.tensor_tensor(by_group(masked[:]), by_group(biased[:]),
                               keep[:].rearrange("p t g -> p (t g)").unsqueeze(2).to_broadcast([P, NT * 8, 4]), ALU.mult))
        step(dve.tensor_scalar(masked[:], masked[:], 0.0, None, ALU.add))
        for i in range(NT):
            m = dve.max(best[:, i], masked[:, i])
        step(m)
        for i in range(NT):
            m = dve.match_replace(rest[:, i], best[:, i], masked[:, i], -3.0e38)
        step(m)
        step(dve.tensor_tensor(chosen[:], rest[:], masked[:], ALU.not_equal))
        step(dve.tensor_tensor(chosen[:], chosen[:], score[:], ALU.mult))
        step(dve.tensor_reduce(total[:], chosen[:], AX.X, ALU.add))
        step(dve.reciprocal(rtotal[:], total[:]))
        dve.scalar_tensor_tensor(wts[:, 0:NE].rearrange("p e t -> p t e"), chosen[:], 2.5,
                                 rtotal[:].unsqueeze(2).to_broadcast([P, NT, NE]), ALU.mult, ALU.mult)


class Step:

    def __init__(self, i, k):
        self.i, self.k = i, k
        self.n = 8 * i + k
        self.g = k % 4
        self.par = (k // 4) % 2
        self.head = 2 * i + k // 4

    def back(self, j):
        return Step(self.i, self.k - j)


def attention1(nc, ctx, zeros, xhi, xlo, s1, args):
    NH, NG = 16, 4
    SCALE = 128.0 ** -0.5

    def sb(name, shape, dt=F32):
        return ctx.enter_context(nc.sbuf_tensor(name, shape, dt))

    def sem(name):
        return ctx.enter_context(nc.semaphore(name))

    raw = sb("raw_head", [P, 2, 1024])
    whi = sb("head_hi", [P, 2, 1024], F32R)
    wlo = sb("head_lo", [P, 2, 1024], F32R)
    ohi = [sb("q1_hi", [P, 512], F32R), sb("k1_hi", [P, 512], F32R)]
    olo = [sb("q1_lo", [P, 512], F32R), sb("k1_lo", [P, 512], F32R)]
    negmax = sb("negmax1", [P, 4])
    e = sb("e1", [P, 4, 256])
    den = sb("den1", [P, 4])
    rden = sb("rden1", [P, 4])
    rden_b = sb("rden1_b", [P, 4, P])
    csum = sb("csum", [P, 512])
    val = sb("val", [P, 512])
    vhi = sb("val_hi", [P, 2, 512], F32R)
    vlo = sb("val_lo", [P, 2, 512], F32R)
    ps = lambda n: ctx.enter_context(nc.psum_tensor(n, [P, 512], F32))
    psQK, psV, psS, psC, psO = [ps("psQ1"), ps("psK1")], ps("psV1"), [ps("psS10"), ps("psS11")], ps("psC1"), [ps("psO0"), ps("psO1")]

    raw_in = [sem("head_in0"), sem("head_in1")]
    whi_ok, wlo_ok, v_ok, scores_ok, max_ok, exp_ok, rden_ok, rdenb_ok, c_ok, csum_ok, val_ok, vhi_ok, vlo_ok, o_ok, acc_ok, zeroed = (
        sem("a1_" + n) for n in ("whi_ok", "wlo_ok", "v_ok", "scores_ok", "max_ok", "exp_ok", "rden_ok", "rdenb_ok",
                                 "c_ok", "csum_ok", "val_ok", "vhi_ok", "vlo_ok", "o_ok", "acc_ok", "zeroed"))
    p_ok = [sem("a1_q_ok"), sem("a1_k_ok")]
    phi_ok = [sem("a1_qhi_ok"), sem("a1_khi_ok")]
    plo_ok = [sem("a1_qlo_ok"), sem("a1_klo_ok")]
    block = ctx.enter_context(nc.Block())

    def drive(eng, step, tail):
        for k in range(8):
            step(Step(0, k))
        with eng.Fori(1, NH // 2) as i:
            for k in range(8):
                step(Step(i, k))
        for k in range(2):
            tail(Step(NH // 2, k))

    exists = lambda n: not isinstance(n, int) or n >= 0

    @block.sync
    def _(sp):
        def load(head_i, par, uses):
            wait(sp, wlo_ok, 2 * (uses - 2) + par + 1)
            src = args["heads"][2 * head_i + par]
            sp.dma_start(raw[:, par], src).then_inc(raw_in[par], 16)
        for par in range(2):
            load(0, par, 1)
        with sp.Fori(1, NH // 2) as i:
            for par in range(2):
                load(i, par, i + 1)

    @block.gpsimd
    def _(pool):
        def split(i, par):
            pool.wait_ge(raw_in[par], 16 * (i + 1))
            wait(pool, o_ok, 8 * i + 4 * par - 4)
            pool.tensor_tensor(whi[:, par], raw[:, par], zeros[:, 0:raw.shape[2]], ALU.add).then_inc(whi_ok, 1)
            pool.wait_ge(whi_ok, 2 * i + par + 1)
            pool.tensor_tensor(wlo[:, par], raw[:, par], whi[:, par].bitcast(F32), ALU.subtract).then_inc(wlo_ok, 1)

        def finish(s):
            pool.wait_ge(val_ok, s.n + 1)
            wait(pool, o_ok, s.n - 1)
            pool.tensor_tensor(vhi[:, s.k % 2], val[:], zeros[:, 0:512], ALU.add).then_inc(vhi_ok, 1)
            pool.wait_ge(vhi_ok, s.n + 1)
            pool.tensor_tensor(vlo[:, s.k % 2], val[:], vhi[:, s.k % 2].bitcast(F32), ALU.subtract).then_inc(vlo_ok, 1)

        def step(s, last=False):
            if exists(s.n - 1):
                finish(s.back(1))
            if s.g == 2 and not last:
                nxt = Step(s.i, s.k + 4)
                split(nxt.i if nxt.k < 8 else nxt.i + 1, nxt.par)

        pool.memset(s1[:], 0.0).then_inc(zeroed, 1)
        split(0, 0)
        for k in range(8):
            step(Step(0, k))
        with pool.Fori(1, NH // 2 - 1) as i:
            for k in range(8):
                step(Step(i, k))
        for k in range(8):
            step(Step(NH // 2 - 1, k), last=k >= 4)
        finish(Step(NH // 2, -1))

    @block.tensor
    def _(pe):
        mm = pe.matmul

        def proj(s, j, out, done):
            for c in range(2):
                wc = (slice(None), s.par, slice(256 * j + P * c, 256 * j + P * (c + 1)))
                tok = (slice(None), c, slice(512 * s.g, 512 * s.g + 512))
                last = split3(mm, out[:], whi[wc], wlo[wc], xhi[tok], xlo[tok], c == 0, c == 1)
            last.then_inc(done, 1)

        def column_sums(s):
            pe.wait_ge(rdenb_ok, s.n + 1)
            wait(pe, csum_ok, s.n)
            for b in range(2):
                mm(psC[:, 256 * b:256 * b + 256], rden_b[:, 2 * b], e[:, 2 * b], start=True, stop=False)
                last = mm(psC[:, 256 * b:256 * b + 256], rden_b[:, 2 * b + 1], e[:, 2 * b + 1], start=False, stop=True)
            last.then_inc(c_ok, 1)

        def out_proj(s):
            pe.wait_ge(vlo_ok, s.n + 1)
            wait(pe, acc_ok, s.n)
            wo = (slice(None), s.par, slice(768, 1024))
            for i in range(4):
                tok = (slice(None), s.k % 2, slice(P * i, P * i + P))
                last = split3(mm, psO[i // 2][:, 256 * (i % 2):256 * (i % 2) + 256], vhi[tok], vlo[tok], whi[wo], wlo[wo], True, True)
            last.then_inc(o_ok, 1)

        def step(s):
            if s.g == 0:
                pe.wait_ge(wlo_ok, s.head + 1)
            for j in range(2):
                wait(pe, plo_ok[j], s.n)
                proj(s, j, psQK[j], p_ok[j])
            if exists(s.n - 2):
                out_proj(s.back(2))
            if exists(s.n - 1):
                column_sums(s.back(1))
            pe.wait_ge(plo_ok[1], s.n + 1)
            for b in range(2):
                wait(pe, exp_ok, 2 * s.n + b - 1)
                for i in range(2):
                    qt = slice(256 * b + P * i, 256 * b + P * (i + 1))
                    kt = slice(256 * b, 256 * b + 256)
                    last = split3(mm, psS[b][:, 256 * i:256 * i + 256], ohi[0][:, qt], olo[0][:, qt], ohi[1][:, kt], olo[1][:, kt], True, True)
                last.then_inc(scores_ok, 1)
            wait(pe, val_ok, s.n)
            proj(s, 2, psV, v_ok)

        def tail(s):
            if s.k == 0:
                column_sums(s.back(1))
            out_proj(s.back(2))

        drive(pe, step, tail)

    @block.scalar
    def _(act):
        def csum_copy(s):
            act.wait_ge(c_ok, s.n + 1)
            wait(act, val_ok, s.n)
            act.activation(csum[:], psC[:], ACT.Copy).then_inc(csum_ok, 1)

        def step(s):
            for j in range(2):
                act.wait_ge(p_ok[j], s.n + 1)
                wait(act, scores_ok, 2 * s.n)
                act.activation(ohi[j][:], psQK[j][:], ACT.Copy, scale=SCALE if j == 0 else 1.0).then_inc(phi_ok[j], 1)
            if exists(s.n - 1):
                csum_copy(s.back(1))
            for b in range(2):
                act.wait_ge(max_ok, 2 * s.n + b + 1)
                for i in range(2):
                    c = 2 * b + i
                    m = act.activation(e[:, c], psS[b][:, 256 * i:256 * i + 256], ACT.Exp, bias=negmax[:, c:c + 1], accum_out=den[:, c:c + 1])
                m.then_inc(exp_ok, 1)

        drive(act, step, lambda s: csum_copy(s.back(1)) if s.k == 0 else None)

    @block.vector
    def _(dve):
        def proj_lo(s, j):
            dve.wait_ge(phi_ok[j], s.n + 1)
            if j == 0:
                dve.scalar_tensor_tensor(olo[0][:], psQK[0][:], SCALE, ohi[0][:].bitcast(F32), ALU.mult, ALU.subtract).then_inc(plo_ok[0], 1)
            else:
                dve.tensor_tensor(olo[1][:], psQK[1][:], ohi[1][:].bitcast(F32), ALU.subtract).then_inc(plo_ok[1], 1)

        def reciprocals(s):
            dve.wait_ge(exp_ok, 2 * s.n + 2)
            dve.reciprocal(rden[:], den[:]).then_inc(rden_ok, 1)
            wait(dve, c_ok, s.n)
            dve.wait_ge(rden_ok, s.n + 1)
            dve.tensor_copy(rden_b[:], rden[:].unsqueeze(2).to_broadcast([P, 4, P])).then_inc(rdenb_ok, 1)

        def values(s):
            dve.wait_ge(csum_ok, s.n + 1)
            dve.wait_ge(v_ok, s.n + 1)
            wait(dve, vlo_ok, s.n)
            dve.tensor_tensor(val[:], psV[:], csum[:], ALU.mult).then_inc(val_ok, 1)

        def accumulate(s):
            dve.wait_ge(o_ok, s.n + 1)
            for i in range(2):
                dst = s1[:, 4 * s.g + 2 * i:4 * s.g + 2 * i + 2].rearrange("p t d -> p (t d)")
                m = dve.tensor_tensor(dst, psO[i][:], dst, ALU.add)
            m.then_inc(acc_ok, 1)

        def step(s):
            proj_lo(s, 0)
            if exists(s.n - 1):
                reciprocals(s.back(1))
            proj_lo(s, 1)
            if exists(s.n - 1):
                values(s.back(1))
            for b in range(2):
                dve.wait_ge(scores_ok, 2 * s.n + b + 1)
                dve.tensor_reduce(negmax[:, 2 * b:2 * b + 2], psS[b][:].rearrange("p (i k) -> p i k", i=2), AX.X, ALU.max, negate=True).then_inc(max_ok, 1)
            if exists(s.n - 2):
                accumulate(s.back(2))

        def tail(s):
            if s.k == 0:
                reciprocals(s.back(1))
                values(s.back(1))
            accumulate(s.back(2))

        dve.wait_ge(zeroed, 1)
        drive(dve, step, tail)


def experts(nc, ctx, zeros, xhi, xlo, wts, f, args):
    NE = 34

    def sb(name, shape, dt=F32):
        return ctx.enter_context(nc.sbuf_tensor(name, shape, dt))

    def sem(name):
        return ctx.enter_context(nc.semaphore(name))

    raw = sb("raw_expert", [P, 2, 768])
    whi = sb("expert_hi", [P, 2, 768], F32R)
    wlo = sb("expert_lo", [P, 2, 768], F32R)
    wcol = sb("wcol", [P, 2, 16])
    sil = sb("sil", [P, 2, 512])
    hid = sb("hid1", [P, 2, 512])
    hhi = sb("hid1_hi", [P, 2, 512], F32R)
    hlo = sb("hid1_lo", [P, 2, 512], F32R)
    ps = lambda n: ctx.enter_context(nc.psum_tensor(n, [P, 512], F32))
    psG, psU = [ps("psG0"), ps("psG1")], [ps("psU0"), ps("psU1")]
    psD = [[ps("psD00"), ps("psD01")], [ps("psD10"), ps("psD11")]]
    raw_in = [sem("expert_in0"), sem("expert_in1")]
    whi_ok, wlo_ok, wcol_ok, g_ok, u_ok, sil_ok, hid_ok, hhi_ok, hlo_ok, d_ok, acc_ok, zeroed = (
        sem("m_" + n) for n in ("whi_ok", "wlo_ok", "wcol_ok", "g_ok", "u_ok", "sil_ok", "hid_ok", "hhi_ok", "hlo_ok", "d_ok", "acc_ok", "zeroed"))
    block = ctx.enter_context(nc.Block())
    exists = lambda n: not isinstance(n, int) or n >= 0

    def drive(eng, step, tail):
        for k in range(8):
            step(Step(0, k))
        with eng.Fori(1, NE // 2) as i:
            for k in range(8):
                step(Step(i, k))
        tail(Step(NE // 2, 0))

    @block.sync
    def _(sp):
        def load(i, par):
            wait(sp, wlo_ok, 2 * i + par - 1)
            sp.dma_start(raw[:, par], args["experts"][2 * i + par]).then_inc(raw_in[par], 16)
        for par in range(2):
            load(0, par)
        with sp.Fori(1, NE // 2) as i:
            for par in range(2):
                load(i, par)

    @block.gpsimd
    def _(pool):
        def split(i, par):
            pool.wait_ge(raw_in[par], 16 * (i + 1))
            wait(pool, d_ok, 8 * i + 4 * par - 4)
            pool.tensor_tensor(whi[:, par], raw[:, par], zeros[:, 0:raw.shape[2]], ALU.add).then_inc(whi_ok, 1)
            pool.wait_ge(whi_ok, 2 * i + par + 1)
            pool.tensor_tensor(wlo[:, par], raw[:, par], whi[:, par].bitcast(F32), ALU.subtract).then_inc(wlo_ok, 1)
            wait(pool, acc_ok, 8 * i + 4 * par - 4)
            src = wts[:, 2 * i + par] if isinstance(i, int) else wts[:, bass.ds(2 * i + par, 1)].rearrange("p o t -> p (o t)")
            pool.tensor_tensor(wcol[:, par], src, zeros[:, 0:16], ALU.add).then_inc(wcol_ok, 1)

        def step(s, last=False):
            pool.wait_ge(hhi_ok, s.n + 1)
            pool.tensor_tensor(hlo[:, s.k % 2], hid[:, s.k % 2], hhi[:, s.k % 2].bitcast(F32), ALU.subtract).then_inc(hlo_ok, 1)
            if s.g == 1 and not last:
                nxt = Step(s.i, s.k + 4)
                split(nxt.i if nxt.k < 8 else nxt.i + 1, nxt.par)

        pool.memset(f[:], 0.0).then_inc(zeroed, 1)
        split(0, 0)
        for k in range(8):
            step(Step(0, k))
        with pool.Fori(1, NE // 2 - 1) as i:
            for k in range(8):
                step(Step(i, k))
        for k in range(8):
            step(Step(NE // 2 - 1, k), last=k >= 4)

    @block.tensor
    def _(pe):
        mm = pe.matmul

        def proj(s, j, out, done):
            for c in range(2):
                wc = (slice(None), s.par, slice(256 * j + P * c, 256 * j + P * (c + 1)))
                tok = (slice(None), c, slice(512 * s.g, 512 * s.g + 512))
                last = split3(mm, out[:], whi[wc], wlo[wc], xhi[tok], xlo[tok], c == 0, c == 1)
            last.then_inc(done, 1)

        def down(s):
            pe.wait_ge(hlo_ok, s.n + 1)
            wait(pe, acc_ok, s.n - 1)
            wd = (slice(None), s.par, slice(512, 768))
            for i in range(4):
                tok = (slice(None), s.k % 2, slice(P * i, P * i + P))
                out = psD[s.k % 2][i // 2][:, 256 * (i % 2):256 * (i % 2) + 256]
                last = split3(mm, out, hhi[tok], hlo[tok], whi[wd], wlo[wd], True, True)
            last.then_inc(d_ok, 1)

        def step(s):
            if s.g == 0:
                pe.wait_ge(wlo_ok, s.head + 1)
            wait(pe, sil_ok, s.n - 1)
            proj(s, 0, psG[s.k % 2], g_ok)
            wait(pe, hid_ok, s.n - 1)
            proj(s, 1, psU[s.k % 2], u_ok)
            if exists(s.n - 1):
                down(s.back(1))

        drive(pe, step, lambda s: down(s.back(1)))

    @block.scalar
    def _(act):
        def step(s):
            act.wait_ge(g_ok, s.n + 1)
            wait(act, hid_ok, s.n - 1)
            act.activation(sil[:, s.k % 2], psG[s.k % 2][:], ACT.Silu).then_inc(sil_ok, 1)
            act.wait_ge(hid_ok, s.n + 1)
            wait(act, d_ok, s.n - 1)
            act.activation(hhi[:, s.k % 2], hid[:, s.k % 2], ACT.Copy).then_inc(hhi_ok, 1)

        drive(act, step, lambda s: None)

    @block.vector
    def _(dve):
        def accumulate(s):
            dve.wait_ge(d_ok, s.n + 1)
            if s.g == 0:
                dve.wait_ge(wcol_ok, s.head + 1)
            for i in range(4):
                tile = 4 * s.g + i
                m = dve.scalar_tensor_tensor(f[:, tile], psD[s.k % 2][i // 2][:, 256 * (i % 2):256 * (i % 2) + 256],
                                             wcol[:, s.par, tile:tile + 1], f[:, tile], ALU.mult, ALU.add)
            m.then_inc(acc_ok, 1)

        def step(s):
            dve.wait_ge(sil_ok, s.n + 1)
            dve.wait_ge(u_ok, s.n + 1)
            wait(dve, hlo_ok, s.n - 1)
            dve.tensor_tensor(hid[:, s.k % 2], psU[s.k % 2][:], sil[:, s.k % 2], ALU.mult).then_inc(hid_ok, 1)
            if exists(s.n - 1):
                accumulate(s.back(1))

        dve.wait_ge(zeroed, 1)
        drive(dve, step, lambda s: accumulate(s.back(1)))


def combine(nc, ctx, x2, s1, f, out):
    NP = 8
    sil = ctx.enter_context(nc.sbuf_tensor("silf", [P, 16, 256], F32))
    sil_ok, prod_ok, sum_ok, stored = (ctx.enter_context(nc.semaphore(n)) for n in ("silf_ok", "prod_ok", "sum_ok", "out_stored"))
    block = ctx.enter_context(nc.Block())
    two = lambda z, k: z[:, 2 * k:2 * k + 2].rearrange("p t d -> p (t d)")

    @block.scalar
    def _(act):
        for k in range(NP):
            act.activation(two(sil, k), two(f, k), ACT.Silu).then_inc(sil_ok, 1)

    @block.vector
    def _(dve):
        for k in range(NP):
            dve.wait_ge(sil_ok, k + 1)
            dve.tensor_tensor(two(sil, k), two(sil, k), two(s1, k), ALU.mult).then_inc(prod_ok, 1)

    @block.gpsimd
    def _(pool):
        for k in range(NP):
            pool.wait_ge(prod_ok, k + 1)
            pool.tensor_tensor(two(sil, k), two(sil, k), two(x2, k), ALU.add).then_inc(sum_ok, 1)

    @block.sync
    def _(sp):
        for k in range(NP):
            sp.wait_ge(sum_ok, k + 1)
            sp.dma_start(out.rearrange("(i p) d -> p i d", p=P)[:, 2 * k:2 * k + 2], sil[:, 2 * k:2 * k + 2]).then_inc(stored, 16)
        sp.wait_ge(stored, 16 * NP)


def build(nc, args, out, stop_after=None):
    T, D = 2048, 256
    with ExitStack() as all_ctx:
        def sb(ctx, name, shape, dt=F32):
            return ctx.enter_context(nc.sbuf_tensor(name, shape, dt))

        t = {
            "ident": sb(all_ctx, "ident", [P, P]),
            "neg_half": sb(all_ctx, "neg_half", [P, 16]),
        }
        x2 = sb(all_ctx, "x2", [P, T // P, D])
        with ExitStack() as c0:
            t["ident_r"] = sb(c0, "ident_r", [P, P], F32R)
            t["mask_r"] = sb(c0, "mask_r", [P, P], F32R)
            w = {
                "hi": sb(c0, "w_hi", [P, 4, 2, 256], F32R), "lo": sb(c0, "w_lo", [P, 4, 2, 256], F32R),
                "up_hi": sb(c0, "up_hi", [P, 2, 2, 1024], F32R), "up_lo": sb(c0, "up_lo", [P, 2, 2, 1024], F32R),
                "dn_hi": sb(c0, "dn_hi", [P, 8, 256], F32R), "dn_lo": sb(c0, "dn_lo", [P, 8, 256], F32R),
            }
            with ExitStack() as c:
                prepare_weights(nc, c, t, w, args)
            with ExitStack() as c:
                layer0(nc, c, t, args["x"], x2, w, None)
        def dump(src):
            with nc.semaphore("dumped") as done, nc.Block() as block:
                @block.sync
                def _(sp):
                    sp.dma_start(out.rearrange("(i p) d -> p i d", p=P), src[:]).then_inc(done, 16)
                    sp.wait_ge(done, 16)
        if stop_after == "0":
            return dump(x2)
        xhi = sb(all_ctx, "x1_hi", [P, 2, T], F32R)
        xlo = sb(all_ctx, "x1_lo", [P, 2, T], F32R)
        wts = sb(all_ctx, "wts", [P, 34, T // P])
        s1 = sb(all_ctx, "s1", [P, T // P, D])
        zeros = sb(all_ctx, "zeros", [P, 1024])
        f = sb(all_ctx, "f1", [P, T // P, D])
        with ExitStack() as c:
            normalise_and_route(nc, c, t, zeros, x2, xhi, xlo, wts, args)
        with ExitStack() as c:
            attention1(nc, c, zeros, xhi, xlo, s1, args)
        if stop_after == "1":
            return dump(s1)
        with ExitStack() as c:
            experts(nc, c, zeros, xhi, xlo, wts, f, args)
        with ExitStack() as c:
            combine(nc, c, x2, s1, f, out)


def layout(inputs):
    import numpy as np

    f = lambda name: np.asarray(inputs[name])
    hadamard = np.ones((1, 1), np.float32)
    for _ in range(7):
        hadamard = np.block([[hadamard, hadamard], [hadamard, -hadamard]])
    w_qkv = f("L1_attn_w_qkv")
    halves = lambda w: w.reshape(-1, 2, 128, 128).transpose(0, 2, 1, 3).reshape(-1, 128, 256)
    out = {
        "x": f("L0_attn_x").reshape(2048, 256),
        "qkvoT": np.stack([f("L0_attn_" + n).T for n in ("Wq", "Wk", "Wv", "Wo")]),
        "upT": np.stack([f("L0_ffn_W1").T, f("L0_ffn_W3").T]),
        "W2T": f("L0_ffn_W2").T,
        "ident": np.eye(128, dtype=np.float32),
        "hadamard": hadamard,
        "heads": np.concatenate(
            [halves(w_qkv[:, 2048 * j:2048 * (j + 1)].reshape(256, 16, 128).transpose(1, 0, 2)) for j in range(3)]
            + [f("L1_attn_w_o").reshape(16, 128, 256)], axis=2),
        "experts": np.concatenate(
            [halves(np.concatenate([f("L1_ffn_w_" + n), f("L1_ffn_sw_" + n).reshape(256, 2, 128).transpose(1, 0, 2)])) for n in ("gate", "up")]
            + [np.concatenate([f("L1_ffn_w_down"), f("L1_ffn_sw_down").reshape(2, 128, 256)])], axis=2),
        "router_w": f("L1_ffn_router_w"),
        "router_bias": f("L1_ffn_router_bias").reshape(1, 32),
        "earlier": np.tril(np.ones((8, 8), np.float32), -1).reshape(1, 64),
        "mask": np.triu(np.full((128, 128), MASKED, np.float32), 1),
    }
    return {k: np.ascontiguousarray(v) for k, v in out.items()}


def kernel(**inputs):
    import numpy as np
    import concourse.bacc as bacc
    from concourse.bass_utils import run_bass_kernel_spmd

    nc = bacc.Bacc("TRN2", target_bir_lowering=False, num_devices=1)
    arrays = {"in_" + k: v for k, v in layout(inputs).items()}
    args = {k[3:]: nc.dram_tensor(k, v.shape, mybir.dt.from_np(v.dtype), kind="ExternalInput").ap() for k, v in arrays.items()}
    out = nc.dram_tensor("out", (2048, 256), F32, kind="ExternalOutput").ap()
    build(nc, args, out)
    r = run_bass_kernel_spmd(nc, [arrays], core_ids=[0])
    return np.asarray(r.results[0]["out"]).reshape(8, 256, 256)
```

```python
from contextlib import ExitStack

import concourse.bass as bass
from concourse import mybir

P = 128
ALU = mybir.AluOpType
ACT = mybir.ActivationFunctionType
AX = mybir.AxisListType
F32 = mybir.dt.float32
F32R = mybir.dt.float32r
F16 = mybir.dt.float16
I32 = mybir.dt.int32
EPS = 1e-5
MASKED = -1e30
NBLK = 160
RING = 8
TOP = 32768.0


class Batch:

    def __init__(self, half, off):
        self.half, self.off = half, off
        self.par = off % 2
        self.n = 2 * half + off
        self.uses = half + off // 2 + 1

    def back(self, k):
        return Batch(self.half, self.off - k)


def wait(eng, sem, value):
    if isinstance(value, int) and value <= 0:
        return
    eng.wait_ge(sem, value)


def layer0(nc, ctx, t, x2, x2_dram, w):
    D, S, NB, NH = 256, 256, 8, 16
    NJ = 8

    def sb(name, shape, dt=F32):
        return ctx.enter_context(nc.sbuf_tensor(name, shape, dt))

    def ps(name, shape):
        return ctx.enter_context(nc.psum_tensor(name, shape, F32))

    def sem(name):
        return ctx.enter_context(nc.semaphore(name))

    stats = sb("stats", [P, 2, 6])
    mv = sb("mv", [P, 2, 2])
    veps = sb("veps", [P, 2])
    rstd = sb("rstd", [P, 2])
    xn = sb("xn", [P, 2, D])
    xhi = sb("xhi", [P, 2, 2, S], F32R)
    xlo = sb("xlo", [P, 2, 2, S], F32R)
    ch = [sb("qch", [P, 2, 2, S], F32R), sb("kch", [P, 2, 2, S], F32R)]
    chi, clo = [c[:, 0] for c in ch], [c[:, 1] for c in ch]
    qst = sb("qst", [P, 2, 8, S], F32R)
    kst = sb("kst", [P, 2, 8, S], F32R)
    VW = 8 * 144
    vhi = sb("vhi", [P, 2, 2, VW], F32R)
    vlo = sb("vlo", [P, 2, 2, VW], F32R)
    negmax = sb("negmax", [P, NH, 2])
    den = sb("den", [P, 2, 2, NH])
    rden = sb("rden", [P, 2, NH])
    rden_b = sb("rden_b", [P, 2, NH, 16])
    e = sb("e", [P, 4, 384])
    eThi = sb("eThi", [P, 4, 384], F32R)
    eTlo = sb("eTlo", [P, 4, 384], F32R)
    rT = sb("rT", [P, 512])
    ctxn = sb("ctxn", [P, 512])
    cxhi = sb("cxhi", [P, 2, S], F32R)
    cxlo = sb("cxlo", [P, 2, S], F32R)
    th = sb("th", [P, S])
    ga = sb("ga", [P, S])
    hid = sb("hid", [P, S])
    hhi = sb("hhi", [P, 2, S], F32R)
    hlo = sb("hlo", [P, 2, S], F32R)
    gf = sb("gf", [P, 512])
    sg = sb("sg", [P, 512])

    psS = [ps("psS0", [P, 512]), ps("psS1", [P, 512])]
    psT = [ps("psT0", [P, 512]), ps("psT1", [P, 512])]
    psC = ps("psC", [P, 512])
    psG = ps("psG", [P, 512])
    psF = ps("psF", [P, 512])
    psM = ps("psM", [P, 512])

    qk_dram = nc.dram_tensor("qk_scratch", [2, 2, 2, 2, P, S], F32, kind="Internal").ap()

    stats_ok, aggr_ok, veps_ok, rstd_ok, xn_ok = (sem(n) for n in ("stats_ok", "aggr_ok", "veps_ok", "rstd_ok", "xn_ok"))
    xT_ok, xhi_ok, xlo_ok = sem("xT_ok"), sem("xhi_ok"), sem("xlo_ok")
    proj_ok = [sem("q_ok"), sem("k_ok"), sem("v_ok")]
    phi_ok = [sem("qhi_ok"), sem("khi_ok"), sem("vhi_ok")]
    plo_ok = [sem("qlo_ok"), sem("klo_ok"), sem("vlo_ok")]
    stored = [[sem("q_stored0"), sem("q_stored1")], [sem("k_stored0"), sem("k_stored1")]]
    stacked = [sem("stacked0"), sem("stacked1")]
    scores_ok, max_ok, exp_ok, eT_ok, eThi_ok, eTlo_ok, pv_ok = (
        sem(n) for n in ("scores_ok", "max_ok", "exp_ok", "eT_ok", "eThi_ok", "eTlo_ok", "pv_ok"))
    up_ok, tanh_ok, gate_ok, hid_ok, hhi_ok, hlo_ok, down_ok = (
        sem(n) for n in ("up_ok", "tanh_ok", "gate_ok", "hid_ok", "hhi_ok", "hlo_ok", "down_ok"))
    rden_ok, rdenb_ok, rT_ok, rTc_ok, ctxn_ok, cxhi_ok, cxlo_ok, so_ok = (
        sem(n) for n in ("rden_ok", "rdenb_ok", "rT_ok", "rTc_ok", "ctxn_ok", "cxhi_ok", "cxlo_ok", "so_ok"))
    tanhf_ok, gf_ok, sg_ok, x2_ok = sem("tanhf_ok"), sem("gf_ok"), sem("sg_ok"), sem("x2_ok")
    x2_stored = t["x2_stored"]
    zeroed = sem("zeroed")
    wait_done = t["wait_done"]

    def drive(eng, prepare, step):
        def batch(b, a, before):
            for h in range(NH):
                step(h, b, a, before)

        prepare(Batch(0, 0))
        batch(Batch(0, 0), Batch(0, 1), None)
        with eng.Fori(0, (NB - 2) // 2) as i:
            batch(Batch(i, 1), Batch(i, 2), Batch(i, 0))
            batch(Batch(i, 2), Batch(i, 3), Batch(i, 1))
        batch(Batch(NB // 2 - 1, 1), None, Batch(NB // 2 - 1, 0))
        for h in range(8):
            step(h, None, None, Batch(NB // 2 - 1, 1))

    def lagging(h, lag, b, before):
        if h >= lag:
            return (b, h - lag) if b is not None else None
        return (before, NH + h - lag) if before is not None else None

    def values_at(h, b, before):
        if h < 3:
            return [(before, k) for k in ((12, 13), (14,), (15,))[h]] if before is not None else []
        if h < 5 or b is None:
            return []
        return [(b, k) for k in ((0, 1) if h == 5 else (h - 4,))]

    def of_batch(buf, b):
        tiles = buf[:].rearrange("p (b t) d -> p b (t d)", t=2)
        return tiles[:, b.n] if isinstance(b.n, int) else tiles[:, bass.ds(b.n, 1)].rearrange("p o n -> p (o n)")

    block = ctx.enter_context(nc.Block())

    @block.sync
    def _(sp):
        def restack(a):
            done = a.n + 1 if isinstance(a.n, int) else sp.snap(a.n + 1)
            in_scratch = 16 * a.uses if isinstance(a.n, int) else sp.snap(16 * a.uses)
            used = 16 * (a.n - 1) if isinstance(a.n, int) else sp.snap(16 * (a.n - 1))
            wait(sp, stacked[a.par], 192 * (a.uses - 1))
            sp.sem_inc(wait_done, 1)
            wait(sp, scores_ok, used)
            sp.sem_inc(wait_done, 1)
            def to_scratch(i):
                sp.wait_ge(plo_ok[i], done)
                sp.dma_start(qk_dram[a.par, i].rearrange("a m p s -> p (a m) s"), ch[i][:].rearrange("p a m s -> p (a m) s").bitcast(F32)).then_inc(stored[i][a.par], 16)

            at_first = isinstance(a.n, int) and a.n == 0
            if at_first:
                to_scratch(0)
                to_scratch(1)
            for i, dst in enumerate((qst, kst)):
                if not at_first:
                    to_scratch(i)
                sp.wait_ge(stored[i][a.par], in_scratch)
                for r in range(2):
                    for c, part in enumerate(((0, 0, 1), (0, 1, 0))[i]):
                        src = qk_dram[a.par, i, part].rearrange("m (j r d) s -> r d (m j) s", r=2, d=16)[r]
                        row = 64 * r + 16 * c
                        sp.dma_start(dst[row:row + 16, a.par].bitcast(F32), src).then_inc(stacked[a.par], 16)

        def store_x2(b):
            done = b.n + 1 if isinstance(b.n, int) else sp.snap(b.n + 1)
            sp.wait_ge(x2_ok, done)
            sp.sem_inc(wait_done, 1)
            dst = x2_dram.rearrange("(b t p) d -> b p t d", t=2, p=P)[b.n]
            sp.dma_start(dst, of_batch(x2, b).rearrange("p (t d) -> p t d", t=2)).then_inc(x2_stored, 16)

        def step(h, b, a, before):
            if a is not None and h == 0:
                restack(a)
            if before is not None and h == 7:
                store_x2(before)

        drive(sp, restack, step)
        sp.wait_ge(stacked[0], 192 * (NB // 2))
        sp.wait_ge(stacked[1], 192 * (NB // 2))

    @block.tensor
    def _(pe):
        mm = pe.matmul

        def x_turn(a):
            pe.wait_ge(xn_ok, 2 * a.n + 2)
            if isinstance(a.n, int) and a.n < 2:
                wait(pe, plo_ok[2], a.n)
            else:
                pe.wait_ge(sg_ok, a.n - 1)
            for c in range(2):
                for i in range(2):
                    m = pe.transpose(psM[:, c * S + i * P:c * S + (i + 1) * P], xn[:, i, c * P:(c + 1) * P], t["ident"][:])
            m.then_inc(xT_ok, 1)

        def proj_qk(a, i):
            pe.wait_ge(xlo_ok if i == 0 else plo_ok[0], a.n + 1)
            for m in range(2):
                for c in range(2):
                    wc = (slice(None), i, c, slice(m * P, (m + 1) * P))
                    last = split3(mm, psM[:, m * S:(m + 1) * S], w["hi"][wc], w["lo"][wc],
                                  xhi[:, a.par, c], xlo[:, a.par, c], c == 0, c == 1)
            last.then_inc(proj_ok[i], 1)

        def proj_v(a):
            if isinstance(a.n, int) and a.n == 0:
                pe.wait_ge(plo_ok[1], 1)
            else:
                pe.wait_ge(rTc_ok, a.n)
            for m in range(2):
                for c in range(2):
                    tok = (slice(None), a.par, c, slice(m * P, (m + 1) * P))
                    last = split3(mm, psM[:, m * S:(m + 1) * S], xhi[tok], xlo[tok], w["hi"][:, 2, c], w["lo"][:, 2, c], c == 0, c == 1)
            last.then_inc(proj_ok[2], 1)

        def scores(b, h):
            wait(pe, exp_ok, 16 * b.n + h - 1)
            if h == 0:
                pe.wait_ge(stacked[b.par], 192 * b.uses)
            out = psS[h % 2]
            r = slice(64 * (h % 2), 64 * (h % 2) + 48)
            j = (h // 8) * 4 + (h % 8) // 2
            mm(out[:, 0:P], qst[r, b.par, j, 0:P], kst[r, b.par, j, 0:P], start=True, stop=False)
            mm(out[:, 0:P], t["ident_r"][:], t["mask_r"][:], start=False, stop=True)
            mm(out[:, P:3 * P], qst[r, b.par, j, P:2 * P], kst[r, b.par, j, 0:2 * P], start=True, stop=False, skip_group_check=True)
            mm(out[:, 2 * P:3 * P], t["ident_r"][:], t["mask_r"][:], start=False, stop=True, skip_group_check=True).then_inc(scores_ok, 1)

        def e_turn(b, h):
            pe.wait_ge(exp_ok, 16 * b.n + h + 1)
            wait(pe, eTlo_ok, 16 * b.n + h - 1)
            out = psT[h % 2]
            pe.transpose(out[:, 0:P], e[:, h % 4, 0:P], t["ident"][:])
            pe.transpose(out[:, P:2 * P], e[:, h % 4, P:2 * P], t["ident"][:])
            pe.transpose(out[:, 2 * P:3 * P], e[:, h % 4, 2 * P:3 * P], t["ident"][:]).then_inc(eT_ok, 1)

        def pv(b, h):
            pe.wait_ge(eTlo_ok, 16 * b.n + h + 1)
            if h == 0:
                pe.wait_ge(plo_ok[2], b.n + 1)
                wait(pe, ctxn_ok, b.n)
            g, hh = h // 8, h % 8
            vb = slice(hh * P, hh * P + P)
            o, q = g * S, h % 4
            split3(mm, psC[:, o:o + S], vhi[:, 0, g, vb], vlo[:, 0, g, vb], eThi[:, q, 0:S], eTlo[:, q, 0:S], hh == 0, False, True)
            split3(mm, psC[:, o + P:o + S], vhi[:, 1, g, vb], vlo[:, 1, g, vb], eThi[:, q, S:384], eTlo[:, q, S:384],
                   False, hh == 7, True).then_inc(pv_ok, 1)

        def up(b, j):
            wait(pe, hid_ok, 8 * b.n + j)
            for k in range(2):
                for c in range(2):
                    wc = (slice(None), k, c, slice(j * P, (j + 1) * P))
                    last = split3(mm, psG[:, k * S:(k + 1) * S], w["up_hi"][wc], w["up_lo"][wc],
                                  xhi[:, b.par, c], xlo[:, b.par, c], c == 0, c == 1)
            last.then_inc(up_ok, 1)

        def down(b, j):
            pe.wait_ge(hlo_ok, 8 * b.n + j + 1)
            if j == 0:
                wait(pe, gf_ok, b.n)
            for i in range(2):
                tok = (slice(None), j % 2, slice(i * P, (i + 1) * P))
                last = split3(mm, psF[:, i * D:(i + 1) * D], hhi[tok], hlo[tok], w["dn_hi"][:, j], w["dn_lo"][:, j],
                              j == 0 and i == 0, j == NJ - 1, True)
            last.then_inc(down_ok, 1)

        def rden_turn(b, a):
            pe.wait_ge(rdenb_ok, b.n + 1)
            if a is not None:
                pe.wait_ge(plo_ok[1], a.n + 1)
            else:
                pe.wait_ge(sg_ok, b.n)
            for g in range(2):
                for i in range(2):
                    src = rden_b[:, i, 8 * g:8 * g + 8].rearrange("p h d -> p (h d)")
                    m = pe.transpose(psM[:, g * S + i * P:g * S + (i + 1) * P], src, t["ident"][:])
            m.then_inc(rT_ok, 1)

        def out_proj(b, a):
            if a is not None:
                pe.wait_ge(plo_ok[2], a.n + 1)
            else:
                pe.wait_ge(rTc_ok, b.n + 1)
            pe.wait_ge(cxlo_ok, b.n + 1)
            for i in range(2):
                for g in range(2):
                    tok = (slice(None), g, slice(i * P, (i + 1) * P))
                    last = split3(mm, psM[:, i * D:(i + 1) * D], cxhi[tok], cxlo[tok], w["hi"][:, 3, g], w["lo"][:, 3, g], g == 0, g == 1)
            last.then_inc(so_ok, 1)

        def prepare(a):
            x_turn(a)
            proj_qk(a, 0)
            proj_qk(a, 1)

        def step(h, b, a, before):
            if b is not None:
                scores(b, h)
                if h % 2 == 0:
                    up(b, h // 2)
            if h % 2 == 1:
                late = lagging(h, 3, b, before)
                if late:
                    down(late[0], late[1] // 2)
            late = lagging(h, 2, b, before)
            if late:
                e_turn(*late)
            if before is not None and h == 1:
                rden_turn(before, b)
            for late in values_at(h, b, before):
                pv(*late)
            if b is not None and h == 2:
                proj_v(b)
            if before is not None and h == 5:
                out_proj(before, b)
            if a is not None and h == 7:
                x_turn(a)
            if a is not None and h in (8, 10):
                proj_qk(a, (8, 10).index(h))

        drive(pe, prepare, step)

    @block.scalar
    def _(act):
        def x_hi(a):
            act.wait_ge(xT_ok, a.n + 1)
            act.activation(xhi[:, a.par].rearrange("p c s -> p (c s)"), psM[:], ACT.Copy).then_inc(xhi_ok, 1)

        def qk_hi(a, i):
            act.wait_ge(proj_ok[i], a.n + 1)
            prev = a.back(1)
            wait(act, stored[i][prev.par], 16 * prev.uses)
            act.activation(chi[i].rearrange("p c s -> p (c s)"), psM[:], ACT.Copy, scale=0.25 if i == 0 else 1.0).then_inc(phi_ok[i], 1)

        def v_dst(buf, i):
            return buf[:, i].rearrange("p g (h c) -> p g h c", c=144)[:, :, :, 0:16]

        def v_hi(a):
            act.wait_ge(proj_ok[2], a.n + 1)
            if a.off == 0:
                act.wait_ge(zeroed, 1)
            wait(act, pv_ok, 16 * a.n)
            for i in range(2):
                m = act.activation(v_dst(vhi, i), psM[:, i * D:(i + 1) * D].rearrange("p (g h d) -> p g h d", g=2, d=16), ACT.Copy)
            m.then_inc(phi_ok[2], 1)

        def exp(b, h):
            act.wait_ge(max_ok, 16 * b.n + h + 1)
            wait(act, eT_ok, 16 * b.n + h - 3)
            act.activation(e[:, h % 4, 0:P], psS[h % 2][:, 0:P], ACT.Exp, bias=negmax[:, h, 0:1], accum_out=den[:, b.par, 0, h:h + 1])
            act.activation(e[:, h % 4, P:384], psS[h % 2][:, P:384], ACT.Exp, bias=negmax[:, h, 1:2],
                           accum_out=den[:, b.par, 1, h:h + 1]).then_inc(exp_ok, 1)

        def eT_hi(b, h):
            act.wait_ge(eT_ok, 16 * b.n + h + 1)
            wait(act, pv_ok, 16 * b.n + h - 3)
            act.activation(eThi[:, h % 4], psT[h % 2][:, 0:384], ACT.Copy).then_inc(eThi_ok, 1)

        def gate_tanh(b, j):
            act.wait_ge(up_ok, 8 * b.n + j + 1)
            wait(act, gate_ok, 8 * b.n + j)
            act.activation(th[:], psG[:, 0:S], ACT.Tanh, scale=0.5).then_inc(tanh_ok, 1)

        def hid_hi(b, j):
            act.wait_ge(hid_ok, 8 * b.n + j + 1)
            wait(act, down_ok, 8 * b.n + j - 1)
            act.activation(hhi[:, j % 2], hid[:], ACT.Copy).then_inc(hhi_ok, 1)

        def prepare(a):
            x_hi(a)
            qk_hi(a, 0)
            qk_hi(a, 1)

        def finish(b, part):
            if part == 0:
                act.wait_ge(down_ok, 8 * b.n + 8)
                wait(act, sg_ok, b.n)
                act.activation(gf[:], psF[:], ACT.Tanh, scale=0.5).then_inc(tanhf_ok, 1)
            elif part == 1:
                act.wait_ge(rT_ok, b.n + 1)
                wait(act, ctxn_ok, b.n)
                act.activation(rT[:], psM[:], ACT.Copy).then_inc(rTc_ok, 1)
            else:
                act.wait_ge(ctxn_ok, b.n + 1)
                wait(act, so_ok, b.n)
                act.activation(cxhi[:].rearrange("p g s -> p (g s)"), ctxn[:], ACT.Copy).then_inc(cxhi_ok, 1)

        def step(h, b, a, before):
            if b is not None:
                exp(b, h)
                if a is not None and h == 8:
                    x_hi(a)
                if a is not None and h in (9, 11):
                    qk_hi(a, (9, 11).index(h))
                if h % 2 == 0:
                    gate_tanh(b, h // 2)
                else:
                    hid_hi(b, h // 2)
            if before is not None and h == 2:
                finish(before, 0)
            late = lagging(h, 2, b, before)
            if late:
                eT_hi(*late)
            if before is not None and h == 1:
                finish(before, 1)
            if b is not None and h == 3:
                v_hi(b)
            if before is not None and h == 4:
                finish(before, 2)

        drive(act, prepare, step)

    @block.vector
    def _(dve):
        def x_stats(a):
            for i in range(2):
                m = dve.bn_stats(stats[:, i], of_batch(x2, a)[:, D * i:D * (i + 1)])
            m.then_inc(stats_ok, 1)
            dve.wait_ge(stats_ok, a.n + 1)
            dve.sem_inc(wait_done, 1)
            for i in range(2):
                m = dve.bn_aggr(mv[:, i], stats[:, i])
            m.then_inc(aggr_ok, 1)
            dve.wait_ge(aggr_ok, a.n + 1)
            dve.tensor_scalar(veps[:], mv[:, :, 1], EPS, None, ALU.add).then_inc(veps_ok, 1)

        def x_norm(a):
            dve.wait_ge(rstd_ok, a.n + 1)
            wait(dve, xT_ok, a.n)
            for i in range(2):
                dve.tensor_scalar(xn[:, i], of_batch(x2, a)[:, D * i:D * (i + 1)], mv[:, i, 0:1], rstd[:, i:i + 1], ALU.subtract, ALU.mult).then_inc(xn_ok, 1)

        def x_lo(a):
            dve.wait_ge(xhi_ok, a.n + 1)
            dve.tensor_tensor(xlo[:, a.par].rearrange("p c s -> p (c s)"), psM[:], xhi[:, a.par].bitcast(F32).rearrange("p c s -> p (c s)"),
                              ALU.subtract).then_inc(xlo_ok, 1)

        def qk_lo(a, i):
            dve.wait_ge(phi_ok[i], a.n + 1)
            flat = lambda z: z.rearrange("p c s -> p (c s)")
            if i == 0:
                dve.scalar_tensor_tensor(flat(clo[0]), psM[:], 0.25, flat(chi[0].bitcast(F32)), ALU.mult, ALU.subtract).then_inc(plo_ok[0], 1)
            else:
                dve.tensor_tensor(flat(clo[1]), psM[:], flat(chi[1].bitcast(F32)), ALU.subtract).then_inc(plo_ok[1], 1)

        def v_dst(buf, i):
            return buf.rearrange("p g (h c) -> p g h c", c=144)[:, :, :, 0:16]

        def v_lo(a):
            dve.wait_ge(phi_ok[2], a.n + 1)
            if a.off == 0:
                dve.wait_ge(zeroed, 2)
            for i in range(2):
                m = dve.tensor_tensor(v_dst(vlo[:, i], i), psM[:, i * D:(i + 1) * D].rearrange("p (g h d) -> p g h d", g=2, d=16),
                                      v_dst(vhi[:, i].bitcast(F32), i), ALU.subtract)
            m.then_inc(plo_ok[2], 1)

        def row_max(b, h):
            dve.wait_ge(scores_ok, 16 * b.n + h + 1)
            dve.tensor_reduce(negmax[:, h, 0:1], psS[h % 2][:, 0:P], AX.X, ALU.max, negate=True)
            dve.tensor_reduce(negmax[:, h, 1:2], psS[h % 2][:, P:384], AX.X, ALU.max, negate=True).then_inc(max_ok, 1)

        def eT_lo(b, h):
            dve.wait_ge(eThi_ok, 16 * b.n + h + 1)
            dve.tensor_tensor(eTlo[:, h % 4], psT[h % 2][:, 0:384], eThi[:, h % 4].bitcast(F32), ALU.subtract).then_inc(eTlo_ok, 1)

        def gate(b, j):
            dve.wait_ge(tanh_ok, 8 * b.n + j + 1)
            dve.scalar_tensor_tensor(ga[:], th[:], 1.0, psG[:, 0:S], ALU.add, ALU.mult).then_inc(gate_ok, 1)
            dve.wait_ge(gate_ok, 8 * b.n + j + 1)
            wait(dve, hlo_ok, 8 * b.n + j)
            dve.scalar_tensor_tensor(hid[:], ga[:], 0.5, psG[:, S:2 * S], ALU.mult, ALU.mult).then_inc(hid_ok, 1)

        def prepare(a):
            x_stats(a)
            x_norm(a)
            x_lo(a)
            qk_lo(a, 0)
            qk_lo(a, 1)

        def finish(b, part):
            if part == 0:
                dve.wait_ge(exp_ok, 16 * b.n + 16)
                dve.reciprocal(rden[:], den[:, b.par]).then_inc(rden_ok, 1)
                dve.wait_ge(rden_ok, b.n + 1)
                wait(dve, rT_ok, b.n)
                dve.tensor_copy(rden_b[:], rden[:].unsqueeze(3).to_broadcast([P, 2, NH, 16])).then_inc(rdenb_ok, 1)
            elif part == 1:
                dve.wait_ge(tanhf_ok, b.n + 1)
                dve.scalar_tensor_tensor(gf[:], gf[:], 1.0, psF[:], ALU.add, ALU.mult).then_inc(gf_ok, 1)
            elif part == 2:
                dve.wait_ge(rTc_ok, b.n + 1)
                dve.wait_ge(pv_ok, 16 * b.n + 16)
                dve.tensor_tensor(ctxn[:], psC[:], rT[:], ALU.mult).then_inc(ctxn_ok, 1)
            elif part == 3:
                dve.wait_ge(cxhi_ok, b.n + 1)
                dve.tensor_tensor(cxlo[:].rearrange("p g s -> p (g s)"), ctxn[:], cxhi[:].bitcast(F32).rearrange("p g s -> p (g s)"),
                                  ALU.subtract).then_inc(cxlo_ok, 1)
            else:
                dve.wait_ge(so_ok, b.n + 1)
                wait(dve, x2_ok, b.n)
                dve.scalar_tensor_tensor(sg[:], gf[:], 0.5, psM[:], ALU.mult, ALU.mult).then_inc(sg_ok, 1)

        def next_stats(b):
            dve.wait_ge(x2_ok, b.n + 1)
            dve.sem_inc(wait_done, 1)
            dst = t["stats1"][:].rearrange("p (b t) s -> p b (t s)", t=2)
            dst = dst[:, b.n] if isinstance(b.n, int) else dst[:, bass.ds(b.n, 1)].rearrange("p o s -> p (o s)")
            for i in range(2):
                m = dve.bn_stats(dst[:, 6 * i:6 * i + 6], of_batch(x2, b)[:, D * i:D * (i + 1)])

        def step(h, b, a, before):
            late = lagging(h, 3, b, before)
            if b is not None:
                row_max(b, h)
            if late:
                eT_lo(*late)
            if b is not None:
                if a is not None:
                    if h == 1:
                        x_stats(a)
                    if h == 5:
                        x_norm(a)
                    if h == 8:
                        x_lo(a)
                    if h in (9, 11):
                        qk_lo(a, (9, 11).index(h))
                if h % 2 == 0:
                    gate(b, h // 2)
            if before is not None and h == 0:
                finish(before, 0)
            if before is not None and h == 2:
                finish(before, 1)
            if before is not None and h == 3:
                finish(before, 2)
            if b is not None and h == 3:
                v_lo(b)
            if before is not None and h == 4:
                finish(before, 3)
            if before is not None and h == 6:
                finish(before, 4)
            if b is not None and before is not None and h == 9:
                next_stats(before)

        drive(dve, prepare, step)

    @block.gpsimd
    def _(pool):
        def deviation(a):
            pool.wait_ge(veps_ok, a.n + 1)
            pool.tensor_tensor(rstd[:], veps[:], t["neg_half"][:, 0:2], ALU.pow).then_inc(rstd_ok, 1)

        def hid_lo(b, j):
            pool.wait_ge(hhi_ok, 8 * b.n + j + 1)
            pool.tensor_tensor(hlo[:, j % 2], hid[:], hhi[:, j % 2].bitcast(F32), ALU.subtract).then_inc(hlo_ok, 1)

        def residual(b):
            pool.wait_ge(sg_ok, b.n + 1)
            pool.tensor_tensor(of_batch(x2, b), sg[:], of_batch(x2, b), ALU.add).then_inc(x2_ok, 1)

        def step(h, b, a, before):
            if b is not None and h % 2 == 1:
                hid_lo(b, h // 2)
            if a is not None and h == 2:
                deviation(a)
            if before is not None and h == 7:
                residual(before)

        def prepare(a):
            deviation(a)
            pool.memset(vhi[:].bitcast(F32), 0.0).then_inc(zeroed, 1)
            pool.memset(vlo[:].bitcast(F32), 0.0).then_inc(zeroed, 1)

        drive(pool, prepare, step)


def prepare_weights(nc, ctx, t, w, x2, args):
    def sb(name, shape, dt=F32):
        return ctx.enter_context(nc.sbuf_tensor(name, shape, dt))

    def sem(name):
        return ctx.enter_context(nc.semaphore(name))

    raw = sb("raw_qkvo", [P, 4, 2, 256])
    raw_up = sb("raw_up", [P, 2, 2, 1024])
    raw_dn = sb("raw_dn", [P, 8, 256])
    fold = [sb("fold0", [P, 8, 256]), sb("fold1", [P, 8, 256])]
    had = sb("had", [P, P])
    mask = sb("mask", [P, P])
    psW = [ctx.enter_context(nc.psum_tensor(f"psW{i}", [P, 512], F32)) for i in range(4)]
    const_in, dn_in, qkvo_in, up_in, x_in = sem("const_in"), sem("dn_in"), sem("qkvo_in"), sem("up_in"), sem("x_in")
    folded, rotated, dnhi_ok, split_a = (sem(n) for n in ("folded", "rotated", "dnhi_ok", "split_a"))
    block = ctx.enter_context(nc.Block())
    flat4 = lambda z: z.rearrange("p a b c -> p (a b c)")

    @block.sync
    def _(sp):
        sp.dma_start(raw_dn[:], args["W2T"].rearrange("(c p) d -> p c d", p=P)).then_inc(dn_in, 16)
        sp.dma_start(had[:], args["hadamard"]).then_inc(const_in, 16)
        sp.dma_start(t["ident"][:], args["ident"]).then_inc(const_in, 16)
        sp.dma_start(mask[:], args["mask"]).then_inc(const_in, 16)
        sp.dma_start(raw[:], args["qkvoT"].rearrange("a (c p) n -> p a c n", p=P)).then_inc(qkvo_in, 16)
        sp.dma_start(raw_up[:], args["upT"].rearrange("a (c p) n -> p a c n", p=P)).then_inc(up_in, 16)
        sp.dma_start(x2[:], args["x"].rearrange("(i p) d -> p i d", p=P)).then_inc(x_in, 16)
        sp.wait_ge(x_in, 16)

    @block.vector
    def _(dve):
        dve.wait_ge(dn_in, 16)
        src = raw_dn
        for n, half in enumerate((1, 2, 4)):
            dst = fold[n % 2]
            s = src[:].rearrange("p (a two b) d -> p a two (b d)", two=2, b=half)
            d = dst[:].rearrange("p (a two b) d -> p a two (b d)", two=2, b=half)
            if n:
                dve.wait_ge(folded, 2 * n)
            dve.tensor_tensor(d[:, :, 0], s[:, :, 0], s[:, :, 1], ALU.add).then_inc(folded, 1)
            dve.tensor_tensor(d[:, :, 1], s[:, :, 0], s[:, :, 1], ALU.subtract).then_inc(folded, 1)
            src = dst
        dve.wait_ge(split_a, 4)
        dve.tensor_tensor(w["up_lo"][:, 0].rearrange("p c n -> p (c n)"), raw_up[:, 0].rearrange("p c n -> p (c n)"),
                          w["up_hi"][:, 0].bitcast(F32).rearrange("p c n -> p (c n)"), ALU.subtract)
        for i in range(4):
            dve.wait_ge(dnhi_ok, i + 1)
            dve.scalar_tensor_tensor(w["dn_lo"][:, 2 * i:2 * i + 2].rearrange("p c d -> p (c d)"), psW[i][:], 1.0 / 32.0,
                                     w["dn_hi"][:, 2 * i:2 * i + 2].bitcast(F32).rearrange("p c d -> p (c d)"), ALU.mult, ALU.subtract)

    @block.tensor
    def _(pe):
        pe.wait_ge(folded, 6)
        pe.wait_ge(const_in, 48)
        for i in range(4):
            src = fold[0][:, 2 * i:2 * i + 2].rearrange("p c d -> p (c d)")
            pe.matmul(psW[i][:], had[:], src, start=True, stop=True).then_inc(rotated, 1)

    @block.scalar
    def _(act):
        act.wait_ge(const_in, 48)
        act.activation(t["ident_r"][:], t["ident"][:], ACT.Copy).then_inc(split_a, 1)
        act.activation(t["mask_r"][:], mask[:], ACT.Copy).then_inc(split_a, 1)
        act.wait_ge(qkvo_in, 16)
        act.activation(flat4(w["hi"][:]), flat4(raw[:]), ACT.Copy).then_inc(split_a, 1)
        act.wait_ge(up_in, 16)
        act.activation(flat4(w["up_hi"][:]), flat4(raw_up[:]), ACT.Copy).then_inc(split_a, 1)
        for i in range(4):
            act.wait_ge(rotated, i + 1)
            act.activation(w["dn_hi"][:, 2 * i:2 * i + 2].rearrange("p c d -> p (c d)"), psW[i][:], ACT.Copy, scale=1.0 / 32.0).then_inc(dnhi_ok, 1)

    @block.gpsimd
    def _(pool):
        pool.memset(t["neg_half"][:], -0.5)
        pool.wait_ge(split_a, 3)
        pool.tensor_tensor(flat4(w["lo"][:]), flat4(raw[:]), flat4(w["hi"][:].bitcast(F32)), ALU.subtract)
        pool.wait_ge(split_a, 4)
        pool.tensor_tensor(w["up_lo"][:, 1].rearrange("p c n -> p (c n)"), raw_up[:, 1].rearrange("p c n -> p (c n)"),
                           w["up_hi"][:, 1].bitcast(F32).rearrange("p c n -> p (c n)"), ALU.subtract)


def split3(mm, out, a_hi, a_lo, b_hi, b_lo, start, stop, skip=False):
    mm(out, a_hi, b_hi, start=start, stop=False, skip_group_check=skip)
    mm(out, a_hi, b_lo, start=False, stop=False, skip_group_check=skip)
    return mm(out, a_lo, b_hi, start=False, stop=stop, skip_group_check=skip)


LEAD = 3
SHARED_BEFORE_RANKS = 2


def normalise_and_route(nc, ctx, t, x2, xhi, xlo, routed, args):
    NT, NE = 16, 32

    def sb(name, shape, dt=F32):
        return ctx.enter_context(nc.sbuf_tensor(name, shape, dt))

    def sem(name):
        return ctx.enter_context(nc.semaphore(name))

    stats = t["stats1"]
    mv = sb("mv1", [P, NT, 2])
    veps = sb("veps1", [P, NT])
    rstd = sb("rstd1", [P, NT])
    xn = f = x2
    rw = sb("rw", [P, 2, NE])
    rw_hi = sb("rw_hi", [P, 2, NE], F32R)
    rw_lo = sb("rw_lo", [P, 2, NE], F32R)
    bias = sb("bias", [P, NE])
    tri = sb("tri", [P, 64])
    score = sb("score", [P, NT, NE])
    biased = routed["key"]
    pmax = sb("pmax", [P, NT * 8, 2])
    pmin = sb("pmin", [P, NT * 8, 2])
    top = sb("top", [P, NT * 8])
    low = sb("low", [P, NT * 8])
    other = sb("other", [P, NT * 8])
    second = sb("second", [P, NT * 8])
    group = sb("group", [P, NT, 8])
    above = sb("above", [P, NT, 8, 8])
    equal = sb("equal", [P, NT, 8, 8])
    rank = sb("rank", [P, NT, 8])
    keep = sb("keep", [P, NT, 8])
    masked = biased
    best = sb("best", [P, NT, 8])
    rest = sb("rest", [P, NT, NE])
    chosen = routed["chosen"]
    total = sb("total", [P, NT])
    rtotal = sb("rtotal", [P, NT])
    psX = [ctx.enter_context(nc.psum_tensor(f"psX{i}", [P, 512], F32)) for i in range(4)]
    psL = [ctx.enter_context(nc.psum_tensor(f"psL{i}", [P, 512], F32)) for i in range(2)]
    psR = ctx.enter_context(nc.psum_tensor("psR", [P, NT, NE], F32))
    psN = ctx.enter_context(nc.psum_tensor("psN", [P, 512], F32))
    work = sb("shared_work", [P, 3, 512])
    sw_raw = work[:].rearrange("p (a b) d -> p (a b d)", a=1).rearrange("p (e n) -> p e n", e=2)
    sw_hi = sb("shared_hi", [P, 2, 768], F32R)
    sw_lo = sb("shared_lo", [P, 2, 768], F32R)
    sil, up, hid = work[:, 0], work[:, 1], work[:, 2]
    hhi = sb("hid1_hi", [P, 2, 512], F32R)
    hlo = sb("hid1_lo", [P, 2, 512], F32R)
    flat64 = lambda z: z.rearrange("p t g h -> p (t g h)")
    scoreT = flat64(above[:])[0:NE].rearrange("e (a s) -> e a s", a=2)
    psG, psU, psD = psX[2], psX[3], psL
    shared_steps = [(g, e) for g in range(4) for e in range(2)]
    firsts = sb("firsts", [P, NT])
    part = sb("part", [P, 2])
    tokens = sb("tokens", [P, NT])
    before = flat64(equal[:])[:, 0:P]
    before_h = sb("before_h", [P, P], F16)
    ones_h = sb("ones_h", [P, P], F16)
    mask_h = sb("mask_h", [P, NT, NE], F16)
    count = sb("count", [P, NE])
    blocks = sb("blocks", [P, NE])
    start = sb("start", [P, NE])
    passed = sb("passed", [P, 2, NE])
    owner = sb("owner", [P, 2])
    key = routed["key"]
    best_key = routed["best_key"]
    slot = sb("slot", [P, NT * 8])
    slot_lo_i = sb("slot_lo_i", [P, NT * 8], I32)
    slot_hi_i = sb("slot_hi_i", [P, NT * 8], I32)
    slot_lo = sb("slot_lo", [P, NT, 8], F16)
    slot_hi = sb("slot_hi", [P, NT, 8], F16)
    at_lo = flat64(above[:]).bitcast(F16).rearrange("p (a s k) -> p a s k", a=4, k=4)
    at_hi = sb("at_hi", [P, 4, NBLK, 4], F16)
    iota_h = flat64(equal[:]).bitcast(F16)[:, 0:4 * NBLK].rearrange("p (s k) -> p s k", k=4)
    in_at_hi = at_hi[:].rearrange("p a s k -> p (a s k)").bitcast(F32)
    tri32 = in_at_hi[:, 0:NE * NE]
    iota = in_at_hi[:, NE * NE:NE * NE + 256]

    const_in, expert_in, sraw_in, xn_stored = (sem(n) for n in ("const1_in", "expert_in", "shared_in", "xn_stored"))
    stats_ok, veps_ok, rstd_ok, xn_ok, xT_ok, xhi_ok, xlo_ok, prep_ok, logits_ok, scoreT_ok, score_ok = (
        sem(n) for n in ("stats1_ok", "veps1_ok", "rstd1_ok", "xn1_ok", "xT1_ok", "xhi1_ok", "xlo1_ok", "prep_ok", "logits_ok",
                         "scoreT_ok", "score_ok"))
    chain, mask_ok, ranked, owner_ok, owner_turned, hot_ok, token_ok, hot_used = (
        sem(n) for n in ("route_step", "mask_ok", "ranked", "owner_ok", "owner_turned", "hot_ok", "token_ok", "hot_used"))
    swhi_ok, swlo_ok, g_ok, u_ok, sil_ok, up_ok, hid_ok, hhi_ok, hlo_ok, d_ok, f_ok = (
        sem(n) for n in ("swhi_ok", "swlo_ok", "sg_ok", "su_ok", "ssil_ok", "sup_ok", "shid_ok", "shhi_ok", "shlo_ok", "sd_ok", "sf_ok"))
    block = ctx.enter_context(nc.Block())
    pair = lambda z, k: z[:, :, 256 * k:256 * (k + 1)]

    @block.sync
    def _(sp):
        sp.dma_start(rw[:], args["router_w"].rearrange("(c p) e -> p c e", p=P)).then_inc(const_in, 16)
        sp.dma_start(bias[:], args["router_bias"].broadcast_to([P, NE])).then_inc(const_in, 16)
        sp.dma_start(tri[:], args["earlier"].broadcast_to([P, 64])).then_inc(const_in, 16)
        sp.dma_start(tri32, args["earlier32"].broadcast_to([P, NE * NE])).then_inc(const_in, 16)
        sp.dma_start(iota, args["iota"].broadcast_to([P, 256])).then_inc(const_in, 16)
        sp.dma_start(firsts[:], args["firsts"].broadcast_to([P, NT])).then_inc(const_in, 16)
        sp.dma_start(part[:], args["part"]).then_inc(const_in, 16)
        sp.dma_start(tokens[:], args["tokens"]).then_inc(const_in, 16)
        sp.dma_start(before, args["before"]).then_inc(const_in, 16)
        sp.dma_start(sw_raw, args["experts"][32:34].rearrange("e p n -> p e n")).then_inc(sraw_in, 16)
        for q in range(4):
            sp.dma_start(routed["w"][:, 8 * q:8 * q + 8], args["experts"][8 * q:8 * q + 8].rearrange("e p n -> p e n")).then_inc(expert_in, 16)
        sp.wait_ge(xn_stored, 16)
        sp.wait_ge(expert_in, 64)

    @block.gpsimd
    def _(pool):
        pool.wait_ge(veps_ok, 1)
        pool.tensor_tensor(rstd[:], veps[:], t["neg_half"][:], ALU.pow).then_inc(rstd_ok, 1)
        pool.wait_ge(const_in, 144)
        pool.tensor_copy(rw_hi[:], rw[:]).then_inc(prep_ok, 1)
        pool.wait_ge(prep_ok, 1)
        pool.tensor_tensor(rw_lo[:], rw[:], rw_hi[:].bitcast(F32), ALU.subtract).then_inc(prep_ok, 1)
        pool.memset(ones_h[:], 1.0).then_inc(prep_ok, 1)
        pool.tensor_copy(before_h[:], before).then_inc(prep_ok, 1)
        pool.wait_ge(swhi_ok, 1)
        pool.tensor_tensor(sw_lo[:], sw_raw, sw_hi[:].bitcast(F32), ALU.subtract).then_inc(swlo_ok, 1)
        for n in range(len(shared_steps)):
            pool.wait_ge(sil_ok, n + 1)
            pool.wait_ge(up_ok, n + 1)
            wait(pool, hlo_ok, n)
            pool.tensor_tensor(hid, up, sil, ALU.mult).then_inc(hid_ok, 1)
            pool.wait_ge(hhi_ok, n + 1)
            pool.tensor_tensor(hlo[:, n % 2], hid, hhi[:, n % 2].bitcast(F32), ALU.subtract).then_inc(hlo_ok, 1)
    @block.tensor
    def _(pe):
        def logits(g):
            wait(pe, scoreT_ok, g - 1)
            pe.wait_ge(xlo_ok, 2 * g + 2)
            for c in range(2):
                tok = (slice(None), c, slice(512 * g, 512 * g + 512))
                m = split3(pe.matmul, psL[g % 2][0:NE], rw_hi[:, c], rw_lo[:, c], xhi[tok], xlo[tok], c == 0, c == 1)
            m.then_inc(logits_ok, 1)

        def turn_scores(g):
            pe.wait_ge(scoreT_ok, g + 1)
            for i in range(4):
                m = pe.transpose(psR[:, 4 * g + i], scoreT[:, g % 2, i * P:(i + 1) * P], t["ident"][0:NE, 0:NE])
            m.then_inc(score_ok, 1)

        for k in range(NT // 2):
            pe.wait_ge(xn_ok, 2 * k + 2)
            wait(pe, xlo_ok, k - 3)
            for c in range(2):
                for i in range(2):
                    m = pe.transpose(psX[k % 4][:, c * 256 + i * P:c * 256 + (i + 1) * P], xn[:, 2 * k + i, c * P:(c + 1) * P], t["ident"][:])
            m.then_inc(xT_ok, 1)
            if k == 1:
                pe.wait_ge(prep_ok, 2)
            if k % 2 == 1 and k >= 3:
                logits(k // 2 - 1)
            if k == 6:
                turn_scores(0)
        turn_scores(1)
        logits(3)
        turn_scores(2)
        turn_scores(3)

        def shared_proj(n, j, out, done):
            g, e = shared_steps[n]
            for c in range(2):
                wc = (slice(None), e, slice(256 * c + P * j, 256 * c + P * (j + 1)))
                tok = (slice(None), c, slice(512 * g, 512 * g + 512))
                last = split3(pe.matmul, out[:], sw_hi[wc], sw_lo[wc], xhi[tok], xlo[tok], c == 0, c == 1)
            last.then_inc(done, 1)

        def shared_gate(n):
            wait(pe, sil_ok, n)
            shared_proj(n, 0, psG, g_ok)

        def shared_up(n):
            wait(pe, up_ok, n)
            shared_proj(n, 1, psU, u_ok)

        def shared_down(n):
            g, e = shared_steps[n]
            pe.wait_ge(hlo_ok, n + 1)
            wait(pe, f_ok, g)
            wd = (slice(None), e, slice(512, 768))
            for i in range(4):
                tok = (slice(None), n % 2, slice(P * i, P * i + P))
                out = psD[i // 2][:, 256 * (i % 2):256 * (i % 2) + 256]
                last = split3(pe.matmul, out, hhi[tok], hlo[tok], sw_hi[wd], sw_lo[wd], e == 0 and i % 2 == 0, e == 1, True)
            last.then_inc(d_ok, 1)

        def shared(first, last):
            for n in range(first, last):
                shared_gate(n)
                shared_up(n)
                if n > 0:
                    shared_down(n - 1)

        pe.wait_ge(swlo_ok, 1)
        pe.wait_ge(xlo_ok, NT // 2)
        shared(0, SHARED_BEFORE_RANKS)
        pe.wait_ge(prep_ok, 4)
        pe.wait_ge(mask_ok, 1)
        pe.matmul(psR[:].rearrange("p t e -> p (t e)"), before_h[:], mask_h[:].rearrange("p t e -> p (t e)"), start=True, stop=False, skip_group_check=True)
        for i in range(NT - 1):
            later = mask_h[:, i:i + 1].to_broadcast([P, NT - 1 - i, NE])
            m = pe.matmul(psR[:, i + 1:], ones_h[:], later, start=False, stop=i == NT - 2, skip_group_check=True)
        for i in range(NT):
            m = pe.matmul(psN[:, 0:NE], ones_h[:], mask_h[:, i], start=i == 0, stop=i == NT - 1)
        m.then_inc(ranked, 1)
        shared(SHARED_BEFORE_RANKS, 5)
        pe.wait_ge(owner_ok, 1)
        for c in range(2):
            m = pe.transpose(psX[0][0:1, c * P:(c + 1) * P], owner[:, c:c + 1], t["ident"][:])
        m.then_inc(owner_turned, 1)
        for u in range(2 * NT):
            pe.wait_ge(hot_ok, 2 * u + 2)
            pe.wait_ge(token_ok, u + 1)
            for k in range(4):
                m = pe.matmul(psX[1][:, 0:NBLK], at_lo[:, u % 4, :, k], at_hi[:, u % 4, :, k], start=u == 0 and k == 0, stop=u == 2 * NT - 1 and k == 3)
            m.then_inc(hot_used, 1)
            i = u // 2 if u % 2 else -1
            if i in (0, 3, 6):
                shared_gate(5 + i // 3)
            if i in (1, 4, 7):
                shared_up(5 + i // 3)
            if i in (2, 5, 8):
                shared_down(4 + i // 3)
            if i == 10:
                shared_down(7)

    @block.scalar
    def _(act):
        def scores(g):
            act.wait_ge(logits_ok, g + 1)
            wait(act, score_ok, g - 1)
            act.activation(scoreT[:, g % 2], psL[g % 2][0:NE], ACT.Sigmoid).then_inc(scoreT_ok, 1)

        def set_tokens(u):
            act.wait_ge(hot_ok, 2 * u + 1)
            act.activation(at_lo[:, u % 4], at_lo[:, u % 4], ACT.Copy, scale=tokens[:, u // 2:u // 2 + 1]).then_inc(token_ok, 1)

        def collect(g):
            act.wait_ge(d_ok, 2 * g + 2)
            if g == 0:
                act.wait_ge(xn_stored, 16)
            for i in range(2):
                m = act.activation(f[:, 4 * g + 2 * i:4 * g + 2 * i + 2].rearrange("p t d -> p (t d)"), psD[i][:], ACT.Copy)
            m.then_inc(f_ok, 1)

        for k in range(NT // 2):
            act.wait_ge(xT_ok, k + 1)
            act.activation(pair(xhi, k), psX[k % 4][:].rearrange("p (c s) -> p c s", c=2), ACT.Copy).then_inc(xhi_ok, 1)
            if k == 0:
                act.wait_ge(sraw_in, 16)
                act.activation(sw_hi[:], sw_raw, ACT.Copy).then_inc(swhi_ok, 1)
            if k % 2 == 1 and k >= 5:
                scores(k // 2 - 2)
        scores(2)
        act.wait_ge(xn_ok, NT)
        act.dma_start(routed["xn_dram"].rearrange("(i p) d -> p i d", p=P), xn[:]).then_inc(xn_stored, 16)
        scores(3)
        def shared_silu(n):
            act.wait_ge(g_ok, n + 1)
            wait(act, hid_ok, n)
            act.activation(sil, psG[:], ACT.Silu).then_inc(sil_ok, 1)

        def shared_copy(n):
            act.wait_ge(u_ok, n + 1)
            act.activation(up, psU[:], ACT.Copy).then_inc(up_ok, 1)

        def shared_round(n):
            act.wait_ge(hid_ok, n + 1)
            wait(act, hlo_ok, n)
            wait(act, d_ok, n - 1)
            act.activation(hhi[:, n % 2], hid, ACT.Copy).then_inc(hhi_ok, 1)

        for n in range(5):
            shared_silu(n)
            shared_copy(n)
            if n in (2, 4):
                collect(n // 2 - 1)
            shared_round(n)
        for u in range(LEAD):
            set_tokens(u)
        for u in range(2 * NT):
            if u + LEAD < 2 * NT:
                set_tokens(u + LEAD)
            i = u // 2 if u % 2 else -1
            if i in (0, 3, 6):
                shared_silu(5 + i // 3)
            if i in (1, 4, 7):
                shared_copy(5 + i // 3)
            if i == 5:
                collect(2)
            if i in (2, 5, 8):
                shared_round(5 + i // 3)
            if i == 11:
                collect(3)

    @block.vector
    def _(dve):
        for i in (NT - 2, NT - 1):
            m = dve.bn_stats(stats[:, i], x2[:, i])
        m.then_inc(stats_ok, 1)
        dve.wait_ge(stats_ok, 1)
        for i in range(NT):
            m = dve.bn_aggr(mv[:, i], stats[:, i])
        m.then_inc(stats_ok, 1)
        dve.wait_ge(stats_ok, 2)
        dve.tensor_scalar(veps[:], mv[:, :, 1], EPS, None, ALU.add).then_inc(veps_ok, 1)
        dve.wait_ge(rstd_ok, 1)
        dve.wait_ge(t["x2_stored"], 16 * 8)

        def x_lo(k):
            dve.wait_ge(xhi_ok, k + 1)
            dve.tensor_tensor(pair(xlo, k), psX[k % 4][:].rearrange("p (c s) -> p c s", c=2), pair(xhi, k).bitcast(F32), ALU.subtract).then_inc(xlo_ok, 1)

        for i in range(NT):
            dve.tensor_scalar(xn[:, i], x2[:, i], mv[:, i, 0:1], rstd[:, i:i + 1], ALU.subtract, ALU.mult).then_inc(xn_ok, 1)
            if i % 2 == 1 and i >= 3:
                x_lo((i - 3) // 2)
        x_lo(NT // 2 - 1)
        dve.wait_ge(score_ok, 4)
        dve.wait_ge(const_in, 144)
        steps = 0

        def step(ins):
            nonlocal steps
            steps += 1
            ins.then_inc(chain, 1)
            dve.wait_ge(chain, steps)

        step(dve.tensor_copy(score[:], psR[:]))
        step(dve.tensor_tensor(biased[:], score[:], bias[:].unsqueeze(1).to_broadcast([P, NT, NE]), ALU.add))
        quad = biased[:].rearrange("p t (g b a) -> p (t g) b a", b=2, a=2)
        dve.tensor_tensor(pmax[:], quad[:, :, :, 0], quad[:, :, :, 1], ALU.max)
        step(dve.tensor_tensor(pmin[:], quad[:, :, :, 0], quad[:, :, :, 1], ALU.min))
        dve.tensor_tensor(top[:], pmax[:, :, 0], pmax[:, :, 1], ALU.max)
        dve.tensor_tensor(low[:], pmax[:, :, 0], pmax[:, :, 1], ALU.min)
        step(dve.tensor_tensor(other[:], pmin[:, :, 0], pmin[:, :, 1], ALU.max))
        step(dve.tensor_tensor(second[:], low[:], other[:], ALU.max))
        step(dve.tensor_tensor(group[:].rearrange("p t g -> p (t g)"), top[:], second[:], ALU.add))
        mine = group[:].unsqueeze(3).to_broadcast([P, NT, 8, 8])
        theirs = group[:].unsqueeze(2).to_broadcast([P, NT, 8, 8])
        dve.tensor_tensor(above[:], theirs, mine, ALU.is_gt)
        dve.wait_ge(prep_ok, 4)
        step(dve.tensor_tensor(equal[:], theirs, mine, ALU.is_equal))
        flat = lambda z: z.rearrange("p t g h -> p t (g h)")
        step(dve.tensor_tensor(flat(equal[:]), flat(equal[:]), tri[:].unsqueeze(1).to_broadcast([P, NT, 64]), ALU.mult))
        step(dve.tensor_tensor(flat(above[:]), flat(above[:]), flat(equal[:]), ALU.add))
        step(dve.tensor_reduce(rank[:], above[:], AX.X, ALU.add))
        step(dve.tensor_scalar(keep[:], rank[:], 3.5, None, ALU.is_lt))
        by_group = lambda z: z.rearrange("p t (g a) -> p (t g) a", a=4)
        step(dve.tensor_tensor(by_group(masked[:]), by_group(biased[:]),
                               keep[:].rearrange("p t g -> p (t g)").unsqueeze(2).to_broadcast([P, NT * 8, 4]), ALU.mult))
        step(dve.tensor_scalar(masked[:], masked[:], 0.0, None, ALU.add))
        for i in range(NT):
            m = dve.max(best[:, i], masked[:, i])
        step(m)
        for i in range(NT):
            m = dve.match_replace(rest[:, i], best[:, i], masked[:, i], -3.0e38)
        step(m)
        step(dve.tensor_tensor(rest[:], rest[:], masked[:], ALU.not_equal))
        dve.tensor_copy(mask_h[:], rest[:]).then_inc(mask_ok, 1)
        step(dve.tensor_tensor(chosen[:], rest[:], score[:], ALU.mult))
        step(dve.tensor_reduce(total[:], chosen[:], AX.X, ALU.add))
        step(dve.reciprocal(rtotal[:], total[:]))
        step(dve.scalar_tensor_tensor(chosen[:], chosen[:], 2.5, rtotal[:].unsqueeze(2).to_broadcast([P, NT, NE]), ALU.mult, ALU.mult))
        step(dve.tensor_copy(iota_h, iota[:, 0:NBLK].unsqueeze(2).to_broadcast([P, NBLK, 4])))
        dve.wait_ge(ranked, 1)
        step(dve.tensor_copy(count[:], psN[:, 0:NE]))
        cmp = above[:].rearrange("p t g h -> p (t g h)")
        step(dve.tensor_tensor(cmp[:, 0:NE * NT].rearrange("p (e j) -> p e j", e=NE), count[:].unsqueeze(2).to_broadcast([P, NE, NT]),
                               firsts[:].unsqueeze(1).to_broadcast([P, NE, NT]), ALU.is_gt))
        step(dve.tensor_reduce(blocks[:], cmp[:, 0:NE * NT].rearrange("p (e j) -> p e j", e=NE), AX.X, ALU.add))
        step(dve.tensor_tensor(cmp.rearrange("p (e j) -> p e j", e=NE), tri32.rearrange("p (e j) -> p e j", e=NE),
                               blocks[:].unsqueeze(1).to_broadcast([P, NE, NE]), ALU.mult))
        step(dve.tensor_reduce(start[:], cmp.rearrange("p (e j) -> p e j", e=NE), AX.X, ALU.add))
        for c in range(2):
            m = dve.tensor_scalar(passed[:, c], start[:], part[:, c:c + 1], None, ALU.is_le)
        step(m)
        step(dve.tensor_reduce(owner[:], passed[:], AX.X, ALU.add))
        dve.tensor_scalar(owner[:], owner[:], -1.0, None, ALU.add).then_inc(owner_ok, 1)
        step(dve.scalar_tensor_tensor(key[:], start[:].unsqueeze(1).to_broadcast([P, NT, NE]), 128.0, psR[:], ALU.mult, ALU.add))
        step(dve.tensor_scalar(key[:], key[:], -1.0, TOP, ALU.mult, ALU.add))
        step(dve.tensor_tensor(key[:], key[:], rest[:], ALU.mult))
        for i in range(NT):
            m = dve.max(best_key[:, i], key[:, i])
        step(m)
        step(dve.tensor_scalar(slot[:], best_key[:].rearrange("p t k -> p (t k)"), -1.0, TOP, ALU.mult, ALU.add))
        step(dve.tensor_copy(routed["slots"][:].rearrange("p t k -> p (t k)"), slot[:]))
        flat_slots = routed["slots"][:].rearrange("p t k -> p (t k)")
        dve.tensor_scalar(slot_lo_i[:], flat_slots, P - 1, None, ALU.bitwise_and)
        step(dve.tensor_scalar(slot_hi_i[:], flat_slots, 7, None, ALU.logical_shift_right))
        dve.tensor_copy(slot_lo[:].rearrange("p t k -> p (t k)"), slot_lo_i[:])
        step(dve.tensor_copy(slot_hi[:].rearrange("p t k -> p (t k)"), slot_hi_i[:]))
        for u in range(2 * NT):
            wait(dve, hot_used, u - 3)
            four = slice(4 * (u % 2), 4 * (u % 2) + 4)
            for out, slots, n in ((at_lo, slot_lo, P), (at_hi, slot_hi, NBLK)):
                dve.tensor_tensor(out[:, u % 4], iota_h[:, 0:n], slots[:, u // 2:u // 2 + 1, four].to_broadcast([P, n, 4]), ALU.is_equal).then_inc(hot_ok, 1)
        dve.wait_ge(owner_turned, 1)
        dve.tensor_copy(routed["owner"][0:1], psX[0][0:1, 0:NBLK])
        dve.wait_ge(hot_used, 2 * NT)
        dve.tensor_copy(routed["ids"][:], psX[1][:, 0:NBLK])


class Tile:

    def __init__(self, i, k):
        self.i, self.k = i, k
        self.n = RING * i + k
        self.q = k % RING
        self.uses = i + k // RING + 1
        self.yq = k % 4
        self.y_uses = RING // 4 * i + k // 4 + 1

    def back(self, j):
        return Tile(self.i, self.k - j)


def routed_experts(nc, ctx, t, routed):
    def sb(name, shape, dt=F32):
        return ctx.enter_context(nc.sbuf_tensor(name, shape, dt))

    def sem(name):
        return ctx.enter_context(nc.semaphore("r_" + name))

    w, ids, owner = routed["w"], routed["ids"], routed["owner"]
    idx = sb("idx", [P, RING, 1], I32)
    xg = sb("xg", [P, RING, 256])
    xT = sb("xT", [P, 2, 256])
    sil = sb("sil_r", [P, 2, P])
    hid = sb("hid_r", [P, 2, P])
    wgu = sb("wgu", [P, 2, 512])
    y = sb("y", [P, 4, 256])
    ps = lambda n: ctx.enter_context(nc.psum_tensor(n, [P, 512], F32))
    psX, psG, psD = ([ps(f"ps{c}r{i}") for i in range(2)] for c in "XGD")
    gathered = [sem(f"gathered{i}") for i in range(RING)]
    stored = [sem(f"stored{i}") for i in range(4)]
    match = sb("match", [P, 2, 8, 32])
    matched = sem("matched")
    idx_ok, xT_ok, xTc_ok, wgu_ok, gu_ok, sil_ok, hid_ok, d_ok, y_ok = (
        sem(n) for n in ("idx_ok", "xT_ok", "xTc_ok", "wgu_ok", "gu_ok", "sil_ok", "hid_ok", "d_ok", "y_ok"))
    wait_done = t["wait_done"]
    block = ctx.enter_context(nc.Block())
    exists = lambda n: not isinstance(n, int) or n >= 0

    def drive(eng, step, lag):
        for k in range(RING):
            step(Tile(0, k), True)
        with eng.Fori(1, NBLK // RING) as i:
            for k in range(RING):
                step(Tile(i, k), True)
        for k in range(lag):
            step(Tile(NBLK // RING, k), False)

    def load_owner(eng, regs, s):
        eng.reg_load(regs[s.k % len(regs)], owner[0:1, s.n:s.n + 1] if isinstance(s.n, int) else owner[0:1, bass.ds(s.n, 1)])

    def owner_of(eng, regs, s):
        return eng.snap(regs[s.k % len(regs)], min_val=0, max_val=31)

    @block.gpsimd
    def _(pool):
        def step(s, new):
            wait(pool, xT_ok, s.n - RING + 1)
            pool.sem_inc(wait_done, 1)
            src = ids[:, s.n:s.n + 1] if isinstance(s.n, int) else ids[:, bass.ds(s.n, 1)]
            pool.tensor_copy(idx[:, s.q], src).then_inc(idx_ok, 1)
            pool.wait_ge(idx_ok, s.n + 1)
            pool.sem_inc(wait_done, 1)
            pool.indirect_dma_start(xg[:, s.q], None, routed["xn_dram"], bass.IndirectOffsetOnAxis(ap=idx[:, s.q], axis=0)).then_inc(gathered[s.q], 16)

        drive(pool, step, 0)

    @block.tensor
    def _(pe):
        regs = [pe.alloc_register(f"owner{j}") for j in range(RING)]

        def step(s, new):
            if new:
                pe.wait_ge(gathered[s.q], 16 * s.uses)
                wait(pe, xTc_ok, s.n - 1)
                for c in range(2):
                    m = pe.transpose(psX[s.k % 2][:, c * P:(c + 1) * P], xg[:, s.q, c * P:(c + 1) * P], t["ident"][:])
                m.then_inc(xT_ok, 1)
            if exists(s.n - 1) and (new or s.k < 1):
                b = s.back(1)
                pe.wait_ge(xTc_ok, b.n + 1)
                pe.wait_ge(wgu_ok, b.n + 1)
                wait(pe, hid_ok, b.n - 1)
                for j in range(2):
                    for c in range(2):
                        m = pe.matmul(psG[b.k % 2][:, P * j:P * (j + 1)], wgu[:, b.k % 2, 256 * c + P * j:256 * c + P * (j + 1)],
                                      xT[:, b.k % 2, c * P:(c + 1) * P], start=c == 0, stop=c == 1)
                m.then_inc(gu_ok, 1)
            if new:
                load_owner(pe, regs, s)
            if exists(s.n - 2) and (new or s.k < 2):
                b = s.back(2)
                pe.wait_ge(hid_ok, b.n + 1)
                wait(pe, y_ok, b.n - 1)
                pe.matmul(psD[b.k % 2][:, 0:256], hid[:, b.k % 2], w[:, bass.ds(owner_of(pe, regs, b), 1), 512:768].rearrange("p o n -> p (o n)"),
                          start=True, stop=True).then_inc(d_ok, 1)

        drive(pe, step, 2)

    @block.scalar
    def _(act):
        def step(s, new):
            if new:
                act.wait_ge(xT_ok, s.n + 1)
                wait(act, gu_ok, s.n - 1)
                act.activation(xT[:, s.k % 2], psX[s.k % 2][:, 0:256], ACT.Copy).then_inc(xTc_ok, 1)
            if exists(s.n - 1) and (new or s.k < 1):
                b = s.back(1)
                act.wait_ge(gu_ok, b.n + 1)
                wait(act, hid_ok, b.n - 1)
                act.activation(sil[:, b.k % 2], psG[b.k % 2][:, 0:P], ACT.Silu).then_inc(sil_ok, 1)

        drive(act, step, 1)

    @block.vector
    def _(dve):
        regs = [dve.alloc_register(f"expert{j}") for j in range(2)]

        def slot_weights(k):
            r = slice(2 * k, 2 * k + 2)
            by_slot = lambda z: routed[z][:, r].unsqueeze(2).to_broadcast([P, 2, 8, 32])
            keys = routed["best_key"][:, r].unsqueeze(3).to_broadcast([P, 2, 8, 32])
            wait(dve, matched, 3 * k)
            dve.tensor_tensor(match[:], by_slot("key"), keys, ALU.is_equal).then_inc(matched, 1)
            dve.wait_ge(matched, 3 * k + 1)
            dve.tensor_tensor(match[:], match[:], by_slot("chosen"), ALU.mult).then_inc(matched, 1)
            dve.wait_ge(matched, 3 * k + 2)
            dve.tensor_reduce(routed["weights"][:, r], match[:], AX.X, ALU.add).then_inc(matched, 1)

        def step(s, new):
            if new:
                load_owner(dve, regs, s)
                wait(dve, gu_ok, s.n - 1)
                dve.tensor_copy(wgu[:, s.k % 2], w[:, bass.ds(owner_of(dve, regs, s), 1), 0:512].rearrange("p o n -> p (o n)")).then_inc(wgu_ok, 1)
            if exists(s.n - 1) and (new or s.k < 1):
                b = s.back(1)
                dve.wait_ge(sil_ok, b.n + 1)
                wait(dve, d_ok, b.n - 1)
                dve.tensor_tensor(hid[:, b.k % 2], psG[b.k % 2][:, P:2 * P], sil[:, b.k % 2], ALU.mult).then_inc(hid_ok, 1)
            if isinstance(s.i, int) and s.i == 0:
                slot_weights(s.k)
            if exists(s.n - 2):
                b = s.back(2)
                dve.wait_ge(d_ok, b.n + 1)
                wait(dve, stored[b.yq], 16 * (b.y_uses - 1))
                dve.tensor_copy(y[:, b.yq], psD[b.k % 2][:, 0:256]).then_inc(y_ok, 1)

        drive(dve, step, 2)

    @block.sync
    def _(sp):
        out = routed["y_dram"].rearrange("(n p) d -> n p d", p=P)

        def step(s, new):
            sp.wait_ge(y_ok, s.n + 1)
            sp.dma_start(out[s.n], y[:, s.yq]).then_inc(stored[s.yq], 16)

        drive(sp, step, 0)
        for q in range(4):
            sp.wait_ge(stored[q], 16 * (NBLK // 4))


POOL_SUMS = 4


class Step:

    def __init__(self, i, k):
        self.i, self.k = i, k
        self.n = 8 * i + k
        self.g = k % 4
        self.par = (k // 4) % 2
        self.head = 2 * i + k // 4

    def back(self, j):
        return Step(self.i, self.k - j)


def attention1(nc, ctx, t, xhi, xlo, s1, f, x2, x2_dram, routed, args, out):
    NH, NP = 16, 8
    SCALE = 128.0 ** -0.5

    def sb(name, shape, dt=F32):
        return ctx.enter_context(nc.sbuf_tensor(name, shape, dt))

    def sem(name):
        return ctx.enter_context(nc.semaphore(name))

    raw = sb("raw_head", [P, 2, 1024])
    whi = sb("head_hi", [P, 2, 1024], F32R)
    wlo = sb("head_lo", [P, 2, 1024], F32R)
    ohi = [sb("q1_hi", [P, 512], F32R), sb("k1_hi", [P, 512], F32R)]
    olo = [sb("q1_lo", [P, 512], F32R), sb("k1_lo", [P, 512], F32R)]
    negmax = sb("negmax1", [P, 4])
    e = sb("e1", [P, 4, 256])
    den = sb("den1", [P, 4])
    rden = sb("rden1", [P, 4])
    first = sb("probs_first", [P, 2, 256])
    probs = sb("probs", [P, 2, 256])
    one = sb("one", [P, 1])
    csum = sb("csum", [P, 4])
    vhi = sb("val_hi", [P, 512], F32R)
    vlo = sb("val_lo", [P, 512], F32R)
    ps = lambda n: ctx.enter_context(nc.psum_tensor(n, [P, 512], F32))
    psQK, psV, psS, psC, psO = [ps("psQ1"), ps("psK1")], ps("psV1"), [ps("psS10"), ps("psS11")], ps("psC1"), [ps("psO0"), ps("psO1")]

    zeros = sb("zeros", [P, 1024])
    gidx = sb("gidx", [P, 2, 8], I32)
    gw = sb("gw", [P, 2, 8])
    yg = sb("yg", [P, 4, 256])
    mix = sb("mix", [P, 2, 256])
    gidx_ok, gw_ok, mixed, f_ok = (sem("a1_" + n) for n in ("gidx_ok", "gw_ok", "mixed", "f_ok"))
    wait_done = t["wait_done"]
    gathered = [sem(f"a1_gathered{i}") for i in range(4)]
    raw_in = [sem("head_in0"), sem("head_in1")]
    x2_in = sem("x2_in")
    silf_ok, prod_ok, sum_ok, out_stored = sem("silf_ok"), sem("prod_ok"), sem("sum_ok"), sem("out_stored")
    two = lambda z, k: z[:, 2 * k:2 * k + 2].rearrange("p t d -> p (t d)")
    whi_ok, wlo_ok, v_ok, scores_ok, max_ok, exp_ok, rden_ok, first_ok, probs_ok, c_ok, csum_ok, vhi_ok, vlo_ok, o_ok, acc_ok, zeroed = (
        sem("a1_" + n) for n in ("whi_ok", "wlo_ok", "v_ok", "scores_ok", "max_ok", "exp_ok", "rden_ok", "first_ok", "probs_ok",
                                 "c_ok", "csum_ok", "vhi_ok", "vlo_ok", "o_ok", "acc_ok", "zeroed"))
    p_ok = [sem("a1_q_ok"), sem("a1_k_ok")]
    phi_ok = [sem("a1_qhi_ok"), sem("a1_khi_ok")]
    plo_ok = [sem("a1_qlo_ok"), sem("a1_klo_ok")]
    block = ctx.enter_context(nc.Block())

    def drive(eng, step, tail):
        for k in range(8):
            step(Step(0, k))
        with eng.Fori(1, NH // 2) as i:
            for k in range(8):
                step(Step(i, k))
        tail(Step(NH // 2, 0))

    exists = lambda n: not isinstance(n, int) or n >= 0

    @block.sync
    def _(sp):
        def load(head_i, par, uses):
            wait(sp, wlo_ok, 2 * (uses - 2) + par + 1)
            src = args["heads"][2 * head_i + par]
            sp.dma_start(raw[:, par], src).then_inc(raw_in[par], 16)
        for par in range(2):
            load(0, par, 1)
        sp.dma_start(x2[:], x2_dram.rearrange("(i p) d -> p i d", p=P)).then_inc(x2_in, 16)
        with sp.Fori(1, NH // 2) as i:
            for par in range(2):
                load(i, par, i + 1)
        for k in range(NP):
            sp.wait_ge(sum_ok, k + 1)
            sp.dma_start(out.rearrange("(i p) d -> p i d", p=P)[:, 2 * k:2 * k + 2], f[:, 2 * k:2 * k + 2]).then_inc(out_stored, 16)
        sp.wait_ge(out_stored, 16 * NP)

    @block.gpsimd
    def _(pool):
        def split(i, par):
            if isinstance(i, int) and i == 0 and par == 1:
                pool.wait_ge(wlo_ok, 1)
            pool.wait_ge(raw_in[par], 16 * (i + 1))
            wait(pool, o_ok, 8 * i + 4 * par - 4)
            pool.tensor_tensor(whi[:, par], raw[:, par], zeros[:, 0:raw.shape[2]], ALU.add).then_inc(whi_ok, 1)
            pool.wait_ge(whi_ok, 2 * i + par + 1)
            pool.tensor_tensor(wlo[:, par], raw[:, par], whi[:, par].bitcast(F32), ALU.subtract).then_inc(wlo_ok, 1)

        def of_tile(buf, s):
            return buf[:, s.head] if isinstance(s.head, int) else buf[:, bass.ds(s.head, 1)].rearrange("p o k -> p (o k)")

        def gather(s):
            if s.g == 0:
                wait(pool, mixed, 8 * s.head - 8)
                pool.sem_inc(wait_done, 1)
                pool.tensor_copy(gidx[:, s.par], of_tile(routed["slots"], s)).then_inc(gidx_ok, 1)
                pool.tensor_copy(gw[:, s.par], of_tile(routed["weights"], s)).then_inc(gw_ok, 1)
                pool.wait_ge(gidx_ok, s.head + 1)
                pool.sem_inc(wait_done, 1)
            for j in range(2):
                q = (2 * s.k + j) % 4
                wait(pool, mixed, 2 * s.n + j - 3)
                pool.sem_inc(wait_done, 1)
                pool.indirect_dma_start(yg[:, q], None, routed["y_dram"],
                                        bass.IndirectOffsetOnAxis(ap=gidx[:, s.par, 2 * s.g + j:2 * s.g + j + 1], axis=0)).then_inc(gathered[q], 16)

        def add_tile(s):
            pool.wait_ge(mixed, 8 * s.head + 8)
            dst = of_tile(f, s)
            pool.tensor_tensor(dst, mix[:, s.par], dst, ALU.add).then_inc(f_ok, 1)

        def step(s, last=False):
            gather(s)
            if s.g == 2 and exists(s.n - 4):
                add_tile(s.back(4))
            if s.g == 2 and not last:
                nxt = Step(s.i, s.k + 4)
                split(nxt.i if nxt.k < 8 else nxt.i + 1, nxt.par)

        pool.memset(one[:], 1.0).then_inc(zeroed, 1)
        pool.memset(zeros[:], 0.0).then_inc(zeroed, 1)
        pool.wait_ge(zeroed, 2)
        for k in range(8):
            step(Step(0, k))
        with pool.Fori(1, NH // 2 - 1) as i:
            for k in range(8):
                step(Step(i, k))
        for k in range(8):
            step(Step(NH // 2 - 1, k), last=k >= 4)
        add_tile(Step(NH // 2, -4))
        pool.wait_ge(x2_in, 16)
        for k in range(POOL_SUMS):
            pool.wait_ge(prod_ok, k + 1)
            pool.tensor_tensor(two(f, k), two(f, k), two(x2, k), ALU.add).then_inc(sum_ok, 1)

    @block.tensor
    def _(pe):
        mm = pe.matmul

        def proj(s, j, out, done):
            for c in range(2):
                wc = (slice(None), s.par, slice(256 * j + P * c, 256 * j + P * (c + 1)))
                tok = (slice(None), c, slice(512 * s.g, 512 * s.g + 512))
                last = split3(mm, out[:], whi[wc], wlo[wc], xhi[tok], xlo[tok], c == 0, c == 1)
            last.then_inc(done, 1)

        def column_sums(s):
            pe.wait_ge(probs_ok, s.n + 1)
            wait(pe, csum_ok, s.n)
            for c in range(4):
                last = mm(psC[:, c:c + 1], probs[:, c // 2, P * (c % 2):P * (c % 2 + 1)], one[:], start=True, stop=True)
            last.then_inc(c_ok, 1)

        def out_proj(s):
            pe.wait_ge(vlo_ok, s.n + 1)
            pe.wait_ge(acc_ok, s.n + 1)
            wo = (slice(None), s.par, slice(768, 1024))
            for i in range(4):
                tok = (slice(None), slice(P * i, P * i + P))
                last = split3(mm, psO[i // 2][:, 256 * (i % 2):256 * (i % 2) + 256], vhi[tok], vlo[tok], whi[wo], wlo[wo], True, True)
            last.then_inc(o_ok, 1)

        def step(s):
            if s.g == 0:
                pe.wait_ge(wlo_ok, s.head + 1)
            for j in range(2):
                wait(pe, plo_ok[j], s.n)
                proj(s, j, psQK[j], p_ok[j])
            if exists(s.n - 1):
                out_proj(s.back(1))
                column_sums(s.back(1))
            pe.wait_ge(plo_ok[1], s.n + 1)
            for b in range(2):
                wait(pe, exp_ok, 2 * s.n + b - 1)
                for i in range(2):
                    qt = slice(256 * b + P * i, 256 * b + P * (i + 1))
                    kt = slice(256 * b, 256 * b + 256)
                    last = split3(mm, psS[b][:, 256 * i:256 * i + 256], ohi[0][:, qt], olo[0][:, qt], ohi[1][:, kt], olo[1][:, kt], True, True)
                last.then_inc(scores_ok, 1)
            wait(pe, vlo_ok, s.n)
            proj(s, 2, psV, v_ok)

        def tail(s):
            out_proj(s.back(1))
            column_sums(s.back(1))

        pe.wait_ge(zeroed, 1)
        drive(pe, step, tail)

    @block.scalar
    def _(act):
        def v_hi(s):
            act.wait_ge(v_ok, s.n + 1)
            wait(act, o_ok, s.n)
            act.activation(vhi[:], psV[:], ACT.Copy).then_inc(vhi_ok, 1)

        def step(s):
            for j in range(2):
                act.wait_ge(p_ok[j], s.n + 1)
                wait(act, scores_ok, 2 * s.n)
                act.activation(ohi[j][:], psQK[j][:], ACT.Copy, scale=SCALE if j == 0 else 1.0).then_inc(phi_ok[j], 1)
            wait(act, probs_ok, s.n)
            for b in range(2):
                act.wait_ge(max_ok, 2 * s.n + b + 1)
                for i in range(2):
                    c = 2 * b + i
                    m = act.activation(e[:, c], psS[b][:, 256 * i:256 * i + 256], ACT.Exp, bias=negmax[:, c:c + 1], accum_out=den[:, c:c + 1])
                m.then_inc(exp_ok, 1)
            v_hi(s)
            act.wait_ge(rden_ok, s.n + 1)
            for b in range(2):
                m = act.activation(first[:, b], e[:, 2 * b], ACT.Copy, scale=rden[:, 2 * b:2 * b + 1])
            m.then_inc(first_ok, 1)

        act.wait_ge(raw_in[0], 16)
        act.activation(whi[:, 0], raw[:, 0], ACT.Copy).then_inc(whi_ok, 1)
        def tail(s):
            for k in range(NP):
                if k in (0, NP - 1):
                    act.wait_ge(f_ok, 14 if k == 0 else 16)
                act.activation(two(f, k), two(f, k), ACT.Silu).then_inc(silf_ok, 1)

        drive(act, step, tail)

    @block.vector
    def _(dve):
        def proj_lo(s, j):
            dve.wait_ge(phi_ok[j], s.n + 1)
            if j == 0:
                dve.scalar_tensor_tensor(olo[0][:], psQK[0][:], SCALE, ohi[0][:].bitcast(F32), ALU.mult, ALU.subtract).then_inc(plo_ok[0], 1)
            else:
                dve.tensor_tensor(olo[1][:], psQK[1][:], ohi[1][:].bitcast(F32), ALU.subtract).then_inc(plo_ok[1], 1)

        def reciprocals(s):
            dve.wait_ge(exp_ok, 2 * s.n + 2)
            dve.reciprocal(rden[:], den[:]).then_inc(rden_ok, 1)

        def add_probs(s):
            dve.wait_ge(first_ok, s.n + 1)
            wait(dve, c_ok, s.n)
            for b in range(2):
                m = dve.scalar_tensor_tensor(probs[:, b], e[:, 2 * b + 1], rden[:, 2 * b + 1:2 * b + 2], first[:, b], ALU.mult, ALU.add)
            m.then_inc(probs_ok, 1)

        def v_lo(s):
            dve.wait_ge(vhi_ok, s.n + 1)
            dve.tensor_tensor(vlo[:], psV[:], vhi[:].bitcast(F32), ALU.subtract).then_inc(vlo_ok, 1)

        def accumulate(s):
            dve.wait_ge(c_ok, s.n + 1)
            dve.wait_ge(acc_ok, s.n + 1)
            dve.tensor_copy(csum[:], psC[:, 0:4]).then_inc(csum_ok, 1)
            dve.wait_ge(csum_ok, s.n + 1)
            dve.wait_ge(o_ok, s.n + 1)
            for i in range(4):
                dst = s1[:, 4 * s.g + i]
                m = dve.scalar_tensor_tensor(dst, psO[i // 2][:, 256 * (i % 2):256 * (i % 2) + 256], csum[:, i:i + 1], dst, ALU.mult, ALU.add)
            m.then_inc(acc_ok, 1)

        def mix_in(s):
            if s.g == 0:
                dve.wait_ge(gw_ok, s.head + 1)
                wait(dve, f_ok, s.head - 1)
            for j in range(2):
                q = (2 * s.k + j) % 4
                dve.wait_ge(gathered[q], 16 * (4 * s.i + s.k // 2 + 1))
                col = gw[:, s.par, 2 * s.g + j:2 * s.g + j + 1]
                if s.g == 0 and j == 0:
                    dve.tensor_scalar(mix[:, s.par], yg[:, q], col, None, ALU.mult).then_inc(mixed, 1)
                else:
                    dve.wait_ge(mixed, 2 * s.n + j)
                    dve.scalar_tensor_tensor(mix[:, s.par], yg[:, q], col, mix[:, s.par], ALU.mult, ALU.add).then_inc(mixed, 1)

        def step(s):
            proj_lo(s, 0)
            proj_lo(s, 1)
            if exists(s.n - 1):
                mix_in(s.back(1))
            for b in range(2):
                dve.wait_ge(scores_ok, 2 * s.n + b + 1)
                dve.tensor_reduce(negmax[:, 2 * b:2 * b + 2], psS[b][:].rearrange("p (i k) -> p i k", i=2), AX.X, ALU.max, negate=True).then_inc(max_ok, 1)
            if exists(s.n - 1):
                accumulate(s.back(1))
            reciprocals(s)
            v_lo(s)
            add_probs(s)

        def combine(k, add):
            dve.wait_ge(silf_ok, k + 1)
            dve.tensor_tensor(two(f, k), two(f, k), two(s1, k), ALU.mult).then_inc(prod_ok, 1)
            if add:
                dve.wait_ge(prod_ok, k + 1)
                dve.wait_ge(sum_ok, k)
                dve.tensor_tensor(two(f, k), two(f, k), two(x2, k), ALU.add).then_inc(sum_ok, 1)

        def tail(s):
            mix_in(s.back(1))
            dve.wait_ge(acc_ok, 4 * NH)
            for k in range(POOL_SUMS):
                combine(k, False)
            accumulate(s.back(1))
            dve.wait_ge(acc_ok, 4 * NH + 1)
            dve.wait_ge(x2_in, 16)
            for k in range(POOL_SUMS, NP):
                combine(k, True)

        dve.memset(s1[:], 0.0).then_inc(acc_ok, 1)
        dve.wait_ge(whi_ok, 1)
        dve.tensor_tensor(wlo[:, 0], raw[:, 0], whi[:, 0].bitcast(F32), ALU.subtract).then_inc(wlo_ok, 1)
        drive(dve, step, tail)


def build(nc, args, out):
    T, D = 2048, 256
    with ExitStack() as all_ctx:
        def sb(ctx, name, shape, dt=F32):
            return ctx.enter_context(nc.sbuf_tensor(name, shape, dt))

        t = {
            "ident": sb(all_ctx, "ident", [P, P]),
            "neg_half": sb(all_ctx, "neg_half", [P, 16]),
            "stats1": sb(all_ctx, "stats1", [P, T // P, 6]),
            "wait_done": all_ctx.enter_context(nc.semaphore("wait_done")),
            "x2_stored": all_ctx.enter_context(nc.semaphore("x2_stored")),
        }
        x2 = sb(all_ctx, "x2", [P, T // P, D])
        x2_dram = nc.dram_tensor("x2_scratch", [T, D], F32, kind="Internal").ap()
        with ExitStack() as c0:
            t["ident_r"] = sb(c0, "ident_r", [P, P], F32R)
            t["mask_r"] = sb(c0, "mask_r", [P, P], F32R)
            w = {
                "hi": sb(c0, "w_hi", [P, 4, 2, 256], F32R), "lo": sb(c0, "w_lo", [P, 4, 2, 256], F32R),
                "up_hi": sb(c0, "up_hi", [P, 2, 2, 1024], F32R), "up_lo": sb(c0, "up_lo", [P, 2, 2, 1024], F32R),
                "dn_hi": sb(c0, "dn_hi", [P, 8, 256], F32R), "dn_lo": sb(c0, "dn_lo", [P, 8, 256], F32R),
            }
            with ExitStack() as c:
                prepare_weights(nc, c, t, w, x2, args)
            with ExitStack() as c:
                layer0(nc, c, t, x2, x2_dram, w)
        xhi = sb(all_ctx, "x1_hi", [P, 2, T], F32R)
        xlo = sb(all_ctx, "x1_lo", [P, 2, T], F32R)
        f = x2
        routed = {
            "xn_dram": nc.dram_tensor("xn_scratch", [T, D], F32, kind="Internal").ap(),
            "y_dram": nc.dram_tensor("y_scratch", [NBLK * P, D], F32, kind="Internal").ap(),
            "ids": sb(all_ctx, "ids", [P, NBLK], I32),
            "owner": sb(all_ctx, "owner_row", [P, NBLK], I32),
            "slots": sb(all_ctx, "slots", [P, T // P, 8], I32),
            "weights": sb(all_ctx, "weights", [P, T // P, 8]),
        }
        with ExitStack() as cw:
            routed["w"] = sb(cw, "expert_w", [P, 32, 768])
            routed["chosen"] = sb(cw, "chosen", [P, T // P, 32])
            routed["key"] = sb(cw, "key", [P, T // P, 32])
            routed["best_key"] = sb(cw, "best_key", [P, T // P, 8])
            with ExitStack() as c:
                normalise_and_route(nc, c, t, x2, xhi, xlo, routed, args)
            with ExitStack() as c:
                routed_experts(nc, c, t, routed)
        s1 = sb(all_ctx, "s1", [P, T // P, D])
        x2 = sb(all_ctx, "x2_again", [P, T // P, D])
        with ExitStack() as c:
            attention1(nc, c, t, xhi, xlo, s1, f, x2, x2_dram, routed, args, out)


def layout(inputs):
    import numpy as np

    f = lambda name: np.asarray(inputs[name])
    hadamard = np.ones((1, 1), np.float32)
    for _ in range(7):
        hadamard = np.block([[hadamard, hadamard], [hadamard, -hadamard]])
    w_qkv = f("L1_attn_w_qkv")
    halves = lambda w: w.reshape(-1, 2, 128, 128).transpose(0, 2, 1, 3).reshape(-1, 128, 256)
    by_half = lambda w: w.reshape(256, 2, 128).transpose(1, 0, 2)
    gate, up = (np.concatenate([f("L1_ffn_w_" + n), by_half(f("L1_ffn_sw_" + n))]) for n in ("gate", "up"))
    down = np.concatenate([f("L1_ffn_w_down"), f("L1_ffn_sw_down").reshape(2, 128, 256)])
    out = {
        "x": f("L0_attn_x").reshape(2048, 256),
        "qkvoT": np.stack([f("L0_attn_" + n).T for n in ("Wq", "Wk", "Wv", "Wo")]),
        "upT": np.stack([f("L0_ffn_W1").T, f("L0_ffn_W3").T]),
        "W2T": f("L0_ffn_W2").T,
        "ident": np.eye(128, dtype=np.float32),
        "hadamard": hadamard,
        "heads": np.concatenate(
            [halves(w_qkv[:, 2048 * j:2048 * (j + 1)].reshape(256, 16, 128).transpose(1, 0, 2)) for j in range(3)]
            + [f("L1_attn_w_o").reshape(16, 128, 256)], axis=2),
        "experts": np.concatenate([gate[:, 0:128], up[:, 0:128], gate[:, 128:256], up[:, 128:256], down], axis=2),
        "earlier32": np.tril(np.ones((32, 32), np.float32), -1).reshape(1, 1024),
        "iota": np.arange(256, dtype=np.float32).reshape(1, 256),
        "firsts": (128 * np.arange(16)).astype(np.float32).reshape(1, 16),
        "part": np.arange(256, dtype=np.float32).reshape(2, 128).T,
        "tokens": np.arange(2048, dtype=np.float32).reshape(16, 128).T,
        "before": np.triu(np.ones((128, 128), np.float32), 1),
        "router_w": f("L1_ffn_router_w"),
        "router_bias": f("L1_ffn_router_bias").reshape(1, 32),
        "earlier": np.tril(np.ones((8, 8), np.float32), -1).reshape(1, 64),
        "mask": np.triu(np.full((128, 128), MASKED, np.float32), 1),
    }
    return {k: np.ascontiguousarray(v) for k, v in out.items()}


def kernel(**inputs):
    import numpy as np
    import concourse.bacc as bacc
    from concourse.bass_utils import run_bass_kernel_spmd

    nc = bacc.Bacc("TRN2", target_bir_lowering=False, num_devices=1)
    arrays = {"in_" + k: v for k, v in layout(inputs).items()}
    args = {k[3:]: nc.dram_tensor(k, v.shape, mybir.dt.from_np(v.dtype), kind="ExternalInput").ap() for k, v in arrays.items()}
    out = nc.dram_tensor("out", (2048, 256), F32, kind="ExternalOutput").ap()
    build(nc, args, out)
    r = run_bass_kernel_spmd(nc, [arrays], core_ids=[0])
    return np.asarray(r.results[0]["out"]).reshape(8, 256, 256)
```
